# Optimizing a Trainium2 kernel written in Bass

```python
import numpy as np
import jax
import jax.numpy as jnp

def _softmax(x, axis=-1):
    return jax.nn.softmax(x, axis=axis)

def _gelu(x):
    return jax.nn.gelu(x, approximate=True)

def _silu(x):
    return jax.nn.silu(x)

def _sigmoid(x):
    return jax.nn.sigmoid(x)

def _layernorm(x, axis=-1, eps=1e-05):
    m = jnp.mean(x, axis=axis, keepdims=True)
    v = jnp.var(x, axis=axis, keepdims=True)
    return (x - m) / jnp.sqrt(v + eps)

def _scatter_add(tgt, idx, src, axis=0):
    return tgt.at[idx].add(src)

def _segment_sum(src, seg, n):
    return jax.ops.segment_sum(src, seg, n)
kernel_name = 'mk_early_fusion_d1_tok_img1024_r4_9262cf'

def setup_inputs(seed: int=0):
    np.random.seed(seed)
    _w = jnp.asarray

    def _rec_inputs():
        import jax
        import jax.numpy as jnp
        _rk = jax.random.key(seed)
        x = -0.00016672 + 0.999947 * jax.random.normal(jax.random.fold_in(_rk, 1), (32, 3, 96, 96), jnp.float32)
        txt = 0.00140885 + 1.4139 * jax.random.normal(jax.random.fold_in(_rk, 2), (32, 77, 256), jnp.float32)
        return (x, txt)
    x, txt = _rec_inputs()

    def _L0_tok_setup():
        import jax, jax.numpy as jnp
        import numpy as np
        B, C, H, W = (64, 3, 96, 96)
        P = 16
        NP = H // P * (W // P)
        PD = C * P * P
        ED = 256
        NCLS = 1

        def _layernorm(x, g, b, eps=1e-05):
            mu = jnp.mean(x, axis=-1, keepdims=True)
            var = jnp.mean(jnp.square(x - mu), axis=-1, keepdims=True)
            return (x - mu) * jax.lax.rsqrt(var + eps) * g + b
        key = jax.random.key(seed)
        ks = jax.random.split(key, 8)
        x = jax.random.normal(ks[0], (B, C, H, W), dtype=jnp.float32)
        ln1_g = jnp.ones((PD,), jnp.float32)
        ln1_b = jnp.zeros((PD,), jnp.float32)
        W_proj = jax.random.normal(ks[1], (PD, ED), jnp.float32) / np.sqrt(PD)
        b_proj = jnp.zeros((ED,), jnp.float32)
        ln2_g = jnp.ones((ED,), jnp.float32)
        ln2_b = jnp.zeros((ED,), jnp.float32)
        cls_token = jax.random.normal(ks[2], (1, NCLS, ED), jnp.float32)
        pos_emb = jax.random.normal(ks[3], (1, NP + NCLS, ED), jnp.float32)
        return {'x': x, 'ln1_g': ln1_g, 'ln1_b': ln1_b, 'W_proj': W_proj, 'b_proj': b_proj, 'ln2_g': ln2_g, 'ln2_b': ln2_b, 'cls_token': cls_token, 'pos_emb': pos_emb}
    _L0_tok_all = _L0_tok_setup()
    _L0_tok_in = {k: v for k, v in _L0_tok_all.items() if k in ('ln1_g', 'ln1_b', 'W_proj', 'b_proj', 'ln2_g', 'ln2_b', 'cls_token', 'pos_emb')}
    del _L0_tok_all

    def _L0_attn_setup():
        import jax, jax.numpy as jnp
        import numpy as np
        NUM_HEADS = 16
        DIM_HEAD = 64
        SCALE = DIM_HEAD ** (-0.5)
        ROPE_BASE = 10000.0

        def _rope(t):
            n, d = (t.shape[2], t.shape[3])
            inv_freq = 1.0 / ROPE_BASE ** (jnp.arange(0, d, 2, dtype=jnp.float32) / d)
            freqs = jnp.arange(n, dtype=jnp.float32)[:, None] * inv_freq[None, :]
            cos = jnp.concatenate([jnp.cos(freqs), jnp.cos(freqs)], axis=-1)
            sin = jnp.concatenate([jnp.sin(freqs), jnp.sin(freqs)], axis=-1)
            t1, t2 = jnp.split(t, 2, axis=-1)
            rot = jnp.concatenate([-t2, t1], axis=-1)
            return t * cos + rot * sin
        key = jax.random.key(seed)
        k1, k2, k3 = jax.random.split(key, 3)
        B, N, D = (2, 2049, 256)
        x = jax.random.normal(k1, (B, N, D), dtype=jnp.float32)
        ln_gamma = jnp.ones((D,), dtype=jnp.float32)
        ln_beta = jnp.zeros((D,), dtype=jnp.float32)
        w_qkv = jax.random.normal(k2, (D, 3 * NUM_HEADS * DIM_HEAD), dtype=jnp.float32) * 0.02
        w_out = jax.random.normal(k3, (NUM_HEADS * DIM_HEAD, D), dtype=jnp.float32) * 0.02
        return {'x': x, 'ln_gamma': ln_gamma, 'ln_beta': ln_beta, 'w_qkv': w_qkv, 'w_out': w_out}
    _L0_attn_all = _L0_attn_setup()
    _L0_attn_in = {k: v for k, v in _L0_attn_all.items() if k in ('ln_gamma', 'ln_beta', 'w_qkv', 'w_out')}
    del _L0_attn_all

    def _L0_ffn_setup():
        import jax, jax.numpy as jnp
        import numpy as np
        DIM = 256
        E = 16
        TOPK = 2
        G = 4
        TOPK_G = 2
        INTER = 128
        N_SHARED = 2
        ROUTE_SCALE = 1.0

        def _gate(xf, gate_w, gate_b):
            scores = xf @ gate_w.T
            scores = jax.nn.softmax(scores.astype(jnp.float32), axis=-1)
            orig = scores
            scores = scores + gate_b
            T = xf.shape[0]
            sg = scores.reshape(T, G, E // G)
            group_scores = jax.lax.top_k(sg, 2)[0].sum(-1)
            _, gidx = jax.lax.top_k(group_scores, TOPK_G)
            keep = jax.nn.one_hot(gidx, G).sum(axis=1) > 0
            sg = jnp.where(keep[:, :, None], sg, -jnp.inf)
            scores = sg.reshape(T, E)
            _, idx = jax.lax.top_k(scores, TOPK)
            weights = jnp.take_along_axis(orig, idx, axis=1)
            weights = (weights * ROUTE_SCALE).astype(xf.dtype)
            return (weights, idx)
        key = jax.random.key(seed)
        ks = jax.random.split(key, 16)
        s = lambda fan_in: 1.0 / np.sqrt(fan_in)
        inp = {'x': jax.random.normal(ks[0], (4, 256, DIM), dtype=jnp.float32), 'gate_w': jax.random.normal(ks[1], (E, DIM), dtype=jnp.float32) * s(DIM), 'gate_b': jnp.zeros((E,), dtype=jnp.float32), 'We1': jax.random.normal(ks[2], (E, DIM, INTER), dtype=jnp.float32) * s(DIM), 'be1': jnp.zeros((E, INTER), dtype=jnp.float32), 'We2': jax.random.normal(ks[3], (E, INTER, DIM), dtype=jnp.float32) * s(INTER), 'be2': jnp.zeros((E, DIM), dtype=jnp.float32), 'We3': jax.random.normal(ks[4], (E, DIM, INTER), dtype=jnp.float32) * s(DIM), 'be3': jnp.zeros((E, INTER), dtype=jnp.float32), 'ws1': jax.random.normal(ks[5], (DIM, N_SHARED * INTER), dtype=jnp.float32) * s(DIM), 'bs1': jnp.zeros((N_SHARED * INTER,), dtype=jnp.float32), 'ws2': jax.random.normal(ks[6], (N_SHARED * INTER, DIM), dtype=jnp.float32) * s(N_SHARED * INTER), 'bs2': jnp.zeros((DIM,), dtype=jnp.float32), 'ws3': jax.random.normal(ks[7], (DIM, N_SHARED * INTER), dtype=jnp.float32) * s(DIM), 'bs3': jnp.zeros((N_SHARED * INTER,), dtype=jnp.float32)}
        return inp
    _L0_ffn_all = _L0_ffn_setup()
    _L0_ffn_in = {k: v for k, v in _L0_ffn_all.items() if k in ('gate_w', 'gate_b', 'We1', 'be1', 'We2', 'be2', 'We3', 'be3', 'ws1', 'bs1', 'ws2', 'bs2', 'ws3', 'bs3')}
    del _L0_ffn_all
    return {'x': x, 'txt': txt, 'L0_tok_ln1_g': _L0_tok_in['ln1_g'], 'L0_tok_ln1_b': _L0_tok_in['ln1_b'], 'L0_tok_W_proj': _L0_tok_in['W_proj'], 'L0_tok_b_proj': _L0_tok_in['b_proj'], 'L0_tok_ln2_g': _L0_tok_in['ln2_g'], 'L0_tok_ln2_b': _L0_tok_in['ln2_b'], 'L0_tok_cls_token': _L0_tok_in['cls_token'], 'L0_tok_pos_emb': _L0_tok_in['pos_emb'], 'L0_attn_ln_gamma': _L0_attn_in['ln_gamma'], 'L0_attn_ln_beta': _L0_attn_in['ln_beta'], 'L0_attn_w_qkv': _L0_attn_in['w_qkv'], 'L0_attn_w_out': _L0_attn_in['w_out'], 'L0_ffn_gate_w': _L0_ffn_in['gate_w'], 'L0_ffn_gate_b': _L0_ffn_in['gate_b'], 'L0_ffn_We1': _L0_ffn_in['We1'], 'L0_ffn_be1': _L0_ffn_in['be1'], 'L0_ffn_We2': _L0_ffn_in['We2'], 'L0_ffn_be2': _L0_ffn_in['be2'], 'L0_ffn_We3': _L0_ffn_in['We3'], 'L0_ffn_be3': _L0_ffn_in['be3'], 'L0_ffn_ws1': _L0_ffn_in['ws1'], 'L0_ffn_bs1': _L0_ffn_in['bs1'], 'L0_ffn_ws2': _L0_ffn_in['ws2'], 'L0_ffn_bs2': _L0_ffn_in['bs2'], 'L0_ffn_ws3': _L0_ffn_in['ws3'], 'L0_ffn_bs3': _L0_ffn_in['bs3']}

def reference(x, txt, L0_tok_ln1_g, L0_tok_ln1_b, L0_tok_W_proj, L0_tok_b_proj, L0_tok_ln2_g, L0_tok_ln2_b, L0_tok_cls_token, L0_tok_pos_emb, L0_attn_ln_gamma, L0_attn_ln_beta, L0_attn_w_qkv, L0_attn_w_out, L0_ffn_gate_w, L0_ffn_gate_b, L0_ffn_We1, L0_ffn_be1, L0_ffn_We2, L0_ffn_be2, L0_ffn_We3, L0_ffn_be3, L0_ffn_ws1, L0_ffn_bs1, L0_ffn_ws2, L0_ffn_bs2, L0_ffn_ws3, L0_ffn_bs3):
    import jax
    import jax.numpy as jnp

    def _L0_tok_ref(x, ln1_g, ln1_b, W_proj, b_proj, ln2_g, ln2_b, cls_token, pos_emb):
        import jax, jax.numpy as jnp
        import numpy as np
        B, C, H, W = (64, 3, 96, 96)
        P = 16
        NP = H // P * (W // P)
        PD = C * P * P
        ED = 256
        NCLS = 1

        def _layernorm(x, g, b, eps=1e-05):
            mu = jnp.mean(x, axis=-1, keepdims=True)
            var = jnp.mean(jnp.square(x - mu), axis=-1, keepdims=True)
            return (x - mu) * jax.lax.rsqrt(var + eps) * g + b
        b = x.shape[0]
        h, w = (H // P, W // P)
        patches = x.reshape(b, C, h, P, w, P)
        patches = patches.transpose(0, 2, 4, 3, 5, 1).reshape(b, h * w, P * P * C)
        z = _layernorm(patches, ln1_g, ln1_b)
        z = jnp.einsum('bnp,pe->bne', z, W_proj) + b_proj
        z = _layernorm(z, ln2_g, ln2_b)
        cls = jnp.broadcast_to(cls_token, (b, NCLS, ED))
        z = jnp.concatenate([cls, z], axis=1)
        z = z + pos_emb
        return z

    def _L0_attn_ref(x, ln_gamma, ln_beta, w_qkv, w_out):
        import jax, jax.numpy as jnp
        import numpy as np
        NUM_HEADS = 16
        DIM_HEAD = 64
        SCALE = DIM_HEAD ** (-0.5)
        ROPE_BASE = 10000.0

        def _rope(t):
            n, d = (t.shape[2], t.shape[3])
            inv_freq = 1.0 / ROPE_BASE ** (jnp.arange(0, d, 2, dtype=jnp.float32) / d)
            freqs = jnp.arange(n, dtype=jnp.float32)[:, None] * inv_freq[None, :]
            cos = jnp.concatenate([jnp.cos(freqs), jnp.cos(freqs)], axis=-1)
            sin = jnp.concatenate([jnp.sin(freqs), jnp.sin(freqs)], axis=-1)
            t1, t2 = jnp.split(t, 2, axis=-1)
            rot = jnp.concatenate([-t2, t1], axis=-1)
            return t * cos + rot * sin
        B, N, D = x.shape
        mu = jnp.mean(x, axis=-1, keepdims=True)
        var = jnp.mean(jnp.square(x - mu), axis=-1, keepdims=True)
        xn = (x - mu) * jax.lax.rsqrt(var + 1e-05) * ln_gamma + ln_beta
        qkv = xn @ w_qkv
        q, k, v = jnp.split(qkv, 3, axis=-1)

        def to_heads(t):
            return t.reshape(B, N, NUM_HEADS, DIM_HEAD).transpose(0, 2, 1, 3)
        q, k, v = (to_heads(q), to_heads(k), to_heads(v))
        q = jnp.concatenate([q[:, :, :1, :], _rope(q[:, :, 1:, :])], axis=2)
        k = jnp.concatenate([k[:, :, :1, :], _rope(k[:, :, 1:, :])], axis=2)
        dots = jnp.einsum('bhqd,bhkd->bhqk', q, k) * SCALE
        attn = jax.nn.softmax(dots, axis=-1)
        out = jnp.einsum('bhqk,bhkd->bhqd', attn, v)
        out = out.transpose(0, 2, 1, 3).reshape(B, N, NUM_HEADS * DIM_HEAD)
        return out @ w_out

    def _L0_ffn_ref(x, gate_w, gate_b, We1, be1, We2, be2, We3, be3, ws1, bs1, ws2, bs2, ws3, bs3):
        import jax, jax.numpy as jnp
        import numpy as np
        DIM = 256
        E = 16
        TOPK = 2
        G = 4
        TOPK_G = 2
        INTER = 128
        N_SHARED = 2
        ROUTE_SCALE = 1.0

        def _gate(xf, gate_w, gate_b):
            scores = xf @ gate_w.T
            scores = jax.nn.softmax(scores.astype(jnp.float32), axis=-1)
            orig = scores
            scores = scores + gate_b
            T = xf.shape[0]
            sg = scores.reshape(T, G, E // G)
            group_scores = jax.lax.top_k(sg, 2)[0].sum(-1)
            _, gidx = jax.lax.top_k(group_scores, TOPK_G)
            keep = jax.nn.one_hot(gidx, G).sum(axis=1) > 0
            sg = jnp.where(keep[:, :, None], sg, -jnp.inf)
            scores = sg.reshape(T, E)
            _, idx = jax.lax.top_k(scores, TOPK)
            weights = jnp.take_along_axis(orig, idx, axis=1)
            weights = (weights * ROUTE_SCALE).astype(xf.dtype)
            return (weights, idx)
        shape = x.shape
        xf = x.reshape(-1, DIM)
        weights, idx = _gate(xf, gate_w, gate_b)
        combine = (jax.nn.one_hot(idx, E, dtype=xf.dtype) * weights[..., None]).sum(1)
        h1 = jnp.einsum('td,edi->tei', xf, We1) + be1
        h3 = jnp.einsum('td,edi->tei', xf, We3) + be3
        h = jax.nn.silu(h1) * h3
        yo = jnp.einsum('tei,eid->ted', h, We2) + be2
        y = jnp.einsum('te,ted->td', combine, yo)
        z = jax.nn.silu(xf @ ws1 + bs1) * (xf @ ws3 + bs3) @ ws2 + bs2
        return (y + z).reshape(shape)
    h = _L0_tok_ref(x, L0_tok_ln1_g, L0_tok_ln1_b, L0_tok_W_proj, L0_tok_b_proj, L0_tok_ln2_g, L0_tok_ln2_b, L0_tok_cls_token, L0_tok_pos_emb)
    h = jnp.concatenate([h, txt], axis=1)
    h = h + _L0_attn_ref(_layernorm(h, axis=-1), L0_attn_ln_gamma, L0_attn_ln_beta, L0_attn_w_qkv, L0_attn_w_out)
    h = h + _L0_ffn_ref(_layernorm(h, axis=-1), L0_ffn_gate_w, L0_ffn_gate_b, L0_ffn_We1, L0_ffn_be1, L0_ffn_We2, L0_ffn_be2, L0_ffn_We3, L0_ffn_be3, L0_ffn_ws1, L0_ffn_bs1, L0_ffn_ws2, L0_ffn_bs2, L0_ffn_ws3, L0_ffn_bs3)
    return h

_drawn_inputs = setup_inputs


def setup_inputs(seed=0):
    import zlib

    import numpy as np

    out = dict(_drawn_inputs(seed))
    spreads = {'L0_tok_ln1_g': (1.0, 0.2),
     'L0_tok_ln1_b': (0.0, 0.1),
     'L0_tok_b_proj': (0.0, 0.1),
     'L0_tok_ln2_g': (1.0, 0.2),
     'L0_tok_ln2_b': (0.0, 0.1),
     'L0_attn_ln_gamma': (1.0, 0.6),
     'L0_attn_ln_beta': (0.0, 0.369),
     'L0_ffn_gate_b': (0.0, 0.1),
     'L0_ffn_be1': (0.0, 0.725),
     'L0_ffn_be2': (0.0, 0.455),
     'L0_ffn_be3': (0.0, 0.733),
     'L0_ffn_bs1': (0.0, 0.1),
     'L0_ffn_bs2': (0.0, 0.1),
     'L0_ffn_bs3': (0.0, 0.1)}
    factors = {}
    for name, (base, spread) in spreads.items():
        noise = np.random.default_rng([zlib.crc32(name.encode()), seed]).standard_normal(out[name].shape)
        drawn = base * np.exp(spread * noise) if base else spread * noise
        out[name] = jnp.asarray(drawn.astype(out[name].dtype))
    for name, factor in factors.items():
        out[name] = (out[name] * factor).astype(out[name].dtype)
    return out
```

```python
from contextlib import ExitStack

import concourse.bass as bass
from concourse import mybir
from concourse.alu_op_type import AluOpType as ALU

F32 = mybir.dt.float32
ACT = mybir.ActivationFunctionType
AX = mybir.AxisListType

B, C, IMG, PATCH = 32, 3, 96, 16
SIDE = IMG // PATCH
NP = SIDE * SIDE
TXT = 77
N = NP + 1 + TXT
D = 256
KD = D // 128
HEADS, DH = 16, 64
HALF = DH // 2
QUADS = HEADS // 4
SCALE = DH ** -0.5
E, G4, EPG = 16, 4, 4
INTER = 128
SHC = 2
GB = 4
GROUPS = B // GB
GT = GB * N
HB = B // 2
PR = HB * SIDE
PCH = 2 * C
EPS = 1e-5
OC = HEADS * DH // 128
TABLES = 17
HIDDEN = ["s0", "s1"] + list(range(E))
OC = HEADS * DH // 128
TABLES = 17
HIDDEN = ["s0", "s1"] + list(range(E))
OC = HEADS * DH // 128
TABLES = 17
HIDDEN = ["s0", "s1"] + list(range(E))
OC = HEADS * DH // 128
TABLES = 17
HIDDEN = ["s0", "s1"] + list(range(E))
OC = HEADS * DH // 128
TABLES = 17
HIDDEN = ["s0", "s1"] + list(range(E))
OC = HEADS * DH // 128
TABLES = 17
HIDDEN = ["s0", "s1"] + list(range(E))
OC = HEADS * DH // 128
TABLES = 17
HIDDEN = ["s0", "s1"] + list(range(E))
OC = HEADS * DH // 128
TABLES = 17
HIDDEN = ["s0", "s1"] + list(range(E))
FAR = 1e30


class Signal:

    def __init__(self, nc, ctx, name, per_pass):
        self.name, self.per_pass, self.given = name, per_pass, 0
        self.sem = ctx.enter_context(nc.semaphore(name))

    def by(self, ins):
        self.given += 1
        ins.then_inc(self.sem, 1)

    def at(self, g, n):
        return g * self.per_pass + (n + 1)


def pe_bank_schedule():
    turns, uses = {}, [0] * 8

    def put(key, bank):
        turns[key] = (bank, uses[bank])
        uses[bank] += 1

    for kc in range(KD):
        put(("xT", kc), kc)
    for i in range(2 * QUADS):
        for half in range(2):
            put(("qk", i, half), (2 * i + 2 + half) % 8)
    for b in range(GB):
        for n in range(2):
            put(("v", b, n), (2 * b + 2 + n) % 8)

    def scores(b):
        for r in range(4):
            put(("s", b, r), r)

    scores(0)
    for b in range(GB):
        if b + 1 < GB:
            scores(b + 1)
        for c in range(4):
            put(("pT", b, c), 4 + c % 2)
        if b:
            for c in range(2):
                put(("oT", b - 1, c), 4 + c)
        for c in range(2):
            put(("o", b, c), 6 + c)
        if b:
            put(("wo", b - 1), 4)
    for c in range(2):
        put(("oT", GB - 1, c), 4 + c)
    put(("wo", GB - 1), 4)

    for kc in range(KD):
        put(("fT", kc), kc)
    put(("gate",), 6)

    def hidden(key, pair):
        put((key, 1), 2 * pair)
        put((key, 3), 2 * pair + 1)

    hidden("s0", 1)
    hidden("s1", 0)
    hidden(0, 1)
    for p in range(2):
        put(("y", "s", p), 4 + p)
    for e in range(E):
        if e + 1 < E:
            hidden(e + 1, e % 2)
        for p in range(2):
            put(("y", e, p), (6 if e % 2 == 0 else 4) + p)
        if e == 5:
            put(("cT",), 6)
        if e == 6:
            for p in range(2):
                put(("y", "b", p), 4 + p)
    return turns, uses


def early_fusion_program(nc, a, out, zscr):
    TURN, USES = pe_bank_schedule()
    ctx = ExitStack()
    with ctx:
        def sb(name, shape, dt=F32):
            return ctx.enter_context(nc.sbuf_tensor(name, shape, dt))

        def sem(name):
            return ctx.enter_context(nc.semaphore(name))

        signals = []

        def signal(name, per_pass):
            signals.append(Signal(nc, ctx, name, per_pass))
            return signals[-1]

        wqk = sb("wqk", [128, KD, 2, 2, HEADS * HALF])
        wv = sb("wv", [128, KD, HEADS * DH])
        wout = sb("wout", [128, OC, D])
        we1 = sb("we1", [128, E, KD, INTER])
        we3 = sb("we3", [128, E, KD, INTER])
        we2 = sb("we2", [128, E, D])
        ws1 = sb("ws1", [128, KD, SHC * INTER])
        ws3 = sb("ws3", [128, KD, SHC * INTER])
        ws2 = sb("ws2", [128, SHC, D])
        gwT = sb("gwT", [128, KD, E])
        be2s = sb("be2s", [E + 1, D])
        be1T = sb("be1T", [128, E])
        be3T = sb("be3T", [128, E])
        bs1T = sb("bs1T", [128, SHC])
        bs3T = sb("bs3T", [128, SHC])
        lngT = sb("lngT", [128, KD])
        lnbT = sb("lnbT", [128, KD])
        gateb = sb("gateb", [128, E])
        cosT = sb("cosT", [128, N])
        sinT = sb("sinT", [128, N])
        ident = sb("ident", [128, 128])
        tri = sb("tri", [128, E, E])
        pos = sb("pos", [NP + 1, D])
        minus_half = sb("minus_half", [128, 2 * SIDE])
        g1T = sb("g1T", [128, PCH])
        b1T = sb("b1T", [128, PCH])

        qk_space = sb("qk_space", [128, 2 * QUADS * 2 * GT])
        vp_space = sb("vp_space", [128, GB * HEADS * DH + 2 * HEADS * N])
        rope_space = sb("rope_space", [128, 8 * GT])
        o_space = sb("o_space", [128, HEADS * DH])
        h = sb("h", [128, GB, D])
        h2 = sb("h2", [128, GB, D])
        xn = sb("xn", [128, GB, D])
        xT = sb("xT", [128, KD, GT])
        probT = sb("probT", [128, 4, 4 * N])
        oT = sb("oT", [128, OC, N])
        smax = sb("smax", [128, 2, 4, 4])
        ssum = sb("ssum", [128, 2, 4, 4])
        srec = sb("srec", [128, 2, 4, 4])
        gate = sb("gate", [128, 8, GB, E])
        few = sb("few", [128, 8, GB, G4])
        cw = sb("cw", [128, GB, E + 1])
        cT = sb("cT", [E + 1, GT])
        ln_stats = sb("ln_stats", [128, 2, GB, 6])
        ln_mv = sb("ln_mv", [128, 2, GB, 2])
        ln_small = sb("ln_small", [128, 2, 8, GB])
        wait_carrier = sb("wait_carrier", [1, 1])
        tok_stats = sb("tok_stats", [PR, 4, SIDE, C * 6])
        tok_mv = sb("tok_mv", [PR, 4, SIDE, 2])
        tok_small = sb("tok_small", [PR, 4, 2, SIDE])

        def view(space, at, p, shape):
            size = 1
            for s in shape:
                size *= s
            flat = space[0:p, at:at + size]
            names = " ".join(f"d{i}" for i in range(len(shape)))
            return flat.rearrange(f"p ({names}) -> p {names}", **{f"d{i}": s for i, s in enumerate(shape)})

        qkr = view(qk_space, 0, 128, [2, QUADS, 2, GT])
        vv = view(vp_space, 0, 128, [GB, HEADS * DH])
        prob = view(vp_space, GB * HEADS * DH, 128, [2, 4, 4, N])
        rope = view(rope_space, 0, 128, [2, 4, GT])
        o = o_space
        sil = view(rope_space, 0, 128, [2, GT])
        hid = view(rope_space, 2 * GT, 128, [2, GT])
        shid = view(o_space, 0, 128, [SHC, GT])
        pairs = view(vp_space, GB * HEADS * DH, 128, [2, GB, E, E])
        IMGF = C * PATCH * IMG
        img = [view(s, 0, PR, [C, PATCH, SIDE, PATCH]) for s in (qk_space, vp_space)]
        PF = C * PATCH * PATCH
        wp = view(vp_space, IMGF, 128, [PCH, D])
        patch = view(vp_space, IMGF + PCH * D, PR, [2, PF])
        z = [view(qk_space, IMGF, PR, [SIDE, D]), view(rope_space, 0, PR, [SIDE, D])]
        patchT = view(qk_space, IMGF + SIDE * D, 128, [2, PCH, PR])
        bproj = view(rope_space, SIDE * D, PR, [D])
        g2 = view(rope_space, (SIDE + 1) * D, PR, [D])
        b2 = view(rope_space, (SIDE + 2) * D, PR, [D])

        ps = ctx.enter_context(nc.psum_tensor("ps", [128, 8, 512], F32))

        img_in = [sem("img0_in"), sem("img1_in")]
        wp_in = sem("wp_in")
        tok_in = sem("tok_in")
        tables_in = sem("tables_in")
        wqk_in = sem("wqk_in")
        wv_in = sem("wv_in")
        wout_in = sem("wout_in")
        shared_in = sem("shared_in")
        experts_in = sem("experts_in")
        consts = sem("consts")
        z_out = sem("z_out")
        p_stats, p_mv, p_ve, p_rstd = sem("p_stats"), sem("p_mv"), sem("p_ve"), sem("p_rstd")
        p_norm, p_turned, p_affine, p_proj = sem("p_norm"), sem("p_turned"), sem("p_affine"), sem("p_proj")
        z_bias, z_stats, z_mv, z_ve = sem("z_bias"), sem("z_stats"), sem("z_mv"), sem("z_ve")
        z_rstd, z_norm, z_scaled, z_done = sem("z_rstd"), sem("z_norm"), sem("z_scaled"), sem("z_done")
        h_in = sem("h_in")
        out_stored = sem("out_stored")
        full = [signal(f"bank{i}_full", USES[i]) for i in range(8)]
        taken = [signal(f"bank{i}_taken", USES[i]) for i in range(8)]
        h_ready = signal("h_ready", 1)
        ln = {}
        for k in "af":
            ln[k] = {n: signal(f"{k}_{n}", c) for n, c in (("stats", GB), ("mv", GB), ("ve", 1), ("rstd", 1), ("norm", GB))}
        a_v1, a_v2, a_v3, a_r2, a_r12 = (signal(n, 1) for n in ("a_v1", "a_v2", "a_v3", "a_r2", "a_r12"))
        rope_mul = signal("rope_mul", 2 * 2 * QUADS)
        rope_sum = signal("rope_sum", 2 * 2 * QUADS)
        s_max = signal("s_max", 4 * GB)
        s_exp = signal("s_exp", 4 * GB)
        s_sum = signal("s_sum", GB)
        s_rec = signal("s_rec", GB)
        acc_half = signal("acc_half", 2 * (E + 2))
        gate_step = signal("gate_step", 27)
        gate_exp = signal("gate_exp", 1)

        def await_full(eng, g, key):
            bank, turn = TURN[key]
            eng.wait_ge(full[bank].sem, full[bank].at(g, turn + 1))
            return bank

        def await_taken(eng, g, key):
            bank, turn = TURN[key]
            eng.wait_ge(taken[bank].sem, taken[bank].at(g, turn + 1))

        def claim(g, key):
            bank, turn = TURN[key]
            nc.tensor.wait_ge(taken[bank].sem, taken[bank].at(g, turn))
            return bank

        block = ctx.enter_context(nc.Block())

        @block.sync
        def _(sp):
            for half in range(2):
                for i in range(HB):
                    b = half * HB + i
                    sp.dma_start(img[half][i * SIDE:(i + 1) * SIDE, :, :, :, :].rearrange("h c p w q -> h c (p w q)"),
                                 a["x"][b].rearrange("c (h p) w -> h c (p w)", p=PATCH)).then_inc(img_in[half], 16)
            sp.dma_start(wv[:, :, :], a["L0_attn_w_qkv"][:, 2 * HEADS * DH:].rearrange("(c k) n -> k c n", c=KD)).then_inc(wv_in, 16)
            sp.dma_start(wout[:, :, :], a["L0_attn_w_out"].rearrange("(c k) n -> k c n", c=OC)).then_inc(wout_in, 16)
            for w, name in ((ws1, "L0_ffn_ws1"), (ws3, "L0_ffn_ws3"), (ws2, "L0_ffn_ws2")):
                sp.dma_start(w[:, :, :], a[name].rearrange("(c k) n -> k c n", k=128)).then_inc(shared_in, 16)
            for w, name in ((we1, "L0_ffn_We1"), (we3, "L0_ffn_We3")):
                for c in range(KD):
                    sp.dma_start(w[:, :, c, :], a[name][:, c * 128:(c + 1) * 128, :].rearrange("e k n -> k e n")).then_inc(experts_in, 16)
            sp.dma_start(we2[:, :, :], a["L0_ffn_We2"].rearrange("e k n -> k e n")).then_inc(experts_in, 16)
            for half in range(2):
                sp.wait_ge(z_done, half + 1)
                sp.dma_start(zscr[half * HB:(half + 1) * HB, :, :].rearrange("b (h w) d -> (b h) w d", w=SIDE), z[half]).then_inc(z_out, 16)
            sp.wait_ge(z_out, 16 * 2)
            with sp.Fori(0, GROUPS) as g:
                sp.wait_ge(ln["f"]["norm"].sem, ln["f"]["norm"].at(g, 0))
                sp.dma_start(h[0:NP, :, :], zscr[bass.ds(g * GB, GB), :, :].rearrange("b n d -> n b d")).then_inc(h_in, 16)
                sp.dma_start(h[NP:NP + 1, :, :], a["L0_tok_cls_token"][0, :, :].unsqueeze(1).to_broadcast([1, GB, D])).then_inc(h_in, 16)
                sp.dma_start(h[NP + 1:N, :, :], a["txt"][bass.ds(g * GB, GB), :, :].rearrange("b n d -> n b d")).then_inc(h_in, 16)
            sp.wait_ge(out_stored, 16 + 48 * GROUPS)

        @block.gpsimd
        def _(pool):
            for s in signals:
                pool.sem_inc(s.sem, 1)
            pool.sem_inc(out_stored, 16)
            nc.gpsimd.memset(minus_half[:, :], -0.5).then_inc(consts, 1)
            nc.gpsimd.memset(cw[:, :, :], 1.0).then_inc(consts, 1)
            pool.wait_ge(consts, 2)
            for ve_sem, rstd_sem, k in ((p_ve, p_rstd, 0), (z_ve, z_rstd, 1)):
                for half in range(2):
                    pool.wait_ge(ve_sem, half + 1)
                    q = 2 * half + k
                    nc.gpsimd.tensor_tensor(tok_small[:, q, 1, :], tok_small[:, q, 0, :], minus_half[0:PR, 0:SIDE],
                                            ALU.pow).then_inc(rstd_sem, 1)
            with pool.Fori(0, GROUPS) as g:
                def power(k, src, dst, wait, done):
                    pool.wait_ge(wait.sem, wait.at(g, 1))
                    done.by(nc.gpsimd.tensor_tensor(ln_small[0:N, k, dst, :], ln_small[0:N, k, src, :],
                                                    minus_half[0:N, 0:GB], ALU.pow))

                power(0, 0, 1, ln["a"]["ve"], ln["a"]["rstd"])
                power(0, 4, 5, a_v3, a_r2)
                for i in range(2 * QUADS):
                    which, j = divmod(i, QUADS)
                    t = rope[:, i % 2, :, :]
                    pool.wait_ge(rope_mul.sem, rope_mul.at(g, 2 * i + 2))
                    rope_sum.by(nc.gpsimd.tensor_tensor(qkr[:, which, j, 0, :], t[:, 0, :], t[:, 2, :], ALU.subtract))
                    for half in range(2):
                        await_taken(pool, g, ("qk", i, half))
                    rope_sum.by(nc.gpsimd.tensor_tensor(qkr[:, which, j, 1, :], t[:, 3, :], t[:, 1, :], ALU.add))
                power(1, 0, 1, ln["f"]["ve"], ln["f"]["rstd"])

        @block.scalar
        def _(act):
            act.dma_start(wp[:, :, :].rearrange("p (c k) e -> p c k e", c=C)[:, :, 0, :],
                          a["L0_tok_W_proj"].rearrange("(k q c) e -> q k c e", k=2, c=C)[:, 0, :, :]).then_inc(wp_in, 16)
            act.dma_start(wp[:, :, :].rearrange("p (c k) e -> p c k e", c=C)[:, :, 1, :],
                          a["L0_tok_W_proj"].rearrange("(k q c) e -> q k c e", k=2, c=C)[:, 1, :, :]).then_inc(wp_in, 16)
            for t, name in ((g1T, "L0_tok_ln1_g"), (b1T, "L0_tok_ln1_b")):
                for c in range(C):
                    act.dma_start(t[:, 2 * c:2 * c + 2], a[name].rearrange("(k q c) -> q c k", k=2, c=C)[:, c, :],
                                  allow_slow_non_contiguous=True).then_inc(tok_in, 16)
            for t, name in ((bproj, "L0_tok_b_proj"), (g2, "L0_tok_ln2_g"), (b2, "L0_tok_ln2_b")):
                act.dma_start(t, a[name].partition_broadcast(PR)).then_inc(tok_in, 16)
            act.dma_start(ident[:, :], a["ident"]).then_inc(tables_in, 16)
            act.dma_start(cosT[:, :], a["cosT"]).then_inc(tables_in, 16)
            act.dma_start(sinT[:, :], a["sinT"]).then_inc(tables_in, 16)
            act.dma_start(tri[:, :, :].rearrange("p a b -> p (a b)"), a["tri"].partition_broadcast(128)).then_inc(tables_in, 16)
            act.dma_start(pos[0:NP, :], a["L0_tok_pos_emb"][0, 1:NP + 1, :]).then_inc(tables_in, 16)
            act.dma_start(pos[NP:NP + 1, :], a["L0_tok_pos_emb"][0, 0:1, :]).then_inc(tables_in, 16)
            act.dma_start(gateb[:, :], a["L0_ffn_gate_b"].partition_broadcast(128)).then_inc(tables_in, 16)
            for t, name in ((lngT, "L0_attn_ln_gamma"), (lnbT, "L0_attn_ln_beta"), (bs1T, "L0_ffn_bs1"), (bs3T, "L0_ffn_bs3")):
                act.dma_start(t[:, :], a[name].rearrange("(c k) -> k c", k=128), allow_slow_non_contiguous=True).then_inc(tables_in, 16)
            for t, name in ((be1T, "L0_ffn_be1"), (be3T, "L0_ffn_be3")):
                act.dma_start(t[:, :], a[name].rearrange("e k -> k e"), allow_slow_non_contiguous=True).then_inc(tables_in, 16)
            for c in range(KD):
                act.dma_start(gwT[:, c, :], a["L0_ffn_gate_w"][:, c * 128:(c + 1) * 128].rearrange("e k -> k e"),
                              allow_slow_non_contiguous=True).then_inc(tables_in, 16)
            act.dma_start(be2s[0:E, :], a["L0_ffn_be2"]).then_inc(tables_in, 16)
            act.dma_start(be2s[E:E + 1, :], a["L0_ffn_bs2"].unsqueeze(0)).then_inc(tables_in, 16)
            for kc in range(KD):
                for which in range(2):
                    for half in range(2):
                        act.dma_start(
                            wqk[:, kc, which, half, :].rearrange("k (h i) -> k h i", i=HALF),
                            a["L0_attn_w_qkv"][kc * 128:(kc + 1) * 128, which * HEADS * DH:(which + 1) * HEADS * DH]
                            .rearrange("k (h f i) -> k f h i", f=2, i=HALF)[:, half, :, :]).then_inc(wqk_in, 16)

            act.wait_ge(tok_in, 16 * 9)
            for t in range(2 * SIDE):
                act.wait_ge(p_turned, t + 1)
                if t >= 2:
                    act.wait_ge(p_proj, t - 1)
                for m in range(PCH):
                    last = nc.scalar.activation(patchT[:, t % 2, m, :], ps[:, 2 * (t % 2) + m // 3, (m % 3) * PR:(m % 3 + 1) * PR],
                                                ACT.Identity, scale=g1T[:, m:m + 1], bias=b1T[:, m:m + 1])
                    last.then_inc(p_affine, 1)
            act.wait_ge(tables_in, 16 * TABLES)

            with act.Fori(0, GROUPS) as g:
                for kc in range(KD):
                    bank = await_full(act, g, ("xT", kc))
                    taken[bank].by(nc.scalar.activation(xT[:, kc, :], ps[:, bank, 0:GT], ACT.Identity,
                                                        scale=lngT[:, kc:kc + 1], bias=lnbT[:, kc:kc + 1]))
                for b in range(GB):
                    for n in range(2):
                        bank = await_full(act, g, ("v", b, n))
                        taken[bank].by(nc.scalar.copy(vv[0:N, b, n * 512:(n + 1) * 512], ps[0:N, bank, :]))

                def softmax_exp(b):
                    for r in range(4):
                        await_taken(act, g, ("s", b, r))
                        p = prob[0:N, b % 2, r, :, :]
                        s_exp.by(nc.scalar.activation(p, p, ACT.Exp, scale=SCALE))

                def take_oT(b):
                    for c in range(2):
                        bank = await_full(act, g, ("oT", b, c))
                        taken[bank].by(nc.scalar.copy(oT[:, 4 * c:4 * c + 4, :], ps[:, bank, 0:4 * N].rearrange("p (m t) -> p m t", m=4)))

                softmax_exp(0)
                for b in range(GB):
                    if b:
                        await_full(act, g, ("o", b - 1, 1))
                    for r in range(4):
                        bank = await_full(act, g, ("pT", b, r))
                        taken[bank].by(nc.scalar.copy(probT[0:N, r, :], ps[0:N, bank, 0:4 * N]))
                    if b:
                        take_oT(b - 1)
                    if b + 1 < GB:
                        softmax_exp(b + 1)
                take_oT(GB - 1)

                for kc in range(KD):
                    bank = await_full(act, g, ("fT", kc))
                    taken[bank].by(nc.scalar.copy(xT[:, kc, :], ps[:, bank, 0:GT]))

                def silu(q):
                    key = HIDDEN[q]
                    bias = bs1T[:, q:q + 1] if q < SHC else be1T[:, key:key + 1]
                    bank = await_full(act, g, (key, 1))
                    if q >= 2:
                        await_taken(act, g, (HIDDEN[q - 2], 3))
                    taken[bank].by(nc.scalar.activation(sil[:, q % 2, :], ps[:, bank, 0:GT], ACT.Silu, bias=bias))

                for q in range(3):
                    silu(q)
                await_taken(act, g, ("gate",))
                gate_exp.by(nc.scalar.activation(gate[0:N, 1, :, :], gate[0:N, 0, :, :], ACT.Exp))
                for q in range(3, len(HIDDEN)):
                    silu(q)
                    if q == 3 + 6:
                        bank = await_full(act, g, ("cT",))
                        taken[bank].by(nc.scalar.copy(cT[:, :], ps[0:E + 1, bank, 0:GT]))
                act.wait_ge(acc_half.sem, acc_half.at(g, 2 * (E + 2)))
                for p in range(2):
                    await_taken(act, g, ("y", E - 1, p))
                for lo, hi, t0 in ((0, NP, 1), (NP, NP + 1, 0), (NP + 1, N, NP + 1)):
                    act.dma_start(out[bass.ds(g * GB, GB), t0:t0 + hi - lo, :].rearrange("b n d -> n b d"),
                                  h2[lo:hi, :, :]).then_inc(out_stored, 16)

        @block.vector
        def _(dve):
            def patch_stats(half):
                dve.wait_ge(img_in[half], 16 * HB)
                for w in range(SIDE):
                    for c in range(C):
                        nc.vector.bn_stats(tok_stats[:, 2 * half, w, 6 * c:6 * c + 6], img[half][:, c, :, w, :]).then_inc(p_stats, 1)
                dve.wait_ge(p_stats, C * SIDE * (half + 1))
                for w in range(SIDE):
                    nc.vector.bn_aggr(tok_mv[:, 2 * half, w, :], tok_stats[:, 2 * half, w, :]).then_inc(p_mv, 1)
                dve.wait_ge(p_mv, SIDE * (half + 1))
                nc.vector.tensor_scalar(tok_small[:, 2 * half, 0, :], tok_mv[:, 2 * half, :, 1], EPS, None, ALU.add).then_inc(p_ve, 1)

            def patch_norm(t):
                half, w = divmod(t, SIDE)
                if t >= 2:
                    dve.wait_ge(p_turned, t - 1)
                nc.vector.tensor_scalar(patch[:, t % 2, :].rearrange("p (c a q) -> p c a q", c=C, a=PATCH), img[half][:, :, :, w, :],
                                        tok_mv[:, 2 * half, w, 0:1], tok_small[:, 2 * half, 1, w:w + 1],
                                        ALU.subtract, ALU.mult).then_inc(p_norm, 1)

            def token_stats(t):
                half, w = divmod(t, SIDE)
                dve.wait_ge(p_proj, t + 1)
                nc.vector.tensor_tensor(z[half][:, w, :], ps[0:PR, 4 + t % 2, 0:D], bproj, ALU.add).then_inc(z_bias, 1)
                dve.wait_ge(z_bias, t + 1)
                nc.vector.bn_stats(tok_stats[:, 2 * half + 1, w, 0:6], z[half][:, w, :]).then_inc(z_stats, 1)

            def token_norm(half):
                q = 2 * half + 1
                dve.wait_ge(z_stats, SIDE * (half + 1))
                for w in range(SIDE):
                    nc.vector.bn_aggr(tok_mv[:, q, w, :], tok_stats[:, q, w, 0:6]).then_inc(z_mv, 1)
                dve.wait_ge(z_mv, SIDE * (half + 1))
                nc.vector.tensor_scalar(tok_small[:, q, 0, :], tok_mv[:, q, :, 1], EPS, None, ALU.add).then_inc(z_ve, 1)
                dve.wait_ge(z_rstd, half + 1)
                for w in range(SIDE):
                    zz = z[half][:, w, :]
                    nc.vector.tensor_scalar(zz, zz, tok_mv[:, q, w, 0:1], tok_small[:, q, 1, w:w + 1], ALU.subtract, ALU.mult).then_inc(z_norm, 1)
                dve.wait_ge(z_norm, SIDE * (half + 1))
                zz = z[half][:, :, :]
                nc.vector.tensor_tensor(zz, zz, g2.unsqueeze(1).to_broadcast([PR, SIDE, D]), ALU.mult).then_inc(z_scaled, 1)
                dve.wait_ge(z_scaled, half + 1)
                nc.vector.tensor_tensor(zz, zz, b2.unsqueeze(1).to_broadcast([PR, SIDE, D]), ALU.add).then_inc(z_done, 1)

            dve.wait_ge(tok_in, 16 * 9)
            patch_stats(0)
            for t in range(2 * SIDE):
                if t % SIDE == 0:
                    dve.wait_ge(p_rstd, t // SIDE + 1)
                patch_norm(t)
                if t:
                    token_stats(t - 1)
                if t == 2:
                    patch_stats(1)
                if t == SIDE:
                    token_norm(0)
            token_stats(2 * SIDE - 1)
            token_norm(1)

            dve.wait_ge(tables_in, 16 * TABLES)
            dve.wait_ge(consts, 2)

            with dve.Fori(0, GROUPS) as g:
                def own(s, n):
                    dve.wait_ge(s.sem, s.at(g, n))

                def normalise(k, src, twice):
                    s, i = ln[k], "af".index(k)
                    sm = ln_small[0:N, i, :, :]
                    var = ln_mv[0:N, i, :, 1]
                    for b in range(GB):
                        s["stats"].by(nc.vector.bn_stats(ln_stats[0:N, i, b, :], src[0:N, b, :]))
                    own(s["stats"], GB)
                    nc.vector.memset(wait_carrier[:, :], 0.0)
                    for b in range(GB):
                        s["mv"].by(nc.vector.bn_aggr(ln_mv[0:N, i, b, :], ln_stats[0:N, i, b, :]))
                    own(s["mv"], GB)
                    s["ve"].by(nc.vector.tensor_scalar(sm[:, 0, :], var, EPS, None, ALU.add))
                    dve.wait_ge(s["rstd"].sem, s["rstd"].at(g, 1))
                    r = 1
                    if twice:
                        a_v1.by(nc.vector.tensor_tensor(sm[:, 2, :], var, sm[:, 1, :], ALU.mult))
                        own(a_v1, 1)
                        a_v2.by(nc.vector.tensor_tensor(sm[:, 3, :], sm[:, 2, :], sm[:, 1, :], ALU.mult))
                        own(a_v2, 1)
                        a_v3.by(nc.vector.tensor_scalar(sm[:, 4, :], sm[:, 3, :], EPS, None, ALU.add))
                        dve.wait_ge(a_r2.sem, a_r2.at(g, 1))
                        a_r12.by(nc.vector.tensor_tensor(sm[:, 6, :], sm[:, 1, :], sm[:, 5, :], ALU.mult))
                        own(a_r12, 1)
                        r = 6
                    for b in range(GB):
                        s["norm"].by(nc.vector.tensor_scalar(xn[0:N, b, :], src[0:N, b, :], ln_mv[0:N, i, b, 0:1], sm[:, r, b:b + 1],
                                                             ALU.subtract, ALU.mult))

                dve.wait_ge(h_in, g * 48 + 48)
                h_ready.by(nc.vector.tensor_tensor(h[0:NP + 1, :, :], h[0:NP + 1, :, :],
                                                   pos[:, :].unsqueeze(1).to_broadcast([NP + 1, GB, D]), ALU.add))
                own(h_ready, 1)
                normalise("a", h, True)

                cos = cosT[:, :].unsqueeze(1).to_broadcast([128, GB, N])
                sin = sinT[:, :].unsqueeze(1).to_broadcast([128, GB, N])

                def by_image(ap):
                    return ap.rearrange("p (b t) -> p b t", b=GB)

                for i in range(2 * QUADS):
                    if i == 0:
                        dve.wait_ge(rope_sum.sem, rope_sum.at(g, 0))
                    if i >= 2:
                        dve.wait_ge(rope_sum.sem, rope_sum.at(g, 2 * i - 2))
                    for half, (first, second) in enumerate(((cos, sin), (sin, cos))):
                        bank = await_full(dve, g, ("qk", i, half))
                        x = by_image(ps[:, bank, 0:GT])
                        t = rope[:, i % 2, 2 * half:2 * half + 2, :]
                        rope_mul.by(nc.vector.tensor_tensor(by_image(t[:, 0, :]), x, first, ALU.mult))
                        taken[bank].by(nc.vector.tensor_tensor(by_image(t[:, 1, :]), x, second, ALU.mult))

                def centre(b):
                    for r in range(4):
                        bank = await_full(dve, g, ("s", b, r))
                        s_max.by(nc.vector.tensor_reduce(smax[0:N, b % 2, r, :], ps[0:N, bank, 0:4 * N].rearrange("p (j t) -> p j t", j=4),
                                                         AX.X, ALU.max))
                    for r in range(4):
                        own(s_max, 4 * b + r + 1)
                        bank = TURN[("s", b, r)][0]
                        taken[bank].by(nc.vector.tensor_tensor(
                            prob[0:N, b % 2, r, :, :], ps[0:N, bank, 0:4 * N].rearrange("p (j t) -> p j t", j=4),
                            smax[0:N, b % 2, r, :].unsqueeze(2).to_broadcast([N, 4, N]), ALU.subtract))

                def add_attention(b):
                    bank = await_full(dve, g, ("wo", b))
                    taken[bank].by(nc.vector.tensor_tensor(h2[0:N, b, :], ps[0:N, bank, 0:D], h[0:N, b, :], ALU.add))

                dve.wait_ge(out_stored, g * 48 + 16)
                centre(0)
                for b in range(GB):
                    if b + 1 < GB:
                        centre(b + 1)
                    dve.wait_ge(s_exp.sem, s_exp.at(g, 4 * b + 4))
                    s_sum.by(nc.vector.tensor_reduce(ssum[0:N, b % 2, :, :], prob[0:N, b % 2, :, :, :], AX.X, ALU.add))
                    own(s_sum, b + 1)
                    s_rec.by(nc.vector.reciprocal(srec[0:N, b % 2, :, :], ssum[0:N, b % 2, :, :]))
                    own(s_rec, b + 1)
                    for c in range(2):
                        bank = await_full(dve, g, ("o", b, c))
                        inv = srec[0:N, b % 2, :, 2 * c:2 * c + 2].rearrange("p r j -> p j r").unsqueeze(3).to_broadcast([N, 2, 4, DH])
                        taken[bank].by(nc.vector.tensor_tensor(
                            o[0:N, c * 512:(c + 1) * 512].rearrange("p (j r d) -> p j r d", j=2, r=4),
                            ps[0:N, bank, :].rearrange("p (j r d) -> p j r d", j=2, r=4), inv, ALU.mult))
                    if b:
                        add_attention(b - 1)
                add_attention(GB - 1)
                await_taken(dve, g, ("wo", GB - 1))
                normalise("f", h2, False)

                def gated(q):
                    key = HIDDEN[q]
                    bias = bs3T[:, q:q + 1] if q < SHC else be3T[:, key:key + 1]
                    dst = shid[:, q, :] if q < SHC else hid[:, key % 2, :]
                    await_taken(dve, g, (key, 1))
                    bank = await_full(dve, g, (key, 3))
                    taken[bank].by(nc.vector.scalar_tensor_tensor(dst, ps[:, bank, 0:GT], bias, sil[:, q % 2, :], ALU.add, ALU.mult))

                summed = []

                def add_out(e):
                    for p in range(2):
                        bank = await_full(dve, g, ("y", e, p))
                        for bb in range(2):
                            b = 2 * p + bb
                            if summed:
                                own(acc_half, 2 * (len(summed) - 1) + p + 1) if bb == 0 else await_taken(dve, g, ("y", summed[-1], p))
                            src = ps[0:N, bank, bb * D:(bb + 1) * D]
                            if e in ("s", "b"):
                                ins = nc.vector.tensor_tensor(h2[0:N, b, :], src, h2[0:N, b, :], ALU.add)
                            else:
                                ins = nc.vector.scalar_tensor_tensor(h2[0:N, b, :], src, cw[0:N, b, e:e + 1], h2[0:N, b, :], ALU.mult, ALU.add)
                            (taken[bank] if bb else acc_half).by(ins)
                    summed.append(e)

                steps = [0]

                def step(ins):
                    gate_step.by(ins)
                    steps[0] += 1
                    own(gate_step, steps[0])

                def beats(dst, tmp, x, n):
                    other = x.unsqueeze(2).to_broadcast([N, GB, n, n])
                    own_x = x.unsqueeze(3).to_broadcast([N, GB, n, n])
                    low = tri[0:N, 0:n, 0:n].unsqueeze(1).to_broadcast([N, GB, n, n])
                    step(nc.vector.tensor_tensor(dst, other, own_x, ALU.is_equal))
                    step(nc.vector.tensor_tensor(dst, dst, low, ALU.mult))
                    step(nc.vector.tensor_tensor(tmp, other, own_x, ALU.is_gt))
                    step(nc.vector.tensor_tensor(dst, dst, tmp, ALU.add))

                def route():
                    bank = await_full(dve, g, ("gate",))
                    logits = ps[0:N, bank, 0:GB * E].rearrange("p (b e) -> p b e", b=GB)
                    G = [gate[0:N, i, :, :] for i in range(8)]
                    S = [few[0:N, i, :, :] for i in range(8)]
                    mx, sm, rs = S[0][:, :, 0], S[0][:, :, 1], S[0][:, :, 2]

                    def over(x, n):
                        return x.unsqueeze(2).to_broadcast([N, GB, n])

                    step(nc.vector.tensor_reduce(mx, logits, AX.X, ALU.max))
                    taken[bank].by(nc.vector.tensor_tensor(G[0], logits, over(mx, E), ALU.subtract))
                    dve.wait_ge(gate_exp.sem, gate_exp.at(g, 1))
                    step(nc.vector.tensor_reduce(sm, G[1], AX.X, ALU.add))
                    step(nc.vector.reciprocal(rs, sm))
                    prob_e, biased = G[2], G[3]
                    step(nc.vector.tensor_tensor(prob_e, G[1], over(rs, E), ALU.mult))
                    step(nc.vector.tensor_tensor(biased, prob_e, gateb[0:N, :].unsqueeze(1).to_broadcast([N, GB, E]), ALU.add))
                    quad = biased.rearrange("p b (g h i) -> p (b g) h i", g=G4, h=2)
                    hi = G[4].rearrange("p b (x i) -> p (b x) i", i=2)[:, 0:GB * G4, :]
                    lo = G[5].rearrange("p b (x i) -> p (b x) i", i=2)[:, 0:GB * G4, :]
                    first, second = (S[i].rearrange("p b g -> p (b g)") for i in (1, 2))
                    tmp = S[3].rearrange("p b g -> p (b g)")
                    step(nc.vector.tensor_tensor(hi, quad[:, :, 0, :], quad[:, :, 1, :], ALU.max))
                    step(nc.vector.tensor_tensor(lo, quad[:, :, 0, :], quad[:, :, 1, :], ALU.min))
                    step(nc.vector.tensor_tensor(first, hi[:, :, 0], hi[:, :, 1], ALU.max))
                    step(nc.vector.tensor_tensor(second, hi[:, :, 0], hi[:, :, 1], ALU.min))
                    step(nc.vector.tensor_tensor(tmp, lo[:, :, 0], lo[:, :, 1], ALU.max))
                    step(nc.vector.tensor_tensor(second, second, tmp, ALU.max))
                    step(nc.vector.tensor_tensor(S[4], S[1], S[2], ALU.add))
                    small = [pairs[0:N, i, :, 0:1, :].rearrange("p b o (x y) -> p b (o x) y", y=G4) for i in range(2)]
                    beats(small[0], small[1], S[4], G4)
                    step(nc.vector.tensor_reduce(S[5], small[0], AX.X, ALU.add))
                    step(nc.vector.tensor_scalar(S[6], S[5], 2.0, None, ALU.is_lt))
                    step(nc.vector.tensor_scalar(S[7], S[6], 1.0, FAR, ALU.subtract, ALU.mult))
                    def spread(x):
                        return x.unsqueeze(3).to_broadcast([N, GB, G4, EPG])

                    def grouped(x):
                        return x.rearrange("p b (g i) -> p b g i", g=G4)

                    step(nc.vector.tensor_tensor(grouped(G[4]), grouped(biased), spread(S[6]), ALU.mult))
                    step(nc.vector.tensor_tensor(grouped(G[4]), grouped(G[4]), spread(S[7]), ALU.add))
                    big = [pairs[0:N, i, :, :, :] for i in range(2)]
                    beats(big[0], big[1], G[4], E)
                    step(nc.vector.tensor_reduce(G[5], big[0], AX.X, ALU.add))
                    step(nc.vector.scalar_tensor_tensor(cw[0:N, :, 0:E], G[5], 2.0, prob_e, ALU.is_lt, ALU.mult))
                    assert steps[0] == gate_step.per_pass, steps

                for q in range(3):
                    gated(q)
                add_out("s")
                route()
                for e in range(E):
                    if e + 1 < E:
                        gated(SHC + e + 1)
                    add_out(e)
                    if e == 6:
                        add_out("b")

        @block.tensor
        def _(pe):
            pe.wait_ge(tables_in, 16 * TABLES)
            pe.wait_ge(wp_in, 16 * 2)
            def turn(t):
                pe.wait_ge(p_norm, t + 1)
                if t >= 2:
                    pe.wait_ge(p_affine, PCH * (t - 1))
                for m in range(PCH):
                    last = nc.tensor.transpose(ps[:, 2 * (t % 2) + m // 3, (m % 3) * PR:(m % 3 + 1) * PR],
                                               patch[:, t % 2, m * 128:(m + 1) * 128], ident[0:PR, 0:PR])
                last.then_inc(p_turned, 1)

            def project(t):
                pe.wait_ge(p_affine, PCH * (t + 1))
                if t >= 2:
                    pe.wait_ge(z_bias, t - 1)
                for m in range(PCH):
                    last = nc.tensor.matmul(ps[0:PR, 4 + t % 2, 0:D], patchT[:, t % 2, m, :], wp[:, m, :],
                                            start=(m == 0), stop=(m == PCH - 1))
                last.then_inc(p_proj, 1)

            turn(0)
            for t in range(2 * SIDE):
                if t + 1 < 2 * SIDE:
                    turn(t + 1)
                project(t)
            for s, n in ((wqk_in, 8), (wv_in, 1), (wout_in, 1), (shared_in, 3), (experts_in, 5)):
                pe.wait_ge(s, 16 * n)

            with pe.Fori(0, GROUPS) as g:
                def turn_tokens(key, s):
                    pe.wait_ge(s.sem, s.at(g, GB))
                    for kc in range(KD):
                        bank = claim(g, (key, kc))
                        for b in range(GB):
                            last = nc.tensor.transpose(ps[:, bank, b * N:(b + 1) * N], xn[0:N, b, kc * 128:(kc + 1) * 128], ident[0:N, 0:N])
                        full[bank].by(last)
                    for kc in range(KD):
                        await_taken(pe, g, (key, kc))

                def over_features(bank, w, rows=slice(0, GT), dst=None):
                    for kc in range(KD):
                        last = nc.tensor.matmul(ps[:, bank, 0:GT], w(kc), xT[:, kc, rows], start=(kc == 0), stop=(kc == KD - 1))
                    full[bank].by(last)

                turn_tokens("xT", ln["a"]["norm"])
                for i in range(2 * QUADS):
                    which, j = divmod(i, QUADS)
                    for half in range(2):
                        over_features(claim(g, ("qk", i, half)), lambda kc: wqk[:, kc, which, half, j * 128:(j + 1) * 128])
                for b in range(GB):
                    for n in range(2):
                        bank = claim(g, ("v", b, n))
                        for kc in range(KD):
                            last = nc.tensor.matmul(ps[0:N, bank, :], xT[:, kc, b * N:(b + 1) * N], wv[:, kc, n * 512:(n + 1) * 512],
                                                    start=(kc == 0), stop=(kc == KD - 1))
                        full[bank].by(last)

                def scores(b):
                    cols = slice(b * N, (b + 1) * N)
                    for r in range(4):
                        claim(g, ("s", b, r))
                    for j in range(QUADS):
                        for r in range(4):
                            rows = slice(HALF * r, HALF * (r + 1))
                            for half in range(2):
                                last = nc.tensor.matmul(ps[0:N, r, j * N:(j + 1) * N], qkr[rows, 0, j, half, cols], qkr[rows, 1, j, half, cols],
                                                        start=(half == 0), stop=(half == 1))
                            if j == QUADS - 1:
                                full[r].by(last)

                def turn_probs(b):
                    for r in range(4):
                        pe.wait_ge(s_exp.sem, s_exp.at(g, 4 * b + r + 1))
                        bank = claim(g, ("pT", b, r))
                        for j in range(QUADS):
                            last = nc.tensor.transpose(ps[0:N, bank, j * N:(j + 1) * N], prob[0:N, b % 2, r, j, :], ident[0:N, 0:N])
                        full[bank].by(last)

                def attend(b):
                    for r in range(4):
                        await_taken(pe, g, ("pT", b, r))
                    for c in range(2):
                        bank = claim(g, ("o", b, c))
                        for i in range(8):
                            head = 8 * c + i
                            j, r = divmod(head, 4)
                            last = nc.tensor.matmul(ps[0:N, bank, i * DH:(i + 1) * DH], probT[0:N, r, j * N:(j + 1) * N],
                                                    vv[0:N, b, head * DH:(head + 1) * DH], start=True, stop=True)
                        full[bank].by(last)

                def turn_heads(b):
                    for c in range(2):
                        await_taken(pe, g, ("o", b, c))
                    for c in range(2):
                        bank = claim(g, ("oT", b, c))
                        for m in range(4):
                            chunk = 4 * c + m
                            last = nc.tensor.transpose(ps[:, bank, m * N:(m + 1) * N], o[0:N, chunk * 128:(chunk + 1) * 128], ident[0:N, 0:N])
                        full[bank].by(last)

                def project_heads(b):
                    for c in range(2):
                        await_taken(pe, g, ("oT", b, c))
                    bank = claim(g, ("wo", b))
                    for c in range(OC):
                        last = nc.tensor.matmul(ps[0:N, bank, 0:D], oT[:, c, :], wout[:, c, :], start=(c == 0), stop=(c == OC - 1))
                    full[bank].by(last)

                pe.wait_ge(rope_sum.sem, rope_sum.at(g, 4 * QUADS))
                scores(0)
                for b in range(GB):
                    if b == 0:
                        for bb in range(GB):
                            for n in range(2):
                                await_taken(pe, g, ("v", bb, n))
                    if b + 1 < GB:
                        scores(b + 1)
                    turn_probs(b)
                    if b:
                        turn_heads(b - 1)
                    attend(b)
                    if b:
                        project_heads(b - 1)
                turn_heads(GB - 1)
                project_heads(GB - 1)

                turn_tokens("fT", ln["f"]["norm"])
                bank = claim(g, ("gate",))
                for b in range(GB):
                    for kc in range(KD):
                        last = nc.tensor.matmul(ps[0:N, bank, b * E:(b + 1) * E], xT[:, kc, b * N:(b + 1) * N], gwT[:, kc, :],
                                                start=(kc == 0), stop=(kc == KD - 1))
                full[bank].by(last)

                def hidden(q):
                    key = HIDDEN[q]
                    for n, (ws, we) in ((1, (ws1, we1)), (3, (ws3, we3))):
                        over_features(claim(g, (key, n)),
                                      (lambda kc: ws[:, kc, q * 128:(q + 1) * 128]) if q < SHC else (lambda kc: we[:, key, kc, :]))

                def out_rows(key, lhs, rhs):
                    for p in range(2):
                        bank = claim(g, ("y", key, p))
                        for bb in range(2):
                            b = 2 * p + bb
                            for c in range(len(lhs)):
                                last = nc.tensor.matmul(ps[0:N, bank, bb * D:(bb + 1) * D], lhs[c][:, b * N:(b + 1) * N], rhs[c],
                                                        start=(c == 0), stop=(c == len(lhs) - 1))
                        full[bank].by(last)

                for q in range(3):
                    hidden(q)
                for q in range(SHC):
                    await_taken(pe, g, (HIDDEN[q], 3))
                out_rows("s", [shid[:, c, :] for c in range(SHC)], [ws2[:, c, :] for c in range(SHC)])
                for e in range(E):
                    if e + 1 < E:
                        hidden(SHC + e + 1)
                    await_taken(pe, g, (e, 3))
                    out_rows(e, [hid[:, e % 2, :]], [we2[:, e, :]])
                    if e == 5:
                        pe.wait_ge(gate_step.sem, gate_step.at(g, gate_step.per_pass))
                        bank = claim(g, ("cT",))
                        for b in range(GB):
                            last = nc.tensor.transpose(ps[0:E + 1, bank, b * N:(b + 1) * N], cw[0:N, b, :], ident[0:N, 0:N])
                        full[bank].by(last)
                    if e == 6:
                        await_taken(pe, g, ("cT",))
                        out_rows("b", [cT[:, :]], [be2s[:, :]])

        for s in signals:
            assert s.given == s.per_pass, (s.name, s.given, s.per_pass)


INPUTS = ["x", "txt", "L0_tok_ln1_g", "L0_tok_ln1_b", "L0_tok_W_proj", "L0_tok_b_proj", "L0_tok_ln2_g", "L0_tok_ln2_b",
          "L0_tok_cls_token", "L0_tok_pos_emb", "L0_attn_ln_gamma", "L0_attn_ln_beta", "L0_attn_w_qkv", "L0_attn_w_out",
          "L0_ffn_gate_w", "L0_ffn_gate_b", "L0_ffn_We1", "L0_ffn_be1", "L0_ffn_We2", "L0_ffn_be2", "L0_ffn_We3",
          "L0_ffn_be3", "L0_ffn_ws1", "L0_ffn_bs1", "L0_ffn_ws2", "L0_ffn_bs2", "L0_ffn_ws3", "L0_ffn_bs3"]


def shape_constants():
    import numpy as np
    inv = (1.0 / 10000.0 ** (np.arange(0, DH, 2, dtype=np.float32) / np.float32(DH))).astype(np.float32)
    rows = np.arange(N)
    step = np.where(rows < NP, rows, np.where(rows == NP, 0, rows - 1)).astype(np.float32)
    angle = (inv[:, None] * step[None, :]).astype(np.float32)
    return {"cosT": np.tile(np.cos(angle), (4, 1)).astype(np.float32), "sinT": np.tile(np.sin(angle), (4, 1)).astype(np.float32),
            "ident": np.eye(128, dtype=np.float32),
            "tri": (np.arange(E)[None, :] < np.arange(E)[:, None]).astype(np.float32).reshape(-1)}


def kernel(**inputs):
    import numpy as np
    import concourse.bacc as bacc
    from concourse.bass_utils import run_bass_kernel_spmd

    nc = bacc.Bacc("TRN2", target_bir_lowering=False, num_devices=1)
    arrays, aps = {}, {}
    for name, array in [(n, inputs[n]) for n in INPUTS] + list(shape_constants().items()):
        array = np.ascontiguousarray(array)
        arrays[f"in_{name}"] = array
        aps[name] = nc.dram_tensor(f"in_{name}", array.shape, F32, kind="ExternalInput").ap()
    zscr = nc.dram_tensor("image_tokens", (B, NP, D), F32, kind="Internal").ap()
    out = nc.dram_tensor("out_0", (B, N, D), F32, kind="ExternalOutput").ap()
    early_fusion_program(nc, aps, out, zscr)
    result = run_bass_kernel_spmd(nc, [arrays], core_ids=[0])
    return result.results[0]["out_0"]
```

```python
from contextlib import ExitStack

import concourse.bass as bass
from concourse import mybir
from concourse.alu_op_type import AluOpType as ALU

F32 = mybir.dt.float32
I32 = mybir.dt.int32
U32 = mybir.dt.uint32
ACT = mybir.ActivationFunctionType
AX = mybir.AxisListType

B, C, IMG, PATCH = 32, 3, 96, 16
SIDE = IMG // PATCH
NP = SIDE * SIDE
TXT = 77
N = NP + 1 + TXT
D = 256
KD = D // 128
HEADS, DH = 16, 64
HALF = DH // 2
QUADS = HEADS // 4
SCALE = DH ** -0.5
E, G4, EPG = 16, 4, 4
INTER = 128
SHC = 2
GB = 4
GROUPS = B // GB
GT = GB * N
HB = B // 2
PR = HB * SIDE
PCH = 2 * C
EPS = 1e-5
OC = HEADS * DH // 128
ROPES = 2
TABLES = 18

TS = 128
TOPK = 2
CAP = B * N + TS
TILES = (B * N * TOPK - E) // TS + E
ONE = D + E
IDS = ONE + 1
ROW = IDS + E
TRASH = TOPK * B * N
PLACES = 4
UNROLL = 4
BEHIND, WINDOW = 3, 6
COUNT_EXPERT, COUNT_BASE, COUNT_TILE, COUNT_TRASH, COUNT_DOWN, COUNT_FULL = 0, E, 2 * E, 2 * E + TILES, 2 * E + 2 * TILES, 3 * E + 2 * TILES
COUNTS = COUNT_FULL + -(-B * N // TS)
CHOSEN_STEP = 33
GATE_STEPS = CHOSEN_STEP + 7
PAD_STEPS = 3
TABLE_STEPS = 20 + 6
FAR = 1e30


class Signal:

    def __init__(self, nc, ctx, name, per_pass, start=1):
        self.name, self.per_pass, self.start, self.given = name, per_pass, start, 0
        self.sem = ctx.enter_context(nc.semaphore(name))

    def by(self, ins, count=1):
        self.given += count
        ins.then_inc(self.sem, count)

    def at(self, g, n):
        return g * self.per_pass + (n + self.start)


LATE_KEYS = [("rank",), ("cT",), ("y", "b", 0), ("y", "b", 1)]


def pe_bank_schedule():
    turns, uses = {}, [0] * 8

    def put(key, bank):
        turns[key] = (bank, uses[bank])
        uses[bank] += 1

    def values(b):
        for n in range(2):
            put(("v", b, n), 2 * b + n)

    def scores(b):
        for r in range(4):
            put(("s", b, r), r)

    scores(0)
    values(2)
    values(3)
    for b in range(GB):
        if b + 1 < GB:
            scores(b + 1)
        for c in range(4):
            put(("pT", b, c), 4 + c % 2)
        if b:
            for c in range(2):
                put(("oT", b - 1, c), 4 + c)
        for c in range(2):
            put(("o", b, c), 6 + c)
        if b:
            put(("wo", b - 1), 4)
    for c in range(2):
        put(("oT", GB - 1, c), 4 + c)
    put(("wo", GB - 1), 4)

    for kc in range(KD):
        put(("fT", kc), kc)
    put(("gate",), 6)

    def hidden(key, pair):
        put((key, 1), 2 * pair)
        put((key, 3), 2 * pair + 1)

    hidden("s0", 1)
    hidden("s1", 0)
    for kc in range(KD):
        put(("xT", kc), 6 + kc)
    for p in range(2):
        put(("y", "s", p), 4 + p)
    for i in range(2 * QUADS):
        for half in range(2):
            put(("qk", i, half), (2 * i + half) % 8)
    values(0)
    values(1)
    put(("rank",), 6)
    put(("cT",), 7)
    for p in range(2):
        put(("y", "b", p), 4 + p)

    def per_bank(belongs):
        return [sum(bank == i and belongs(key) for key, (bank, _) in turns.items()) for i in range(8)]

    count = per_bank(lambda key: key[0] in ("xT", "qk") or key[0] == "v" and key[1] < 2), per_bank(lambda key: key in LATE_KEYS)
    return turns, uses, *count


def early_fusion_program(nc, a, out, zscr, hrows, xrows, yrows):
    TURN, USES, AHEAD, LATE = pe_bank_schedule()
    ctx = ExitStack()
    with ctx:
        def sb(name, shape, dt=F32):
            return ctx.enter_context(nc.sbuf_tensor(name, shape, dt))

        def sem(name):
            return ctx.enter_context(nc.semaphore(name))

        signals = []

        def signal(name, per_pass, start=1):
            signals.append(Signal(nc, ctx, name, per_pass, start))
            return signals[-1]

        wqk = sb("wqk", [128, KD, 2, 2, HEADS * HALF])
        wv = sb("wv", [128, KD, HEADS * DH])
        wout = sb("wout", [128, OC, D])
        w13 = sb("w13", [128, E, KD, 2 * INTER])
        we2 = sb("we2", [128, E, D])
        ws1 = sb("ws1", [128, KD, SHC * INTER])
        ws3 = sb("ws3", [128, KD, SHC * INTER])
        ws2 = sb("ws2", [128, SHC, D])
        gwT = sb("gwT", [128, KD, E])
        be2s = sb("be2s", [E + 1, D])
        bs1T = sb("bs1T", [128, SHC])
        bs3T = sb("bs3T", [128, SHC])
        lngT = sb("lngT", [128, KD])
        lnbT = sb("lnbT", [128, KD])
        gateb = sb("gateb", [128, E])
        cosT = sb("cosT", [128, N])
        sinT = sb("sinT", [128, N])
        ident = sb("ident", [128, 128])
        tri = sb("tri", [128, E, E])
        pos = sb("pos", [NP + 1, D])
        counts = sb("counts", [128, COUNTS])
        before = sb("before", [N, N])
        ones = sb("ones", [128, 128])
        minus_half = sb("minus_half", [128, 2 * SIDE])
        g1T = sb("g1T", [128, PCH])
        b1T = sb("b1T", [128, PCH])

        qk_space = sb("qk_space", [128, 2 * (HEADS // 2) * GT])
        vp_space = sb("vp_space", [128, GB * HEADS * DH + 2 * HEADS * N])
        rope_space = sb("rope_space", [128, (ROPES * 4 + 2 * 2) * GT])
        o_space = sb("o_space", [128, HEADS * DH])
        h = sb("h", [128, GB, D])
        h2 = sb("h2", [128, GB, D])
        xn = sb("xn", [128, GB, D])
        xT = sb("xT", [128, KD, GT])
        probT_space = sb("probT_space", [128, 4 * 4 * N])
        oT_space = sb("oT_space", [128, OC * N])
        smax = sb("smax", [128, 2, 4, 4])
        ssum = sb("ssum", [128, 2, 4, 4])
        srec = sb("srec", [128, 2, 4, 4])
        gate = sb("gate", [128, 8, GB, E])
        few = sb("few", [128, 8, GB, G4])
        chosen = sb("chosen", [128, GB, E])
        next_row = sb("next_row", [128, E])
        number = sb("number", [128, GB + 1])
        row_f = sb("row_f", [128, TOPK, GB])
        row_of = sb("row_of", [128, TOPK, GB], U32)
        windows = sb("windows", [1, TILES // UNROLL + 1], I32)
        tile_row = sb("tile_row", [1, TILES], I32)
        pad_row = sb("pad_row", [1, E], I32)
        ln_stats = sb("ln_stats", [128, 2, GB, 6])
        ln_mv = sb("ln_mv", [128, 2, GB, 2])
        ln_small = sb("ln_small", [128, 2, 8, GB])
        wait_carrier = sb("wait_carrier", [1, 1])

        def view(space, at, p, shape):
            size = 1
            for s in shape:
                size *= s
            flat = space[0:p, at:at + size]
            names = " ".join(f"d{i}" for i in range(len(shape)))
            return flat.rearrange(f"p ({names}) -> p {names}", **{f"d{i}": s for i, s in enumerate(shape)})

        qkr = view(qk_space, 0, 128, [2, HEADS // 2, GT])
        vv = view(vp_space, 0, 128, [GB, HEADS * DH])
        prob = view(vp_space, GB * HEADS * DH, 128, [2, 4, 4, N])
        rotated = view(rope_space, 0, 128, [ROPES, 2, 2, GT])
        product = view(rope_space, ROPES * 4 * GT, 128, [2, 2, GT])
        o = o_space
        probT = view(probT_space, 0, 128, [4, 4 * N])
        oT = view(oT_space, 0, 128, [OC, N])
        sil = view(rope_space, 0, 128, [2, GT])
        fT = view(rope_space, 4 * GT, 128, [KD, GT])
        cT = probT[0:E + 1, 0, :]
        shid = view(o_space, 0, 128, [SHC, GT])
        rows = view(vp_space, GB * HEADS * DH + HEADS * N, 128, [GB, ROW])
        cw = rows[:, :, D:IDS]
        pairs = view(vp_space, GB * HEADS * DH, 128, [2, GB, G4, G4])
        at = 0
        def place(space, p, shape):
            nonlocal at
            size = 1
            for n in shape:
                size *= n
            at += size
            return view(space, at - size, p, shape)
        b13 = place(qk_space, 128, [E, 2 * INTER])
        e_hb = place(qk_space, 128, [2, 2 * INTER])
        e_hid = place(qk_space, 128, [2, INTER])
        e_hidT = place(qk_space, 128, [2, TS])
        e_xT = place(qk_space, 128, [2, KD, TS])
        e_y = place(qk_space, 128, [UNROLL, D])
        at = 0
        e_rows = place(vp_space, 128, [UNROLL, ROW])
        pad_rows = place(vp_space, 128, [ROW])
        e_wid = place(vp_space, 128, [UNROLL, 2])
        t_small = place(vp_space, 1, [8, TILES + 2 * UNROLL])
        t_e = place(vp_space, 1, [4, E])
        assert at <= GB * HEADS * DH
        t_cmp = view(rope_space, 0, 1, [TILES * E])
        e_trash = sb("e_trash", [128, UNROLL])
        e_id = sb("e_id", [128, UNROLL], U32)
        f_h = place(vp_space, 128, [PLACES, GB, D])
        f_y = [view(space, i * GB * TOPK * D, 128, [GB, TOPK, D]) for space in (qk_space, rope_space) for i in range(2)]
        IMGF = C * PATCH * IMG
        img = [view(s, 0, PR, [C, PATCH, SIDE, PATCH]) for s in (qk_space, vp_space)]
        PF = C * PATCH * PATCH
        wp = view(vp_space, IMGF, 128, [PCH, D])
        patch = view(vp_space, IMGF + PCH * D, PR, [2, PF])
        z = [view(qk_space, IMGF, PR, [SIDE, D]), view(probT_space, 0, PR, [SIDE, D])]
        patchT = view(qk_space, IMGF + SIDE * D, 128, [2, PCH, PR])
        bproj, g2, b2 = (view(oT_space, i * D, PR, [D]) for i in range(3))
        at = 0
        tok_stats = place(o_space, PR, [4, SIDE, C * 6])
        tok_mv = place(o_space, PR, [4, SIDE, 2])
        tok_small = place(o_space, PR, [4, 2, SIDE])

        ps = ctx.enter_context(nc.psum_tensor("ps", [128, 8, 512], F32))

        img_in = [sem("img0_in"), sem("img1_in")]
        wp_in = sem("wp_in")
        ident_in = sem("ident_in")
        tok_in = sem("tok_in")
        tables_in = sem("tables_in")
        wqk_in = sem("wqk_in")
        wv_in = sem("wv_in")
        wout_in = sem("wout_in")
        shared_in = sem("shared_in")
        experts_in = sem("experts_in")
        consts = sem("consts")
        z_out = [sem("z0_out"), sem("z1_out")]
        p_stats, p_mv, p_ve, p_rstd = sem("p_stats"), sem("p_mv"), sem("p_ve"), sem("p_rstd")
        p_norm, p_turned, p_affine, p_proj = sem("p_norm"), sem("p_turned"), sem("p_affine"), sem("p_proj")
        z_bias, z_stats, z_mv, z_ve = sem("z_bias"), sem("z_stats"), sem("z_mv"), sem("z_ve")
        z_rstd, z_norm, z_scaled, z_done = sem("z_rstd"), sem("z_norm"), sem("z_scaled"), sem("z_done")
        h_in = sem("h_in")
        h_stored = sem("h_stored")
        full = [signal(f"bank{i}_full", USES[i], AHEAD[i]) for i in range(8)]
        taken = [signal(f"bank{i}_taken", USES[i], AHEAD[i]) for i in range(8)]
        h_ready = signal("h_ready", 1, 1)
        ln = {}
        for k in "af":
            parts = 1 if k == "a" else 2
            ln[k] = {n: signal(f"{k}_{n}", c, c if k == "a" else 1)
                     for n, c in (("stats", GB), ("mv", GB), ("ve", parts), ("rstd", parts), ("norm", GB))}
        a_v1, a_v2, a_v3, a_r2, a_r12 = (signal(n, 1, 1) for n in ("a_v1", "a_v2", "a_v3", "a_r2", "a_r12"))
        ahead = [h_ready, a_v1, a_v2, a_v3, a_r2, a_r12, *ln["a"].values()]
        restacked = []
        for n in range(ROPES):
            moves = 8 * 16 * len(range(n, QUADS, ROPES))
            restacked.append(signal(f"restacked{n}", moves, moves))
        rope_mul = signal("rope_mul", 2 * 2 * QUADS, 2 * 2 * QUADS)
        rope_sum = signal("rope_sum", 2 * 2 * QUADS, 2 * 2 * QUADS)
        ahead += [rope_mul, rope_sum, *full, *taken, *restacked]
        s_max = signal("s_max", 4 * GB)
        s_exp = signal("s_exp", 4 * GB)
        s_sum = signal("s_sum", GB)
        s_rec = signal("s_rec", GB)
        acc_half = signal("acc_half", 2 * 2)
        gate_step = signal("gate_step", GATE_STEPS)
        gate_exp = signal("gate_exp", 1)
        scattered = signal("scattered", 16 * TOPK * GB, 0)
        lists_done = signal("lists_done", 1)
        biases_in = sem("biases_in")
        tables_step = sem("tables_step")
        pads_out = sem("pads_out")
        e_rows_in, e_stored = ([sem(f"{n}{k}") for k in range(UNROLL)] for n in ("e_rows_in", "e_stored"))
        e_turned, e_xT_done = sem("e_turned"), sem("e_xT_done")
        e_wid_done, e_h_done, e_biased, e_silu = sem("e_wid_done"), sem("e_h_done"), sem("e_biased"), sem("e_silu")
        e_hid_done, e_hid_turned, e_hidT_done = sem("e_hid_done"), sem("e_hid_turned"), sem("e_hidT_done")
        e_trash_done = sem("e_trash_done")
        e_y_full, e_y_done, e_id_done = sem("e_y_full"), sem("e_y_done"), sem("e_id_done")
        carrier = sem("carrier")
        f_half, f_sum = sem("f_half"), sem("f_sum")
        f_in, out_stored = ([sem(f"{n}{k}") for k in range(PLACES)] for n in ("f_in", "out_stored"))

        def bank_value(s, g, key, n):
            bank, turn = TURN[key]
            value = s[bank].at(g, turn + n)
            if isinstance(g, int) and g == -1:
                value += LATE[bank]
            if isinstance(g, int) and g == GROUPS - 1 and key in LATE_KEYS:
                value -= AHEAD[bank]
            return value

        def await_full(eng, g, key):
            bank = TURN[key][0]
            eng.wait_ge(full[bank].sem, bank_value(full, g, key, 1))
            return bank

        def await_taken(eng, g, key):
            bank = TURN[key][0]
            eng.wait_ge(taken[bank].sem, bank_value(taken, g, key, 1))

        def claim(g, key):
            bank = TURN[key][0]
            value = bank_value(taken, g, key, 0)
            if not (isinstance(value, int) and value == 0):
                nc.tensor.wait_ge(taken[bank].sem, value)
            return bank

        def images(g):
            return bass.ds(g * GB, GB) if not isinstance(g, int) else slice(g * GB, (g + 1) * GB)

        def passes(eng, body):
            with eng.Fori(0, GROUPS - 1) as g:
                body(g, True)
            body(GROUPS - 1, False)

        def tiles(eng, step, lag):
            for t in range(2 * UNROLL):
                step(lambda n, t=t: t - n, lambda n, t=t: (t - n) // UNROLL + 1, t % UNROLL)
            with eng.Fori(0, TILES // UNROLL - 2) as i:
                for k in range(UNROLL):
                    step(lambda n, k=k: i * UNROLL + (2 * UNROLL + k - n), lambda n, k=k: i + ((2 * UNROLL + k - n) // UNROLL + 1), k)
            for t in range(TILES, TILES + lag):
                step(lambda n, t=t: t - n, lambda n, t=t: (t - n) // UNROLL + 1, t % UNROLL)

        def pad_lists(eng, half):
            eng.wait_ge(tables_step, PAD_STEPS)
            with eng.Fori(0, E // 2) as e:
                row = eng.value_load(pad_row[0:1, bass.ds(e + half * (E // 2), 1)], min_val=0, max_val=E * CAP - TS)
                eng.dma_start(xrows[bass.ds(row, TS), :], pad_rows).then_inc(pads_out, 16)

        def experts_around(eng, at):
            t = at(0)
            window = windows[0:1, t // UNROLL:t // UNROLL + 1] if isinstance(t, int) else windows[0:1, bass.ds(t // UNROLL, 1)]
            return eng.value_load(window, min_val=0, max_val=E ** WINDOW - 1)

        def expert_at(eng, window, k, n):
            return eng.snap((window >> (4 * (k - n + BEHIND))) & (E - 1), min_val=0, max_val=E - 1)

        def live(t):
            return not isinstance(t, int) or 0 <= t < TILES

        def passed(eng, s, t):
            if not isinstance(t, int) or t >= 0:
                eng.wait_ge(s, t + 1)

        def moved_tile(eng, s, k, turn):
            if not isinstance(turn, int) or turn > 0:
                eng.wait_ge(s[k % UNROLL], turn * 16)

        block = ctx.enter_context(nc.Block())

        def load_images(eng, half):
            for i in range(HB):
                eng.dma_start(img[half][i * SIDE:(i + 1) * SIDE, :, :, :, :].rearrange("h c p w q -> h c (p w q)"),
                              a["x"][half * HB + i].rearrange("c (h p) w -> h c (p w)", p=PATCH)).then_inc(img_in[half], 16)

        @block.sync
        def _(sp):
            load_images(sp, 0)
            load_images(sp, 1)
            for kc in range(KD):
                for which in range(2):
                    for half in range(2):
                        sp.dma_start(
                            wqk[:, kc, which, half, :].rearrange("k (h i) -> k h i", i=HALF),
                            a["L0_attn_w_qkv"][kc * 128:(kc + 1) * 128, which * HEADS * DH:(which + 1) * HEADS * DH]
                            .rearrange("k (h f i) -> k f h i", f=2, i=HALF)[:, half, :, :]).then_inc(wqk_in, 16)
            sp.dma_start(cosT[:, :], a["cosT"]).then_inc(tables_in, 16)
            sp.dma_start(sinT[:, :], a["sinT"]).then_inc(tables_in, 16)
            sp.dma_start(tri[:, :, :].rearrange("p a b -> p (a b)"), a["tri"].partition_broadcast(128)).then_inc(tables_in, 16)
            sp.dma_start(pos[0:NP, :], a["L0_tok_pos_emb"][0, 1:NP + 1, :]).then_inc(tables_in, 16)
            sp.dma_start(pos[NP:NP + 1, :], a["L0_tok_pos_emb"][0, 0:1, :]).then_inc(tables_in, 16)
            sp.dma_start(gateb[:, :], a["L0_ffn_gate_b"].partition_broadcast(128)).then_inc(tables_in, 16)
            for t, name in ((lngT, "L0_attn_ln_gamma"), (lnbT, "L0_attn_ln_beta"), (bs1T, "L0_ffn_bs1"), (bs3T, "L0_ffn_bs3")):
                sp.dma_start(t[:, :], a[name].rearrange("(c k) -> k c", k=128), allow_slow_non_contiguous=True).then_inc(tables_in, 16)
            sp.dma_start(counts[:, :], a["counts"].partition_broadcast(128)).then_inc(tables_in, 16)
            sp.dma_start(next_row[:, :], a["counts"][COUNT_BASE:COUNT_BASE + E].partition_broadcast(128)).then_inc(tables_in, 16)
            sp.dma_start(before[:, :], a["before"]).then_inc(tables_in, 16)
            sp.dma_start(number[:, :], a["number"]).then_inc(tables_in, 16)
            for c in range(KD):
                sp.dma_start(gwT[:, c, :], a["L0_ffn_gate_w"][:, c * 128:(c + 1) * 128].rearrange("e k -> k e"),
                              allow_slow_non_contiguous=True).then_inc(tables_in, 16)
            sp.dma_start(be2s[0:E, :], a["L0_ffn_be2"]).then_inc(tables_in, 16)
            sp.dma_start(be2s[E:E + 1, :], a["L0_ffn_bs2"].unsqueeze(0)).then_inc(tables_in, 16)
            sp.dma_start(wv[:, :, :], a["L0_attn_w_qkv"][:, 2 * HEADS * DH:].rearrange("(c k) n -> k c n", c=KD)).then_inc(wv_in, 16)
            sp.dma_start(wout[:, :, :], a["L0_attn_w_out"].rearrange("(c k) n -> k c n", c=OC)).then_inc(wout_in, 16)
            for w, name in ((ws1, "L0_ffn_ws1"), (ws3, "L0_ffn_ws3"), (ws2, "L0_ffn_ws2")):
                sp.dma_start(w[:, :, :], a[name].rearrange("(c k) n -> k c n", k=128)).then_inc(shared_in, 16)
            for half, name in enumerate(("L0_ffn_We1", "L0_ffn_We3")):
                for c in range(KD):
                    sp.dma_start(w13[:, :, c, half * INTER:(half + 1) * INTER],
                                 a[name][:, c * 128:(c + 1) * 128, :].rearrange("e k n -> k e n")).then_inc(experts_in, 16)
            sp.dma_start(we2[:, :, :], a["L0_ffn_We2"].rearrange("e k n -> k e n")).then_inc(experts_in, 16)

            def store_image_tokens(half):
                sp.dma_start(zscr[half * HB:(half + 1) * HB, :, :].rearrange("b (h w) d -> (b h) w d", w=SIDE), z[half]).then_inc(z_out[half], 16)

            sp.wait_ge(z_done, 1)
            store_image_tokens(0)
            sp.wait_ge(z_out[0], 16)

            def load_tokens(g, src):
                sp.dma_start(h[0:NP, :, :], zscr[src, :, :].rearrange("b n d -> n b d")).then_inc(h_in, 16)
                sp.dma_start(h[NP:NP + 1, :, :], a["L0_tok_cls_token"][0, :, :].unsqueeze(1).to_broadcast([1, GB, D])).then_inc(h_in, 16)
                sp.dma_start(h[NP + 1:N, :, :], a["txt"][src, :, :].rearrange("b n d -> n b d")).then_inc(h_in, 16)

            def restack(g):
                for j in range(QUADS):
                    for half in range(2):
                        sp.wait_ge(rope_sum.sem, rope_sum.at(g, 2 * (2 * j + 1) + half + 1))
                        for r in range(4):
                            to = (r % 2) * DH + half * HALF
                            restacked[j % ROPES].by(sp.dma_start(qkr[to:to + HALF, :, 2 * j + r // 2, :],
                                                                 rotated[HALF * r:HALF * (r + 1), j % ROPES, :, half, :]), 16)

            load_tokens(-1, slice(0, GB))
            restack(-1)
            sp.wait_ge(z_done, 2)
            store_image_tokens(1)
            sp.wait_ge(z_out[1], 16)

            def body(g, prepare):
                if prepare:
                    await_taken(sp, g, ("wo", GB - 1))
                    load_tokens(g, bass.ds((g + 1) * GB, GB))
                    restack(g)

            passes(sp, body)
            pad_lists(sp, 0)
            sp.wait_ge(pads_out, 16 * E)
            sp.wait_ge(tables_step, TABLE_STEPS)
            sp.wait_ge(scattered.sem, scattered.at(GROUPS - 1, scattered.per_pass))

            def step(at, turn, k):
                t = at(0)
                if live(t):
                    row = sp.value_load(tile_row[0:1, t:t + 1] if isinstance(t, int) else tile_row[0:1, bass.ds(t, 1)],
                                        min_val=0, max_val=E * CAP - TS)
                    passed(sp, e_turned, at(UNROLL))
                    passed(sp, e_wid_done, at(UNROLL))
                    sp.dma_start(e_rows[:, k, :], xrows[bass.ds(row, TS), :]).then_inc(e_rows_in[k], 16)

            tiles(sp, step, 0)
            def load_sums(t):
                sp.dma_start(f_h[0:N, t % PLACES, :, :], hrows[t, :, :, :]).then_inc(f_in[t % PLACES], 16)

            def load_results(t):
                sp.dma_start(f_y[t % PLACES][0:N, :, :, :].rearrange("n b c d -> n b (c d)"),
                             yrows[t * TOPK * GT:(t + 1) * TOPK * GT, :].rearrange("(b n c) d -> n b (c d)", b=GB, c=TOPK)).then_inc(f_in[t % PLACES], 16)

            sp.wait_ge(h_stored, 16 + 16 * GROUPS)
            for t in range(PLACES):
                load_sums(t)
            for k in range(UNROLL):
                moved_tile(sp, e_stored, k, TILES // UNROLL)
            for t in range(PLACES):
                load_results(t)
            for t in range(PLACES, GROUPS):
                sp.wait_ge(out_stored[t % PLACES], 48)
                load_sums(t)
                load_results(t)
            for k in range(PLACES):
                sp.wait_ge(out_stored[k], 48 * GROUPS // PLACES)

        @block.gpsimd
        def _(pool):
            for s in signals:
                if s not in ahead and s.start:
                    pool.sem_inc(s.sem, 1)
            pool.sem_inc(h_stored, 16)
            nc.gpsimd.memset(minus_half[:, :], -0.5).then_inc(consts, 1)
            nc.gpsimd.memset(ones[:, :], 1.0).then_inc(consts, 1)
            pool.wait_ge(consts, 2)
            def tokenizer_power(ve_sem, rstd_sem, half, k):
                pool.wait_ge(ve_sem, half + 1)
                q = 2 * half + k
                nc.gpsimd.tensor_tensor(tok_small[:, q, 1, :], tok_small[:, q, 0, :], minus_half[0:PR, 0:SIDE],
                                        ALU.pow).then_inc(rstd_sem, 1)

            tokenizer_power(p_ve, p_rstd, 0, 0)
            tokenizer_power(p_ve, p_rstd, 1, 0)
            tokenizer_power(z_ve, z_rstd, 0, 1)

            def power(g, k, src, dst, wait, done, images=(0, GB), part=0):
                pool.wait_ge(wait.sem, wait.at(g, part + 1))
                lo, hi = images
                done.by(nc.gpsimd.tensor_tensor(ln_small[0:N, k, dst, lo:hi], ln_small[0:N, k, src, lo:hi],
                                                minus_half[0:N, lo:hi], ALU.pow))

            def prepare_next(g):
                power(g, 0, 0, 1, ln["a"]["ve"], ln["a"]["rstd"])
                power(g, 0, 4, 5, a_v3, a_r2)

            def rotate(g, tiles_of_heads):
                for i in tiles_of_heads:
                    j, which = divmod(i, 2)
                    t, other = rotated[:, j % ROPES, which, :, :], product[:, i % 2, :, :]
                    pool.wait_ge(rope_mul.sem, rope_mul.at(g, 2 * i + 2))
                    rope_sum.by(nc.gpsimd.tensor_tensor(t[:, 0, :], t[:, 0, :], other[:, 0, :], ALU.subtract))
                    for half in range(2):
                        await_taken(pool, g, ("qk", i, half))
                    rope_sum.by(nc.gpsimd.tensor_tensor(t[:, 1, :], other[:, 1, :], t[:, 1, :], ALU.add))

            def body(g, prepare):
                for part in range(2):
                    power(g, 1, 0, 1, ln["f"]["ve"], ln["f"]["rstd"], (2 * part, 2 * part + 2), part)
                if prepare:
                    prepare_next(g)
                    rotate(g, range(2 * QUADS))
                pool.wait_ge(gate_step.sem, gate_step.at(g, gate_step.per_pass))
                pool.sem_inc(carrier, 1)
                for c in range(TOPK):
                    for b in range(GB):
                        scattered.by(pool.indirect_dma_start(xrows, bass.IndirectOffsetOnAxis(row_of[0:N, c, b:b + 1], 0),
                                                             rows[0:N, b, :], None), 16)
                pool.wait_ge(scattered.sem, scattered.at(g, scattered.per_pass))
                lists_done.given += 1
                pool.sem_inc(lists_done.sem, 1)

            prepare_next(-1)
            rotate(-1, range(2))
            tokenizer_power(z_ve, z_rstd, 1, 1)
            rotate(-1, range(2, 2 * QUADS))
            passes(pool, body)

            def step(at, turn, k):
                t = at(3)
                if live(t):
                    passed(pool, e_y_done, t)
                    passed(pool, e_id_done, t)
                    pool.sem_inc(carrier, 1)
                    j = (k - 3) % UNROLL
                    pool.indirect_dma_start(yrows, bass.IndirectOffsetOnAxis(e_id[:, j:j + 1], 0), e_y[:, j, :], None).then_inc(e_stored[j], 16)

            tiles(pool, step, 3)

        @block.scalar
        def _(act):
            act.dma_start(ident[:, :], a["ident"]).then_inc(ident_in, 16)
            act.dma_start(wp[:, :, :].rearrange("p (c k) e -> p c k e", c=C)[:, :, 0, :],
                          a["L0_tok_W_proj"].rearrange("(k q c) e -> q k c e", k=2, c=C)[:, 0, :, :]).then_inc(wp_in, 16)
            act.dma_start(wp[:, :, :].rearrange("p (c k) e -> p c k e", c=C)[:, :, 1, :],
                          a["L0_tok_W_proj"].rearrange("(k q c) e -> q k c e", k=2, c=C)[:, 1, :, :]).then_inc(wp_in, 16)
            for t, name in ((g1T, "L0_tok_ln1_g"), (b1T, "L0_tok_ln1_b")):
                for c in range(C):
                    act.dma_start(t[:, 2 * c:2 * c + 2], a[name].rearrange("(k q c) -> q c k", k=2, c=C)[:, c, :],
                                  allow_slow_non_contiguous=True).then_inc(tok_in, 16)
            for t, name in ((bproj, "L0_tok_b_proj"), (g2, "L0_tok_ln2_g"), (b2, "L0_tok_ln2_b")):
                act.dma_start(t, a[name].partition_broadcast(PR)).then_inc(tok_in, 16)
            act.wait_ge(tok_in, 16 * 9)
            for t in range(2 * SIDE):
                act.wait_ge(p_turned, t + 1)
                if t >= 2:
                    act.wait_ge(p_proj, t - 1)
                for m in range(PCH):
                    last = nc.scalar.activation(patchT[:, t % 2, m, :], ps[:, 2 * (t % 2) + m // 3, (m % 3) * PR:(m % 3 + 1) * PR],
                                                ACT.Identity, scale=g1T[:, m:m + 1], bias=b1T[:, m:m + 1])
                    last.then_inc(p_affine, 1)
            act.wait_ge(tables_in, 16 * TABLES)

            def prepare_next(g):
                for kc in range(KD):
                    bank = await_full(act, g, ("xT", kc))
                    taken[bank].by(nc.scalar.activation(xT[:, kc, :], ps[:, bank, 0:GT], ACT.Identity,
                                                        scale=lngT[:, kc:kc + 1], bias=lnbT[:, kc:kc + 1]))
                take_v(g, (0, 1))

            def take_v(g, images):
                for b in images:
                    for n in range(2):
                        bank = await_full(act, g, ("v", b, n))
                        taken[bank].by(nc.scalar.copy(vv[0:N, b, n * 512:(n + 1) * 512], ps[0:N, bank, :]))

            def body(g, prepare):
                take_v(g, (2, 3))
                def softmax_exp(b):
                    for r in range(4):
                        await_taken(act, g, ("s", b, r))
                        p = prob[0:N, b % 2, r, :, :]
                        s_exp.by(nc.scalar.activation(p, p, ACT.Exp, scale=SCALE))

                def take_oT(b):
                    for c in range(2):
                        bank = await_full(act, g, ("oT", b, c))
                        taken[bank].by(nc.scalar.copy(oT[:, 4 * c:4 * c + 4, :], ps[:, bank, 0:4 * N].rearrange("p (m t) -> p m t", m=4)))

                softmax_exp(0)
                for b in range(GB):
                    if b:
                        await_full(act, g, ("o", b - 1, 1))
                    for r in range(4):
                        bank = await_full(act, g, ("pT", b, r))
                        taken[bank].by(nc.scalar.copy(probT[0:N, r, :], ps[0:N, bank, 0:4 * N]))
                    if b:
                        take_oT(b - 1)
                    if b + 1 < GB:
                        softmax_exp(b + 1)
                take_oT(GB - 1)
                if not prepare:
                    for half, name in enumerate(("L0_ffn_be1", "L0_ffn_be3")):
                        act.dma_start(b13[:, :, half * INTER:(half + 1) * INTER], a[name].partition_broadcast(128)).then_inc(biases_in, 16)

                for kc in range(KD):
                    bank = await_full(act, g, ("fT", kc))
                    taken[bank].by(nc.scalar.copy(fT[:, kc, :], ps[:, bank, 0:GT]))

                def silu(q):
                    key = f"s{q}"
                    bias = bs1T[:, q:q + 1]
                    bank = await_full(act, g, (key, 1))
                    taken[bank].by(nc.scalar.activation(sil[:, q % 2, :], ps[:, bank, 0:GT], ACT.Silu, bias=bias))

                await_taken(act, g, ("gate",))
                gate_exp.by(nc.scalar.activation(gate[0:N, 1, :, :], gate[0:N, 0, :, :], ACT.Exp))
                for q in range(SHC):
                    silu(q)
                if prepare:
                    prepare_next(g)
                bank = await_full(act, g, ("cT",))
                taken[bank].by(nc.scalar.copy(cT, ps[0:E + 1, bank, 0:GT]))
                act.wait_ge(acc_half.sem, acc_half.at(g, 2 * 2))
                for p in range(2):
                    await_taken(act, g, ("y", "b", p))
                act.dma_start((hrows[bass.ds(g, 1), :, :, :] if prepare else hrows[g:g + 1, :, :, :]).rearrange("o n b d -> n (o b) d"),
                              h2[0:N, :, :]).then_inc(h_stored, 16)

            prepare_next(-1)
            act.wait_ge(z_out[1], 16)
            passes(act, body)

            pad_lists(act, 1)

            def step(at, turn, k):
                t = at(0)
                if live(t):
                    passed(act, e_turned, t)
                    passed(act, e_h_done, at(2))
                    nc.scalar.copy(e_xT[:, k % 2, :, :].rearrange("p c t -> p (c t)"), ps[:, k % 2, 0:KD * TS]).then_inc(e_xT_done, 1)
                t = at(1)
                if live(t):
                    j = (k - 1) % 2
                    passed(act, e_biased, t)
                    x = e_hb[:, j, 0:INTER]
                    nc.scalar.activation(x, x, ACT.Silu).then_inc(e_silu, 1)
                t = at(2)
                if live(t):
                    passed(act, e_hid_turned, t)
                    passed(act, e_y_full, at(4))
                    nc.scalar.copy(e_hidT[:, k % 2, :], ps[:, 4 + k % 2, 0:TS]).then_inc(e_hidT_done, 1)

            tiles(act, step, 2)

            for t in range(GROUPS):
                act.wait_ge(f_sum, t + 1)
                for lo, hi, t0 in ((0, NP, 1), (NP, NP + 1, 0), (NP + 1, N, NP + 1)):
                    act.dma_start(out[images(t), t0:t0 + hi - lo, :].rearrange("b n d -> n b d"),
                                  f_h[lo:hi, t % PLACES, :, :]).then_inc(out_stored[t % PLACES], 16)

        @block.vector
        def _(dve):
            def patch_stats(half, columns):
                dve.wait_ge(img_in[half], 16 * HB)
                for w in columns:
                    for c in range(C):
                        nc.vector.bn_stats(tok_stats[:, 2 * half, w, 6 * c:6 * c + 6], img[half][:, c, :, w, :]).then_inc(p_stats, 1)

            def patch_variance(half):
                dve.wait_ge(p_stats, C * SIDE * (half + 1))
                for w in range(SIDE):
                    nc.vector.bn_aggr(tok_mv[:, 2 * half, w, :], tok_stats[:, 2 * half, w, :]).then_inc(p_mv, 1)
                dve.wait_ge(p_mv, SIDE * (half + 1))
                nc.vector.tensor_scalar(tok_small[:, 2 * half, 0, :], tok_mv[:, 2 * half, :, 1], EPS, None, ALU.add).then_inc(p_ve, 1)

            def patch_norm(t):
                half, w = divmod(t, SIDE)
                if t >= 2:
                    dve.wait_ge(p_turned, t - 1)
                nc.vector.tensor_scalar(patch[:, t % 2, :].rearrange("p (c a q) -> p c a q", c=C, a=PATCH), img[half][:, :, :, w, :],
                                        tok_mv[:, 2 * half, w, 0:1], tok_small[:, 2 * half, 1, w:w + 1],
                                        ALU.subtract, ALU.mult).then_inc(p_norm, 1)

            def token_stats(t):
                half, w = divmod(t, SIDE)
                dve.wait_ge(p_proj, t + 1)
                nc.vector.tensor_tensor(z[half][:, w, :], ps[0:PR, 4 + t % 2, 0:D], bproj, ALU.add).then_inc(z_bias, 1)
                dve.wait_ge(z_bias, t + 1)
                nc.vector.bn_stats(tok_stats[:, 2 * half + 1, w, 0:6], z[half][:, w, :]).then_inc(z_stats, 1)

            def token_variance(half):
                q = 2 * half + 1
                dve.wait_ge(z_stats, SIDE * (half + 1))
                for w in range(SIDE):
                    nc.vector.bn_aggr(tok_mv[:, q, w, :], tok_stats[:, q, w, 0:6]).then_inc(z_mv, 1)
                dve.wait_ge(z_mv, SIDE * (half + 1))
                nc.vector.tensor_scalar(tok_small[:, q, 0, :], tok_mv[:, q, :, 1], EPS, None, ALU.add).then_inc(z_ve, 1)

            def token_norm(half):
                q = 2 * half + 1
                dve.wait_ge(z_rstd, half + 1)
                for w in range(SIDE):
                    zz = z[half][:, w, :]
                    nc.vector.tensor_scalar(zz, zz, tok_mv[:, q, w, 0:1], tok_small[:, q, 1, w:w + 1], ALU.subtract, ALU.mult).then_inc(z_norm, 1)

            def token_gain(half):
                dve.wait_ge(z_norm, SIDE * (half + 1))
                zz = z[half][:, :, :]
                nc.vector.tensor_tensor(zz, zz, g2.unsqueeze(1).to_broadcast([PR, SIDE, D]), ALU.mult).then_inc(z_scaled, 1)

            def token_bias(half):
                dve.wait_ge(z_scaled, half + 1)
                zz = z[half][:, :, :]
                nc.vector.tensor_tensor(zz, zz, b2.unsqueeze(1).to_broadcast([PR, SIDE, D]), ALU.add).then_inc(z_done, 1)

            dve.wait_ge(tok_in, 16 * 9)
            patch_stats(0, range(SIDE))
            patch_variance(0)
            beside = {1: lambda: patch_stats(1, range(0, 2)), 2: lambda: patch_stats(1, range(2, 4)),
                      3: lambda: patch_stats(1, range(4, 5)), 4: lambda: (patch_stats(1, range(5, 6)), patch_variance(1)),
                      6: lambda: token_variance(0), 7: lambda: token_norm(0), 8: lambda: token_gain(0), 9: lambda: token_bias(0)}
            dve.wait_ge(p_rstd, 1)
            patch_norm(0)
            for t in range(2 * SIDE):
                if t + 1 == SIDE:
                    dve.wait_ge(p_rstd, 2)
                if t + 1 < 2 * SIDE:
                    patch_norm(t + 1)
                if t:
                    token_stats(t - 1)
                if t in beside:
                    beside[t]()
            token_stats(2 * SIDE - 1)

            dve.wait_ge(tables_in, 16 * TABLES)
            dve.wait_ge(consts, 2)

            def normalise(g):
                def own(s, n):
                    dve.wait_ge(s.sem, s.at(g, n))

                s = ln["a"]
                sm = ln_small[0:N, 0, :, :]
                var = ln_mv[0:N, 0, :, 1]
                for b in range(GB):
                    s["stats"].by(nc.vector.bn_stats(ln_stats[0:N, 0, b, :], h[0:N, b, :]))
                own(s["stats"], GB)
                nc.vector.memset(wait_carrier[:, :], 0.0)
                for b in range(GB):
                    s["mv"].by(nc.vector.bn_aggr(ln_mv[0:N, 0, b, :], ln_stats[0:N, 0, b, :]))
                own(s["mv"], GB)
                s["ve"].by(nc.vector.tensor_scalar(sm[:, 0, :], var, EPS, None, ALU.add))
                dve.wait_ge(s["rstd"].sem, s["rstd"].at(g, 1))
                a_v1.by(nc.vector.tensor_tensor(sm[:, 2, :], var, sm[:, 1, :], ALU.mult))
                own(a_v1, 1)
                a_v2.by(nc.vector.tensor_tensor(sm[:, 3, :], sm[:, 2, :], sm[:, 1, :], ALU.mult))
                own(a_v2, 1)
                a_v3.by(nc.vector.tensor_scalar(sm[:, 4, :], sm[:, 3, :], EPS, None, ALU.add))
                dve.wait_ge(a_r2.sem, a_r2.at(g, 1))
                a_r12.by(nc.vector.tensor_tensor(sm[:, 6, :], sm[:, 1, :], sm[:, 5, :], ALU.mult))
                own(a_r12, 1)
                for b in range(GB):
                    s["norm"].by(nc.vector.tensor_scalar(xn[0:N, b, :], h[0:N, b, :], ln_mv[0:N, 0, b, 0:1], sm[:, 6, b:b + 1],
                                                         ALU.subtract, ALU.mult))

            def prepare_next(g):
                dve.wait_ge(h_in, g * 48 + 96)
                h_ready.by(nc.vector.tensor_tensor(h[0:NP + 1, :, :], h[0:NP + 1, :, :],
                                                   pos[:, :].unsqueeze(1).to_broadcast([NP + 1, GB, D]), ALU.add))
                dve.wait_ge(h_ready.sem, h_ready.at(g, 1))
                normalise(g)

            cos = cosT[:, :].unsqueeze(1).to_broadcast([128, GB, N])
            sin = sinT[:, :].unsqueeze(1).to_broadcast([128, GB, N])

            def by_image(ap):
                return ap.rearrange("p (b t) -> p b t", b=GB)

            def rotate(g, tiles_of_heads):
                for i in tiles_of_heads:
                    j, which = divmod(i, 2)
                    moved = restacked[j % ROPES]
                    if not (isinstance(g, int) and j < ROPES):
                        dve.wait_ge(moved.sem, moved.at(g, 8 * 16 * (j // ROPES)))
                    if not (isinstance(g, int) and i < 2):
                        dve.wait_ge(rope_sum.sem, rope_sum.at(g, 2 * (i - 2) + 2))
                    for half, (first, second) in enumerate(((cos, sin), (sin, cos))):
                        bank = await_full(dve, g, ("qk", i, half))
                        x = by_image(ps[:, bank, 0:GT])
                        t = product[:, i % 2, :, :] if half else rotated[:, j % ROPES, which, :, :]
                        rope_mul.by(nc.vector.tensor_tensor(by_image(t[:, 0, :]), x, first, ALU.mult))
                        taken[bank].by(nc.vector.tensor_tensor(by_image(t[:, 1, :]), x, second, ALU.mult))

            def body(g, prepare):
                def own(s, n):
                    dve.wait_ge(s.sem, s.at(g, n))

                def centre(b):
                    for r in range(4):
                        bank = await_full(dve, g, ("s", b, r))
                        s_max.by(nc.vector.tensor_reduce(smax[0:N, b % 2, r, :], ps[0:N, bank, 0:4 * N].rearrange("p (j t) -> p j t", j=4),
                                                         AX.X, ALU.max))
                    for r in range(4):
                        own(s_max, 4 * b + r + 1)
                        bank = TURN[("s", b, r)][0]
                        taken[bank].by(nc.vector.tensor_tensor(
                            prob[0:N, b % 2, r, :, :], ps[0:N, bank, 0:4 * N].rearrange("p (j t) -> p j t", j=4),
                            smax[0:N, b % 2, r, :].unsqueeze(2).to_broadcast([N, 4, N]), ALU.subtract))

                def token_stats(b):
                    await_taken(dve, g, ("wo", b))
                    ln["f"]["stats"].by(nc.vector.bn_stats(ln_stats[0:N, 1, b, :], h2[0:N, b, :]))

                def token_variance(part):
                    own(ln["f"]["stats"], 2 * part + 2)
                    nc.vector.memset(wait_carrier[:, :], 0.0)
                    for b in (2 * part, 2 * part + 1):
                        ln["f"]["mv"].by(nc.vector.bn_aggr(ln_mv[0:N, 1, b, :], ln_stats[0:N, 1, b, :]))
                    own(ln["f"]["mv"], 2 * part + 2)
                    both = slice(2 * part, 2 * part + 2)
                    ln["f"]["ve"].by(nc.vector.tensor_scalar(ln_small[0:N, 1, 0, both], ln_mv[0:N, 1, both, 1], EPS, None, ALU.add))

                def token_norm(part):
                    dve.wait_ge(ln["f"]["rstd"].sem, ln["f"]["rstd"].at(g, part + 1))
                    for b in (2 * part, 2 * part + 1):
                        ln["f"]["norm"].by(nc.vector.tensor_scalar(rows[0:N, b, 0:D], h2[0:N, b, :], ln_mv[0:N, 1, b, 0:1],
                                                                   ln_small[0:N, 1, 1, b:b + 1], ALU.subtract, ALU.mult))

                def add_attention(b):
                    bank = await_full(dve, g, ("wo", b))
                    taken[bank].by(nc.vector.tensor_tensor(h2[0:N, b, :], ps[0:N, bank, 0:D], h[0:N, b, :], ALU.add))

                dve.wait_ge(h_stored, g * 16 + 16)
                centre(0)
                for b in range(GB):
                    if b == 0:
                        dve.wait_ge(lists_done.sem, lists_done.at(g, 0))
                    if b + 1 < GB:
                        centre(b + 1)
                    dve.wait_ge(s_exp.sem, s_exp.at(g, 4 * b + 4))
                    s_sum.by(nc.vector.tensor_reduce(ssum[0:N, b % 2, :, :], prob[0:N, b % 2, :, :, :], AX.X, ALU.add))
                    own(s_sum, b + 1)
                    s_rec.by(nc.vector.reciprocal(srec[0:N, b % 2, :, :], ssum[0:N, b % 2, :, :]))
                    own(s_rec, b + 1)
                    for c in range(2):
                        bank = await_full(dve, g, ("o", b, c))
                        inv = srec[0:N, b % 2, :, 2 * c:2 * c + 2].rearrange("p r j -> p j r").unsqueeze(3).to_broadcast([N, 2, 4, DH])
                        taken[bank].by(nc.vector.tensor_tensor(
                            o[0:N, c * 512:(c + 1) * 512].rearrange("p (j r d) -> p j r d", j=2, r=4),
                            ps[0:N, bank, :].rearrange("p (j r d) -> p j r d", j=2, r=4), inv, ALU.mult))
                    if b:
                        add_attention(b - 1)
                        token_stats(b - 1)
                    if b == 2:
                        token_variance(0)
                nc.vector.memset(rows[:, :, ONE:ONE + 1], 1.0)
                token_norm(0)
                add_attention(GB - 1)
                token_stats(GB - 1)
                token_variance(1)
                token_norm(1)

                def gated(q):
                    key = f"s{q}"
                    bias, dst = bs3T[:, q:q + 1], shid[:, q, :]
                    await_taken(dve, g, (key, 1))
                    bank = await_full(dve, g, (key, 3))
                    taken[bank].by(nc.vector.scalar_tensor_tensor(dst, ps[:, bank, 0:GT], bias, sil[:, q % 2, :], ALU.add, ALU.mult))

                summed = []

                def add_out(e):
                    for p in range(2):
                        bank = await_full(dve, g, ("y", e, p))
                        for bb in range(2):
                            b = 2 * p + bb
                            if summed:
                                own(acc_half, 2 * (len(summed) - 1) + p + 1) if bb == 0 else await_taken(dve, g, ("y", summed[-1], p))
                            src = ps[0:N, bank, bb * D:(bb + 1) * D]
                            ins = nc.vector.tensor_tensor(h2[0:N, b, :], src, h2[0:N, b, :], ALU.add)
                            (taken[bank] if bb else acc_half).by(ins)
                    summed.append(e)

                steps = [0]

                def step(ins):
                    gate_step.by(ins)
                    steps[0] += 1
                    own(gate_step, steps[0])

                def beats(dst, tmp, x, n):
                    other = x.unsqueeze(2).to_broadcast([N, GB, n, n])
                    own_x = x.unsqueeze(3).to_broadcast([N, GB, n, n])
                    low = tri[0:N, 0:n, 0:n].unsqueeze(1).to_broadcast([N, GB, n, n])
                    step(nc.vector.tensor_tensor(dst, other, own_x, ALU.is_equal))
                    step(nc.vector.tensor_tensor(dst, dst, low, ALU.mult))
                    step(nc.vector.tensor_tensor(tmp, other, own_x, ALU.is_gt))
                    step(nc.vector.tensor_tensor(dst, dst, tmp, ALU.add))

                G = [gate[0:N, i, :, :] for i in range(8)]
                S = [few[0:N, i, :, :] for i in range(8)]
                mx, sm, rs = S[0][:, :, 0], S[0][:, :, 1], S[0][:, :, 2]
                prob_e, biased = G[2], G[3]

                def over(x, n):
                    return x.unsqueeze(2).to_broadcast([N, GB, n])

                def centre_logits():
                    bank = await_full(dve, g, ("gate",))
                    logits = ps[0:N, bank, 0:GB * E].rearrange("p (b e) -> p b e", b=GB)
                    step(nc.vector.tensor_reduce(mx, logits, AX.X, ALU.max))
                    taken[bank].by(nc.vector.tensor_tensor(G[0], logits, over(mx, E), ALU.subtract))

                def choose_groups():
                    dve.wait_ge(gate_exp.sem, gate_exp.at(g, 1))
                    step(nc.vector.tensor_reduce(sm, G[1], AX.X, ALU.add))
                    step(nc.vector.reciprocal(rs, sm))
                    step(nc.vector.tensor_tensor(prob_e, G[1], over(rs, E), ALU.mult))
                    step(nc.vector.tensor_tensor(biased, prob_e, gateb[0:N, :].unsqueeze(1).to_broadcast([N, GB, E]), ALU.add))
                    quad = biased.rearrange("p b (g h i) -> p (b g) h i", g=G4, h=2)
                    hi = G[4].rearrange("p b (x i) -> p (b x) i", i=2)[:, 0:GB * G4, :]
                    lo = G[5].rearrange("p b (x i) -> p (b x) i", i=2)[:, 0:GB * G4, :]
                    first, second = (S[i].rearrange("p b g -> p (b g)") for i in (1, 2))
                    tmp = S[3].rearrange("p b g -> p (b g)")
                    step(nc.vector.tensor_tensor(hi, quad[:, :, 0, :], quad[:, :, 1, :], ALU.max))
                    step(nc.vector.tensor_tensor(lo, quad[:, :, 0, :], quad[:, :, 1, :], ALU.min))
                    step(nc.vector.tensor_tensor(first, hi[:, :, 0], hi[:, :, 1], ALU.max))
                    step(nc.vector.tensor_tensor(second, hi[:, :, 0], hi[:, :, 1], ALU.min))
                    step(nc.vector.tensor_tensor(tmp, lo[:, :, 0], lo[:, :, 1], ALU.max))
                    step(nc.vector.tensor_tensor(second, second, tmp, ALU.max))
                    step(nc.vector.tensor_tensor(S[4], S[1], S[2], ALU.add))
                    small = [pairs[0:N, i, :, :, :] for i in range(2)]
                    beats(small[0], small[1], S[4], G4)
                    step(nc.vector.tensor_reduce(S[5], small[0], AX.X, ALU.add))
                    step(nc.vector.tensor_scalar(S[6], S[5], 2.0, None, ALU.is_lt))
                    step(nc.vector.tensor_scalar(S[7], S[6], 1.0, FAR, ALU.subtract, ALU.mult))
                    def spread(x):
                        return x.unsqueeze(3).to_broadcast([N, GB, G4, EPG])

                    def grouped(x):
                        return x.rearrange("p b (g i) -> p b g i", g=G4)

                    step(nc.vector.tensor_tensor(grouped(G[4]), grouped(biased), spread(S[6]), ALU.mult))
                    step(nc.vector.tensor_tensor(grouped(G[4]), grouped(G[4]), spread(S[7]), ALU.add))

                def choose_experts():
                    first_of = counts[0:N, COUNT_DOWN:COUNT_DOWN + E].unsqueeze(1).to_broadcast([N, GB, E])
                    for n in range(TOPK):
                        step(nc.vector.tensor_reduce(mx, G[4], AX.X, ALU.max))
                        step(nc.vector.tensor_tensor(G[5], G[4], over(mx, E), ALU.is_equal))
                        step(nc.vector.tensor_tensor(G[5], G[5], first_of, ALU.mult))
                        step(nc.vector.tensor_reduce(sm, G[5], AX.X, ALU.max))
                        step(nc.vector.tensor_tensor(G[6 + n], first_of, over(sm, E), ALU.is_equal))
                        if n == 0:
                            step(nc.vector.scalar_tensor_tensor(G[4], G[6], -FAR, G[4], ALU.mult, ALU.add))
                    step(nc.vector.tensor_tensor(chosen[0:N, :, :], G[6], G[7], ALU.add))
                    assert steps[0] == CHOSEN_STEP, steps
                    step(nc.vector.tensor_tensor(cw[0:N, :, 0:E], chosen[0:N, :, :], prob_e, ALU.mult))

                def list_rows():
                    bank = await_full(dve, g, ("rank",))
                    rank = ps[0:N, bank, 0:GB * E].rearrange("p (b e) -> p b e", b=GB)
                    place = G[1]
                    step(nc.vector.tensor_tensor(place, rank, next_row[0:N, :].unsqueeze(1).to_broadcast([N, GB, E]), ALU.add))
                    step(nc.vector.tensor_tensor(gate[0:N, 4:6, :, :], gate[0:N, 6:8, :, :],
                                                 place.unsqueeze(1).to_broadcast([N, TOPK, GB, E]), ALU.mult))
                    step(nc.vector.tensor_reduce(row_f[0:N, :, :], gate[0:N, 4:6, :, :], AX.X, ALU.add))
                    step(nc.vector.tensor_scalar(row_of[0:N, :, :], row_f[0:N, :, :], 1.0, None, ALU.subtract))
                    step(nc.vector.tensor_tensor(rows[0:N, :, IDS:ROW], G[6], over(number[0:N, 0:GB], E), ALU.add))
                    taken[bank].by(nc.vector.tensor_tensor(next_row[:, :], next_row[:, :], ps[:, bank, GB * E:(GB + 1) * E], ALU.add))
                    await_taken(dve, g, ("rank",))
                    step(nc.vector.tensor_scalar(number[0:N, 0:GB], number[0:N, 0:GB], float(TOPK * GT), None, ALU.add))
                    assert steps[0] == gate_step.per_pass, steps

                centre_logits()
                if prepare:
                    prepare_next(g)
                for q in range(SHC):
                    gated(q)
                add_out("s")
                choose_groups()
                if prepare:
                    rotate(g, range(QUADS))
                choose_experts()
                if prepare:
                    rotate(g, range(QUADS, 2 * QUADS))
                list_rows()
                add_out("b")

            prepare_next(-1)
            rotate(-1, range(2))
            token_variance(1)
            token_norm(1)
            token_gain(1)
            token_bias(1)
            rotate(-1, range(2, 2 * QUADS))
            passes(dve, body)

            steps = [0]

            def step(ins):
                ins.then_inc(tables_step, 1)
                steps[0] += 1
                dve.wait_ge(tables_step, steps[0])

            def table(first, n):
                return counts[0:1, first:first + n]

            tile_no = table(COUNT_TILE, TILES)
            length, n_tiles, first_tile = (t_e[:, i, :] for i in range(3))
            lists_first, list_length, within = (t_small[:, i, 0:TILES] for i in range(3))
            padded = t_small[:, 3, :]
            expert = padded[:, BEHIND:BEHIND + TILES]
            packed = t_small[:, 4, 0:TILES // UNROLL + 1]
            FULL = COUNTS - COUNT_FULL
            step(nc.vector.memset(pad_rows[:, 0:IDS], 0.0))
            step(nc.vector.tensor_copy(pad_rows[:, IDS:ROW], number[:, GB:GB + 1].to_broadcast([128, E])))
            step(nc.vector.tensor_scalar(pad_row[:, :], next_row[0:1, :], 1.0, None, ALU.subtract))
            assert steps[0] == PAD_STEPS, steps
            step(nc.vector.memset(padded, 0.0))
            step(nc.vector.tensor_tensor(length, next_row[0:1, :], table(COUNT_BASE, E), ALU.subtract))
            begun = t_cmp[:, 0:E * FULL].rearrange("p (e n) -> p e n", e=E)
            step(nc.vector.tensor_tensor(begun, length.unsqueeze(2).to_broadcast([1, E, FULL]),
                                         table(COUNT_FULL, FULL).unsqueeze(1).to_broadcast([1, E, FULL]), ALU.is_gt))
            step(nc.vector.tensor_reduce(n_tiles, begun, AX.X, ALU.add))
            lower = t_cmp[:, 0:E * E].rearrange("p (e n) -> p e n", e=E)
            step(nc.vector.tensor_tensor(lower, n_tiles.unsqueeze(1).to_broadcast([1, E, E]), tri[0:1, :, :], ALU.mult))
            step(nc.vector.tensor_reduce(first_tile, lower, AX.X, ALU.add))
            begun = t_cmp[:, 0:TILES * (E - 1)].rearrange("p (t e) -> p t e", e=E - 1)
            firsts = first_tile[:, 1:E].unsqueeze(1).to_broadcast([1, TILES, E - 1])
            step(nc.vector.tensor_tensor(begun, tile_no.unsqueeze(2).to_broadcast([1, TILES, E - 1]), firsts, ALU.is_ge))
            step(nc.vector.tensor_reduce(expert, begun, AX.X, ALU.add))
            step(nc.vector.tensor_tensor(begun, begun, firsts, ALU.mult))
            step(nc.vector.tensor_reduce(lists_first, begun, AX.X, ALU.max))
            own_list = t_cmp[:, 0:TILES * E].rearrange("p (t e) -> p t e", e=E)
            step(nc.vector.tensor_tensor(own_list, table(COUNT_EXPERT, E).unsqueeze(1).to_broadcast([1, TILES, E]),
                                         expert.unsqueeze(2).to_broadcast([1, TILES, E]), ALU.is_equal))
            step(nc.vector.tensor_tensor(own_list, own_list, length.unsqueeze(1).to_broadcast([1, TILES, E]), ALU.mult))
            step(nc.vector.tensor_reduce(list_length, own_list, AX.X, ALU.add))
            step(nc.vector.tensor_tensor(within, tile_no, lists_first, ALU.subtract))
            step(nc.vector.scalar_tensor_tensor(within, within, float(TS), list_length, ALU.mult, ALU.min))
            step(nc.vector.scalar_tensor_tensor(tile_row[:, :], expert, float(CAP), within, ALU.mult, ALU.add))
            for j in range(WINDOW):
                part = padded[:, j:j + (TILES // UNROLL) * UNROLL + 1:UNROLL]
                if j == 0:
                    step(nc.vector.tensor_copy(packed, part))
                else:
                    step(nc.vector.scalar_tensor_tensor(packed, part, float(E ** j), packed, ALU.mult, ALU.add))
            step(nc.vector.tensor_copy(windows[:, :], packed))
            assert steps[0] == TABLE_STEPS, steps

            dve.wait_ge(biases_in, 16 * 2)
            window = [None]

            def step(at, turn, k):
                t0, t1, t2, t3 = (at(n) for n in range(4))
                if k == 0:
                    window[0] = experts_around(dve, at)
                if live(t1):
                    e1 = expert_at(dve, window[0], k, 1)
                if live(t2):
                    j = (k - 2) % 2
                    passed(dve, e_silu, t2)
                    passed(dve, e_hid_turned, at(4))
                    nc.vector.tensor_tensor(e_hid[:, j, :], e_hb[:, j, 0:INTER], e_hb[:, j, INTER:2 * INTER], ALU.mult).then_inc(e_hid_done, 1)
                if live(t1):
                    j = (k - 1) % UNROLL
                    moved_tile(dve, e_rows_in, j, turn(1))
                    passed(dve, e_y_done, at(1 + UNROLL))
                    passed(dve, e_id_done, at(1 + UNROLL))
                    nc.vector.tensor_scalar(e_wid[:, j, 0:1], e_rows[:, j, D:D + E][:, bass.ds(e1, 1)], 1.0, None, ALU.mult)
                    nc.vector.tensor_scalar(e_wid[:, j, 1:2], e_rows[:, j, IDS:ROW][:, bass.ds(e1, 1)], 1.0, None, ALU.mult).then_inc(e_wid_done, 1)
                if live(t1):
                    j = (k - 1) % 2
                    passed(dve, e_h_done, t1)
                    passed(dve, e_hid_done, at(3))
                    nc.vector.tensor_tensor(e_hb[:, j, :], ps[:, 2 + j, 0:2 * INTER],
                                            b13[:, bass.ds(e1, 1), :].rearrange("p o n -> p (o n)"), ALU.add).then_inc(e_biased, 1)
                if live(t3):
                    j = (k - 3) % UNROLL
                    moved_tile(dve, e_stored, j, turn(3 + UNROLL))
                    passed(dve, e_wid_done, t3)
                    trash = counts[:, COUNT_TRASH:COUNT_TRASH + TILES][:, t3:t3 + 1] if isinstance(t3, int) else \
                        counts[:, COUNT_TRASH:COUNT_TRASH + TILES][:, bass.ds(t3, 1)]
                    nc.vector.scalar_tensor_tensor(e_trash[:, j:j + 1], e_wid[:, j, 1:2], float(TRASH), trash, ALU.is_ge, ALU.mult).then_inc(e_trash_done, 1)
                    passed(dve, e_trash_done, t3)
                    nc.vector.tensor_tensor(e_id[:, j:j + 1], e_wid[:, j, 1:2], e_trash[:, j:j + 1], ALU.add).then_inc(e_id_done, 1)
                    passed(dve, e_y_full, t3)
                    nc.vector.tensor_scalar(e_y[:, j, :], ps[:, 6 + j % 2, 0:D], e_wid[:, j, 0:1], None, ALU.mult).then_inc(e_y_done, 1)

            tiles(dve, step, 3)

            for t in range(GROUPS):
                k = t % PLACES
                dve.wait_ge(f_in[k], 32 * (t // PLACES + 1))
                nc.vector.tensor_tensor(f_h[0:N, k, :, :], f_h[0:N, k, :, :], f_y[k][0:N, :, 0, :], ALU.add).then_inc(f_half, 1)
                dve.wait_ge(f_half, t + 1)
                nc.vector.tensor_tensor(f_h[0:N, k, :, :], f_h[0:N, k, :, :], f_y[k][0:N, :, 1, :], ALU.add).then_inc(f_sum, 1)

        @block.tensor
        def _(pe):
            pe.wait_ge(ident_in, 16)
            def turn(t):
                pe.wait_ge(p_norm, t + 1)
                if t >= 2:
                    pe.wait_ge(p_affine, PCH * (t - 1))
                for m in range(PCH):
                    last = nc.tensor.transpose(ps[:, 2 * (t % 2) + m // 3, (m % 3) * PR:(m % 3 + 1) * PR],
                                               patch[:, t % 2, m * 128:(m + 1) * 128], ident[0:PR, 0:PR])
                last.then_inc(p_turned, 1)

            def project(t):
                pe.wait_ge(p_affine, PCH * (t + 1))
                if t >= 2:
                    pe.wait_ge(z_bias, t - 1)
                for m in range(PCH):
                    last = nc.tensor.matmul(ps[0:PR, 4 + t % 2, 0:D], patchT[:, t % 2, m, :], wp[:, m, :],
                                            start=(m == 0), stop=(m == PCH - 1))
                last.then_inc(p_proj, 1)

            turn(0)
            pe.wait_ge(wp_in, 16 * 2)
            for t in range(2 * SIDE):
                if t + 1 < 2 * SIDE:
                    turn(t + 1)
                project(t)
            def turn_tokens(g, key, x, s, images=range(GB)):
                pe.wait_ge(s.sem, s.at(g, images[-1] + 1))
                for kc in range(KD):
                    bank = TURN[(key, kc)][0] if images[0] else claim(g, (key, kc))
                    for b in images:
                        last = nc.tensor.transpose(ps[:, bank, b * N:(b + 1) * N], x[0:N, b, kc * 128:(kc + 1) * 128], ident[0:N, 0:N])
                    if images[-1] == GB - 1:
                        full[bank].by(last)

            def over_features(bank, w, x):
                for kc in range(KD):
                    last = nc.tensor.matmul(ps[:, bank, 0:GT], w(kc), x[:, kc, :], start=(kc == 0), stop=(kc == KD - 1))
                full[bank].by(last)

            def project_qk(g):
                for kc in range(KD):
                    await_taken(pe, g, ("xT", kc))
                for i in range(2 * QUADS):
                    j, which = divmod(i, 2)
                    for half in range(2):
                        over_features(claim(g, ("qk", i, half)), lambda kc: wqk[:, kc, which, half, j * 128:(j + 1) * 128], xT)

            def project_v(g, images):
                for b in images:
                    for n in range(2):
                        bank = claim(g, ("v", b, n))
                        for kc in range(KD):
                            last = nc.tensor.matmul(ps[0:N, bank, :], xT[:, kc, b * N:(b + 1) * N], wv[:, kc, n * 512:(n + 1) * 512],
                                                    start=(kc == 0), stop=(kc == KD - 1))
                        full[bank].by(last)

            turn_tokens(-1, "xT", xn, ln["a"]["norm"])
            pe.wait_ge(wqk_in, 16 * 8)
            project_qk(-1)
            pe.wait_ge(wv_in, 16)
            project_v(-1, (0, 1))

            def body(g, prepare):
                def scores(b):
                    cols = slice(b * N, (b + 1) * N)
                    for r in range(4):
                        claim(g, ("s", b, r))
                    for j in range(QUADS):
                        for r in range(4):
                            rows = slice(DH * (r % 2), DH * (r % 2 + 1))
                            last = nc.tensor.matmul(ps[0:N, r, j * N:(j + 1) * N], qkr[rows, 0, 2 * j + r // 2, cols],
                                                    qkr[rows, 1, 2 * j + r // 2, cols], start=True, stop=True)
                            if j == QUADS - 1:
                                full[r].by(last)

                def turn_probs(b):
                    for r in range(4):
                        pe.wait_ge(s_exp.sem, s_exp.at(g, 4 * b + r + 1))
                        bank = claim(g, ("pT", b, r))
                        for j in range(QUADS):
                            last = nc.tensor.transpose(ps[0:N, bank, j * N:(j + 1) * N], prob[0:N, b % 2, r, j, :], ident[0:N, 0:N])
                        full[bank].by(last)

                def attend(b):
                    for r in range(4):
                        await_taken(pe, g, ("pT", b, r))
                    for c in range(2):
                        bank = claim(g, ("o", b, c))
                        for i in range(8):
                            head = 8 * c + i
                            j, r = divmod(head, 4)
                            last = nc.tensor.matmul(ps[0:N, bank, i * DH:(i + 1) * DH], probT[0:N, r, j * N:(j + 1) * N],
                                                    vv[0:N, b, head * DH:(head + 1) * DH], start=True, stop=True)
                        full[bank].by(last)

                def turn_heads(b):
                    for c in range(2):
                        await_taken(pe, g, ("o", b, c))
                    for c in range(2):
                        bank = claim(g, ("oT", b, c))
                        for m in range(4):
                            chunk = 4 * c + m
                            last = nc.tensor.transpose(ps[:, bank, m * N:(m + 1) * N], o[0:N, chunk * 128:(chunk + 1) * 128], ident[0:N, 0:N])
                        full[bank].by(last)

                def project_heads(b):
                    for c in range(2):
                        await_taken(pe, g, ("oT", b, c))
                    bank = claim(g, ("wo", b))
                    for c in range(OC):
                        last = nc.tensor.matmul(ps[0:N, bank, 0:D], oT[:, c, :], wout[:, c, :], start=(c == 0), stop=(c == OC - 1))
                    full[bank].by(last)

                for moved in restacked:
                    pe.wait_ge(moved.sem, moved.at(g, 0))
                scores(0)
                project_v(g, (2, 3))
                pe.wait_ge(wout_in, 16)
                for b in range(GB):
                    if b == 0:
                        for bb in range(GB):
                            for n in range(2):
                                await_taken(pe, g if bb >= 2 else g - 1, ("v", bb, n))
                    if b + 1 < GB:
                        scores(b + 1)
                    turn_probs(b)
                    if b:
                        turn_heads(b - 1)
                    attend(b)
                    if b:
                        project_heads(b - 1)
                turn_heads(GB - 1)
                project_heads(GB - 1)

                for images in ((0, 1), (2, 3)):
                    turn_tokens(g, "fT", rows, ln["f"]["norm"], images)
                for kc in range(KD):
                    await_taken(pe, g, ("fT", kc))
                bank = claim(g, ("gate",))
                for b in range(GB):
                    for kc in range(KD):
                        last = nc.tensor.matmul(ps[0:N, bank, b * E:(b + 1) * E], fT[:, kc, b * N:(b + 1) * N], gwT[:, kc, :],
                                                start=(kc == 0), stop=(kc == KD - 1))
                full[bank].by(last)

                def hidden(q):
                    key = f"s{q}"
                    for n, ws in ((1, ws1), (3, ws3)):
                        over_features(claim(g, (key, n)), lambda kc: ws[:, kc, q * 128:(q + 1) * 128], fT)

                def out_rows(key, lhs, rhs):
                    for p in range(2):
                        bank = claim(g, ("y", key, p))
                        for bb in range(2):
                            b = 2 * p + bb
                            for c in range(len(lhs)):
                                last = nc.tensor.matmul(ps[0:N, bank, bb * D:(bb + 1) * D], lhs[c][:, b * N:(b + 1) * N], rhs[c],
                                                        start=(c == 0), stop=(c == len(lhs) - 1))
                        full[bank].by(last)

                pe.wait_ge(shared_in, 16 * 3)
                for q in range(SHC):
                    hidden(q)
                for q in range(SHC):
                    await_taken(pe, g, (f"s{q}", 3))
                if prepare:
                    turn_tokens(g, "xT", xn, ln["a"]["norm"])
                out_rows("s", [shid[:, c, :] for c in range(SHC)], [ws2[:, c, :] for c in range(SHC)])
                if prepare:
                    project_qk(g)
                    project_v(g, (0, 1))
                pe.wait_ge(gate_step.sem, gate_step.at(g, CHOSEN_STEP))
                bank = claim(g, ("rank",))
                for b in range(GB):
                    for bb in range(b + 1):
                        nc.tensor.matmul(ps[0:N, bank, b * E:(b + 1) * E], before[:, :] if bb == b else ones[0:N, 0:N],
                                         chosen[0:N, bb, :], start=(bb == 0), stop=(bb == b))
                for b in range(GB):
                    last = nc.tensor.matmul(ps[:, bank, GB * E:(GB + 1) * E], ones[0:N, :], chosen[0:N, b, :],
                                            start=(b == 0), stop=(b == GB - 1))
                full[bank].by(last)
                pe.wait_ge(gate_step.sem, gate_step.at(g, CHOSEN_STEP + 1))
                bank = claim(g, ("cT",))
                for b in range(GB):
                    last = nc.tensor.transpose(ps[0:E + 1, bank, b * N:(b + 1) * N], cw[0:N, b, :], ident[0:N, 0:N])
                full[bank].by(last)
                await_taken(pe, g, ("cT",))
                out_rows("b", [cT], [be2s[:, :]])

            passes(pe, body)

            pe.wait_ge(experts_in, 16 * 5)
            pe.wait_ge(tables_step, TABLE_STEPS)
            for key in [("rank",), ("cT",), ("y", "b", 0), ("y", "b", 1), ("s0", 1), ("s0", 3), ("s1", 1), ("s1", 3)]:
                await_taken(pe, GROUPS - 1, key)
            window = [None]

            def step(at, turn, k):
                t0, t1, t2, t3 = (at(n) for n in range(4))
                if k == 0:
                    window[0] = experts_around(pe, at)
                if live(t1):
                    e1 = expert_at(pe, window[0], k, 1)
                if live(t3):
                    e3 = expert_at(pe, window[0], k, 3)
                if live(t0):
                    moved_tile(pe, e_rows_in, k, turn(0))
                    passed(pe, e_xT_done, at(2))
                    for kc in range(KD):
                        last = nc.tensor.transpose(ps[:, k % 2, kc * TS:(kc + 1) * TS], e_rows[:, k, kc * 128:(kc + 1) * 128], ident[:, :])
                    last.then_inc(e_turned, 1)
                if live(t1):
                    j = (k - 1) % 2
                    passed(pe, e_xT_done, t1)
                    passed(pe, e_biased, at(3))
                    for kc in range(KD):
                        last = nc.tensor.matmul(ps[:, 2 + j, 0:2 * INTER], e_xT[:, j, kc, :],
                                                w13[:, bass.ds(e1, 1), kc, :].rearrange("p o n -> p (o n)"),
                                                start=(kc == 0), stop=(kc == KD - 1))
                    last.then_inc(e_h_done, 1)
                if live(t2):
                    j = (k - 2) % 2
                    passed(pe, e_hid_done, t2)
                    passed(pe, e_hidT_done, at(4))
                    nc.tensor.transpose(ps[:, 4 + j, 0:TS], e_hid[:, j, :], ident[:, :]).then_inc(e_hid_turned, 1)
                if live(t3):
                    j = (k - 3) % 2
                    passed(pe, e_hidT_done, t3)
                    passed(pe, e_y_done, at(5))
                    nc.tensor.matmul(ps[:, 6 + j, 0:D], e_hidT[:, j, :], we2[:, bass.ds(e3, 1), :].rearrange("p o n -> p (o n)"),
                                     start=True, stop=True).then_inc(e_y_full, 1)

            tiles(pe, step, 3)

        for s in signals:
            assert s.given == 2 * s.per_pass, (s.name, s.given, s.per_pass)


INPUTS = ["x", "txt", "L0_tok_ln1_g", "L0_tok_ln1_b", "L0_tok_W_proj", "L0_tok_b_proj", "L0_tok_ln2_g", "L0_tok_ln2_b",
          "L0_tok_cls_token", "L0_tok_pos_emb", "L0_attn_ln_gamma", "L0_attn_ln_beta", "L0_attn_w_qkv", "L0_attn_w_out",
          "L0_ffn_gate_w", "L0_ffn_gate_b", "L0_ffn_We1", "L0_ffn_be1", "L0_ffn_We2", "L0_ffn_be2", "L0_ffn_We3",
          "L0_ffn_be3", "L0_ffn_ws1", "L0_ffn_bs1", "L0_ffn_ws2", "L0_ffn_bs2", "L0_ffn_ws3", "L0_ffn_bs3"]


def shape_constants():
    import numpy as np
    inv = (1.0 / 10000.0 ** (np.arange(0, DH, 2, dtype=np.float32) / np.float32(DH))).astype(np.float32)
    rows = np.arange(N)
    step = np.where(rows < NP, rows, np.where(rows == NP, 0, rows - 1)).astype(np.float32)
    angle = (inv[:, None] * step[None, :]).astype(np.float32)
    return {"cosT": np.tile(np.cos(angle), (4, 1)).astype(np.float32), "sinT": np.tile(np.sin(angle), (4, 1)).astype(np.float32),
            "ident": np.eye(128, dtype=np.float32),
            "counts": np.concatenate([np.arange(E), np.arange(E) * CAP + 1, np.arange(TILES), np.arange(TILES) * TS,
                                      E - np.arange(E),
                                      np.arange(COUNTS - COUNT_FULL) * TS]).astype(np.float32),
            "before": np.triu(np.ones((N, N), np.float32), 1),
            "number": np.concatenate([(TOPK * (np.arange(GB)[None, :] * N + np.arange(128)[:, None])),
                                      TRASH + np.arange(128)[:, None]], axis=1).astype(np.float32),
            "tri": (np.arange(E)[None, :] < np.arange(E)[:, None]).astype(np.float32).reshape(-1)}


def kernel(**inputs):
    import numpy as np
    import concourse.bacc as bacc
    from concourse.bass_utils import run_bass_kernel_spmd

    nc = bacc.Bacc("TRN2", target_bir_lowering=False, num_devices=1)
    arrays, aps = {}, {}
    for name, array in [(n, inputs[n]) for n in INPUTS] + list(shape_constants().items()):
        array = np.ascontiguousarray(array)
        arrays[f"in_{name}"] = array
        aps[name] = nc.dram_tensor(f"in_{name}", array.shape, F32, kind="ExternalInput").ap()
    zscr = nc.dram_tensor("image_tokens", (B, NP, D), F32, kind="Internal").ap()
    out = nc.dram_tensor("out_0", (B, N, D), F32, kind="ExternalOutput").ap()
    hrows = nc.dram_tensor("sums_without_experts", (GROUPS, N, GB, D), F32, kind="Internal").ap()
    xrows = nc.dram_tensor("expert_lists", (E * CAP, ROW), F32, kind="Internal").ap()
    yrows = nc.dram_tensor("expert_results", (TRASH + TILES * TS, D), F32, kind="Internal").ap()
    early_fusion_program(nc, aps, out, zscr, hrows, xrows, yrows)
    result = run_bass_kernel_spmd(nc, [arrays], core_ids=[0])
    return result.results[0]["out_0"]
```

```python
from contextlib import ExitStack

import concourse.bass as bass
from concourse import mybir
from concourse.alu_op_type import AluOpType as ALU

F32 = mybir.dt.float32
F16 = mybir.dt.float16
I32 = mybir.dt.int32
U32 = mybir.dt.uint32
ACT = mybir.ActivationFunctionType
AX = mybir.AxisListType

B, C, IMG, PATCH = 32, 3, 96, 16
SIDE = IMG // PATCH
NP = SIDE * SIDE
TXT = 77
N = NP + 1 + TXT
D = 256
KD = D // 128
HEADS, DH = 16, 64
HALF = DH // 2
QUADS = HEADS // 4
SCALE = DH ** -0.5
E, G4, EPG = 16, 4, 4
INTER = 128
SHC = 2
GB = 4
GROUPS = B // GB
GT = GB * N
HB = B // 2
PR = HB * SIDE
PCH = 2 * C
EPS = 1e-5
OC = HEADS * DH // 128
ROPES = 2
TABLES = 18

SPLIT = ((0, 0), (0, 1), (1, 0))
W_SCALE = 256.0
V_SCALE = 16.0
CHUNK = 1024

TS = 128
TOPK = 2
CAP = B * N + TS
TILES = (B * N * TOPK - E) // TS + E
ONE = D + E
IDS = ONE + 1
ROW = IDS + E
TRASH = TOPK * B * N
PLACES = 4
UNROLL = 4
BEHIND, WINDOW = 3, 6
COUNT_EXPERT, COUNT_BASE, COUNT_TILE, COUNT_TRASH, COUNT_DOWN, COUNT_FULL = 0, E, 2 * E, 2 * E + TILES, 2 * E + 2 * TILES, 3 * E + 2 * TILES
COUNTS = COUNT_FULL + -(-B * N // TS)
CHOSEN_STEP = 33
GATE_STEPS = CHOSEN_STEP + 7
PAD_STEPS = 3
TILE_STEPS = PAD_STEPS + 15
TABLE_STEPS = TILE_STEPS + 3 + 7
FAR = 1e30


class Signal:

    def __init__(self, nc, ctx, name, per_pass, start=1):
        self.name, self.per_pass, self.start, self.given = name, per_pass, start, 0
        self.sem = ctx.enter_context(nc.semaphore(name))

    def by(self, ins, count=1):
        self.given += count
        ins.then_inc(self.sem, count)

    def at(self, g, n):
        return g * self.per_pass + (n + self.start)


LATE_KEYS = [("rank",), ("cT",), ("y", "b", 0), ("y", "b", 1)]


def pe_bank_schedule():
    turns, uses = {}, [0] * 8

    def put(key, bank):
        turns[key] = (bank, uses[bank])
        uses[bank] += 1

    def values(b):
        for n in range(2):
            put(("v", b, n), 2 * b + n)

    def scores(b):
        for r in range(4):
            put(("s", b, r), r)

    scores(0)
    values(3)
    for b in range(GB):
        if b + 1 < GB:
            scores(b + 1)
        for c in range(4):
            put(("pT", b, c), 4 + c % 2)
        if b:
            for c in range(2):
                put(("oT", b - 1, c), 4 + c)
        for c in range(2):
            put(("o", b, c), 6 + c)
        if b:
            put(("wo", b - 1), 4)
    for c in range(2):
        put(("oT", GB - 1, c), 4 + c)
    put(("wo", GB - 1), 4)

    for kc in range(KD):
        put(("fT", kc), 6 + kc)
    put(("gate",), 5)

    def hidden(key, pair):
        put((key, 1), 2 * pair)
        put((key, 3), 2 * pair + 1)

    hidden("s0", 1)
    hidden("s1", 0)
    for kc in range(KD):
        put(("xT", kc), 6 + kc)
    for p in range(2):
        put(("y", "s", p), 4 + p)
    for i in range(2 * QUADS):
        for half in range(2):
            put(("qk", i, half), (2 * i + half) % 8)
    for b in range(3):
        values(b)
    put(("rank",), 6)
    put(("cT",), 7)
    for p in range(2):
        put(("y", "b", p), 4 + p)

    def per_bank(belongs):
        return [sum(bank == i and belongs(key) for key, (bank, _) in turns.items()) for i in range(8)]

    count = per_bank(lambda key: key[0] in ("xT", "qk") or key[0] == "v" and key[1] < 3), per_bank(lambda key: key in LATE_KEYS)
    return turns, uses, *count


def early_fusion_program(nc, a, out, zscr, hrows, xrows, yrows):
    TURN, USES, AHEAD, LATE = pe_bank_schedule()
    ctx = ExitStack()
    with ctx:
        def sb(name, shape, dt=F32):
            return ctx.enter_context(nc.sbuf_tensor(name, shape, dt))

        def sem(name):
            return ctx.enter_context(nc.semaphore(name))

        signals = []

        def signal(name, per_pass, start=1):
            signals.append(Signal(nc, ctx, name, per_pass, start))
            return signals[-1]

        w_parts = sb("w_parts", [128, 2, KD * 4 * HEADS * HALF + KD * HEADS * DH + OC * D], F16)
        w13_space = sb("w13_space", [128, E * KD * 2 * INTER])
        we2 = sb("we2", [128, E, D])
        ws1 = sb("ws1", [128, KD, SHC * INTER])
        ws3 = sb("ws3", [128, KD, SHC * INTER])
        ws2 = sb("ws2", [128, SHC, D])
        gwT = sb("gwT", [128, KD, E])
        be2s = sb("be2s", [E + 1, D])
        bs1T = sb("bs1T", [128, SHC])
        bs3T = sb("bs3T", [128, SHC])
        lngT = sb("lngT", [128, KD])
        lnbT = sb("lnbT", [128, KD])
        gateb = sb("gateb", [128, E])
        cosT = sb("cosT", [128, N])
        sinT = sb("sinT", [128, N])
        ident = sb("ident", [128, 128])
        tri = sb("tri", [128, E, E])
        pos = sb("pos", [NP + 1, D])
        counts = sb("counts", [128, COUNTS])
        before = sb("before", [N, N])
        ones = sb("ones", [128, 128])
        minus_half = sb("minus_half", [128, 2 * SIDE])
        g1T = sb("g1T", [128, PCH])
        b1T = sb("b1T", [128, PCH])

        qk_space = sb("qk_space", [128, 2 * (HEADS // 2) * GT])
        vp_space = sb("vp_space", [128, GB * HEADS * DH + 2 * HEADS * N])
        rope_space = sb("rope_space", [128, (ROPES * 4 + 2 * 2) * GT])
        o_space = sb("o_space", [128, HEADS * DH])
        h = sb("h", [128, GB, D])
        h2 = sb("h2", [128, GB, D])
        xn = sb("xn", [128, GB, D])
        xT = sb("xT", [128, 2, KD, GT], F16)
        probT_space = sb("probT_space", [128, 4 * 4 * N])
        oT = sb("oT", [128, 2, OC, N], F16)
        smax = sb("smax", [128, 2, 4, 4])
        ssum = sb("ssum", [128, 2, 4, 4])
        srec = sb("srec", [128, 2, 4, 4])
        gate = sb("gate", [128, 8, GB, E])
        few = sb("few", [128, 8, GB, G4])
        chosen = sb("chosen", [128, GB, E])
        next_row = sb("next_row", [128, E])
        number = sb("number", [128, GB + 2])
        row_f = sb("row_f", [128, TOPK, GB])
        row_of = sb("row_of", [128, TOPK, GB], U32)
        windows = sb("windows", [1, TILES // UNROLL + 1], I32)
        tile_row = sb("tile_row", [1, TILES], I32)
        pad_row = sb("pad_row", [1, E], I32)
        ln_stats = sb("ln_stats", [128, 2, GB, 6])
        ln_mv = sb("ln_mv", [128, 2, GB, 2])
        ln_small = sb("ln_small", [128, 2, 8, GB])
        wait_carrier = sb("wait_carrier", [1, 1])

        def view(space, at, p, shape):
            size = 1
            for s in shape:
                size *= s
            flat = space[0:p, at:at + size]
            names = " ".join(f"d{i}" for i in range(len(shape)))
            return flat.rearrange(f"p ({names}) -> p {names}", **{f"d{i}": s for i, s in enumerate(shape)})

        at = 0
        def place(space, p, shape):
            nonlocal at
            size = 1
            for n in shape:
                size *= n
            at += size
            return view(space, at - size, p, shape)
        qkr = view(qk_space, 0, 128, [2, HEADS // 2, GT])
        vv = view(vp_space, 0, 128, [GB, HEADS * DH])
        prob = view(vp_space, GB * HEADS * DH, 128, [2, 4, 4, N])
        rotated = view(rope_space, 0, 128, [ROPES, 2, 2, GT])
        product = view(rope_space, ROPES * 4 * GT, 128, [2, 2, GT])
        o = o_space
        probT = view(probT_space, 0, 128, [4, 4 * N])
        w13 = view(w13_space, 0, 128, [E, KD, 2 * INTER])
        at = 0
        wqk32 = place(w13_space, 128, [KD, 2, 2, HEADS * HALF])
        wv32 = place(w13_space, 128, [KD, HEADS * DH])
        wout32 = place(w13_space, 128, [OC, D])
        W_COLUMNS = at
        at = 0

        def parts(shape):
            nonlocal at
            size = 1
            for n in shape:
                size *= n
            at += size
            names = " ".join(f"d{i}" for i in range(len(shape)))
            return w_parts[:, :, at - size:at].rearrange(f"p x ({names}) -> p x {names}", **{f"d{i}": n for i, n in enumerate(shape)})

        wqk = parts([KD, 2, 2, HEADS * HALF])
        wv = parts([KD, HEADS * DH])
        wout = parts([OC, D])
        xT32 = view(rope_space, 6 * GT, 128, [KD, GT])
        sil = view(rope_space, 0, 128, [2, GT])
        fT = view(rope_space, 4 * GT, 128, [KD, GT])
        cT = probT[0:E + 1, 0, :]
        shid = view(o_space, 0, 128, [SHC, GT])
        rows = view(vp_space, GB * HEADS * DH + HEADS * N, 128, [GB, ROW])
        cw = rows[:, :, D:IDS]
        pairs = view(vp_space, GB * HEADS * DH, 128, [2, GB, G4, G4])
        at = 0
        b13 = place(qk_space, 128, [E, 2 * INTER])
        e_hb = place(qk_space, 128, [2, 2 * INTER])
        e_hid = place(qk_space, 128, [2, INTER])
        e_hidT = place(qk_space, 128, [2, TS])
        e_xT = place(qk_space, 128, [2, KD, TS])
        e_y = place(qk_space, 128, [UNROLL, D])
        at = 0
        e_rows = place(vp_space, 128, [UNROLL, ROW])
        pad_rows = place(vp_space, 128, [ROW])
        e_wid = place(vp_space, 128, [UNROLL, 2])
        t_small = place(vp_space, 1, [2, TILES + 2 * UNROLL])
        t_e = place(vp_space, 128, [3, E])
        t_tile = place(vp_space, 128, [8])
        assert at <= GB * HEADS * DH
        t_cmp = view(rope_space, 0, 128, [E * (COUNTS - COUNT_FULL)])
        e_trash = sb("e_trash", [128, UNROLL])
        e_id = sb("e_id", [128, UNROLL], U32)
        f_h = [place(vp_space, 128, [GB, D]) for _ in range(GROUPS - 3)] + [h, xn, view(o_space, 0, 128, [GB, D])]
        f_y = [view(space, i * GB * TOPK * D, 128, [GB, TOPK, D]) for space in (qk_space, rope_space) for i in range(2)]
        IMGF = C * PATCH * IMG
        img = [view(s, 0, PR, [C, PATCH, SIDE, PATCH]) for s in (qk_space, vp_space)]
        PF = C * PATCH * PATCH
        wp = view(vp_space, IMGF, 128, [PCH, D])
        patch = view(vp_space, IMGF + PCH * D, PR, [2, PF])
        z = [view(qk_space, IMGF, PR, [SIDE, D]), view(probT_space, 0, PR, [SIDE, D])]
        patchT = view(qk_space, IMGF + SIDE * D, 128, [2, PCH, PR])
        bproj, g2, b2 = (view(rope_space, 4 * GT + i * D, PR, [D]) for i in range(3))
        at = 0
        tok_stats = place(o_space, PR, [4, SIDE, C * 6])
        tok_mv = place(o_space, PR, [4, SIDE, 2])
        tok_small = place(o_space, PR, [4, 2, SIDE])

        ps = ctx.enter_context(nc.psum_tensor("ps", [128, 8, 512], F32))

        img_in = [sem("img0_in"), sem("img1_in")]
        wp_in = sem("wp_in")
        ident_in = sem("ident_in")
        tok_in = sem("tok_in")
        tables_in = sem("tables_in")
        wqk_in = sem("wqk_in")
        w_scaled, w_high, w_low = sem("w_scaled"), sem("w_high"), sem("w_low")
        wv_in = sem("wv_in")
        wout_in = sem("wout_in")
        shared_in = sem("shared_in")
        experts_in = sem("experts_in")
        consts = sem("consts")
        z_out = [sem("z0_out"), sem("z1_out")]
        p_stats, p_mv, p_ve, p_rstd = sem("p_stats"), sem("p_mv"), sem("p_ve"), sem("p_rstd")
        p_norm, p_turned, p_affine, p_proj = sem("p_norm"), sem("p_turned"), sem("p_affine"), sem("p_proj")
        z_bias, z_stats, z_mv, z_ve = sem("z_bias"), sem("z_stats"), sem("z_mv"), sem("z_ve")
        z_rstd, z_norm, z_scaled, z_done = sem("z_rstd"), sem("z_norm"), sem("z_scaled"), sem("z_done")
        h_in = sem("h_in")
        h_stored = sem("h_stored")
        full = [signal(f"bank{i}_full", USES[i], AHEAD[i]) for i in range(8)]
        taken = [signal(f"bank{i}_taken", USES[i], AHEAD[i]) for i in range(8)]
        h_ready = signal("h_ready", 1, 1)
        ln = {}
        for k in "af":
            parts = 1 if k == "a" else 2
            ln[k] = {n: signal(f"{k}_{n}", c, c if k == "a" else 1)
                     for n, c in (("stats", GB), ("mv", GB), ("ve", parts), ("rstd", parts), ("norm", GB))}
        a_v1, a_v2, a_v3, a_r2, a_r12 = (signal(n, 1, 1) for n in ("a_v1", "a_v2", "a_v3", "a_r2", "a_r12"))
        ahead = [h_ready, a_v1, a_v2, a_v3, a_r2, a_r12, *ln["a"].values()]
        restacked = []
        for n in range(ROPES):
            moves = 8 * 16 * len(range(n, QUADS, ROPES))
            restacked.append(signal(f"restacked{n}", moves, moves))
        f_turned, f_early = signal("f_turned", KD), signal("f_early", KD)
        x_high, x_low = (signal(n, KD, KD) for n in ("x_high", "x_low"))
        o_high = signal("o_high", 2 * GB)
        rope_mul = signal("rope_mul", 2 * 2 * QUADS, 2 * 2 * QUADS)
        rope_sum = signal("rope_sum", 2 * 2 * QUADS, 2 * 2 * QUADS)
        ahead += [x_high, x_low, rope_mul, rope_sum, *full, *taken, *restacked]
        s_max = signal("s_max", 4 * GB)
        s_exp = signal("s_exp", 4 * GB)
        s_sum = signal("s_sum", GB)
        s_rec = signal("s_rec", GB)
        acc_half = signal("acc_half", 2 * 2)
        gate_step = signal("gate_step", GATE_STEPS)
        gate_exp = signal("gate_exp", 1)
        scattered = signal("scattered", 16 * TOPK * GB, 0)
        lists_done = signal("lists_done", 1)
        biases_in = sem("biases_in")
        tables_step = sem("tables_step")
        tables_turned = sem("tables_turned")
        pads_out = sem("pads_out")
        e_rows_in, e_stored = ([sem(f"{n}{k}") for k in range(UNROLL)] for n in ("e_rows_in", "e_stored"))
        e_turned, e_xT_done = sem("e_turned"), sem("e_xT_done")
        e_wid_done, e_h_done, e_biased, e_silu = sem("e_wid_done"), sem("e_h_done"), sem("e_biased"), sem("e_silu")
        e_hid_done, e_hid_turned, e_hidT_done = sem("e_hid_done"), sem("e_hid_turned"), sem("e_hidT_done")
        e_trash_done = sem("e_trash_done")
        e_y_full, e_y_done, e_id_done = sem("e_y_full"), sem("e_y_done"), sem("e_id_done")
        carrier = sem("carrier")
        f_sums_in, f_half, f_sum = sem("f_sums_in"), sem("f_half"), sem("f_sum")
        f_in, out_stored = ([sem(f"{n}{k}") for k in range(PLACES)] for n in ("f_in", "out_stored"))

        def bank_value(s, g, key, n):
            bank, turn = TURN[key]
            value = s[bank].at(g, turn + n)
            if isinstance(g, int) and g == -1:
                value += LATE[bank]
            if isinstance(g, int) and g == GROUPS - 1 and key in LATE_KEYS:
                value -= AHEAD[bank]
            return value

        def await_full(eng, g, key):
            bank = TURN[key][0]
            eng.wait_ge(full[bank].sem, bank_value(full, g, key, 1))
            return bank

        def await_taken(eng, g, key):
            bank = TURN[key][0]
            eng.wait_ge(taken[bank].sem, bank_value(taken, g, key, 1))

        def claim(g, key):
            bank = TURN[key][0]
            value = bank_value(taken, g, key, 0)
            if not (isinstance(value, int) and value == 0):
                nc.tensor.wait_ge(taken[bank].sem, value)
            return bank

        def images(g):
            return bass.ds(g * GB, GB) if not isinstance(g, int) else slice(g * GB, (g + 1) * GB)

        def passes(eng, body):
            with eng.Fori(0, GROUPS - 1) as g:
                body(g, True)
            body(GROUPS - 1, False)

        def tiles(eng, step, lag):
            for t in range(2 * UNROLL):
                step(lambda n, t=t: t - n, lambda n, t=t: (t - n) // UNROLL + 1, t % UNROLL)
            with eng.Fori(0, TILES // UNROLL - 2) as i:
                for k in range(UNROLL):
                    step(lambda n, k=k: i * UNROLL + (2 * UNROLL + k - n), lambda n, k=k: i + ((2 * UNROLL + k - n) // UNROLL + 1), k)
            for t in range(TILES, TILES + lag):
                step(lambda n, t=t: t - n, lambda n, t=t: (t - n) // UNROLL + 1, t % UNROLL)

        def pad_lists(eng, half):
            eng.wait_ge(tables_step, PAD_STEPS)
            with eng.Fori(0, E // 2) as e:
                row = eng.value_load(pad_row[0:1, bass.ds(e + half * (E // 2), 1)], min_val=0, max_val=E * CAP - TS)
                eng.dma_start(xrows[bass.ds(row, TS), :], pad_rows).then_inc(pads_out, 16)

        def experts_around(eng, at):
            t = at(0)
            window = windows[0:1, t // UNROLL:t // UNROLL + 1] if isinstance(t, int) else windows[0:1, bass.ds(t // UNROLL, 1)]
            return eng.value_load(window, min_val=0, max_val=E ** WINDOW - 1)

        def expert_at(eng, window, k, n):
            return eng.snap((window >> (4 * (k - n + BEHIND))) & (E - 1), min_val=0, max_val=E - 1)

        def live(t):
            return not isinstance(t, int) or 0 <= t < TILES

        def passed(eng, s, t):
            if not isinstance(t, int) or t >= 0:
                eng.wait_ge(s, t + 1)

        def moved_tile(eng, s, k, turn):
            if not isinstance(turn, int) or turn > 0:
                eng.wait_ge(s[k % UNROLL], turn * 16)

        block = ctx.enter_context(nc.Block())

        def load_images(eng, half):
            for i in range(HB):
                eng.dma_start(img[half][i * SIDE:(i + 1) * SIDE, :, :, :, :].rearrange("h c p w q -> h c (p w q)"),
                              a["x"][half * HB + i].rearrange("c (h p) w -> h c (p w)", p=PATCH)).then_inc(img_in[half], 16)

        @block.sync
        def _(sp):
            load_images(sp, 0)
            load_images(sp, 1)
            for kc in range(KD):
                for which in range(2):
                    for half in range(2):
                        sp.dma_start(
                            wqk32[:, kc, which, half, :].rearrange("k (h i) -> k h i", i=HALF),
                            a["L0_attn_w_qkv"][kc * 128:(kc + 1) * 128, which * HEADS * DH:(which + 1) * HEADS * DH]
                            .rearrange("k (h f i) -> k f h i", f=2, i=HALF)[:, half, :, :]).then_inc(wqk_in, 16)
            sp.dma_start(cosT[:, :], a["cosT"]).then_inc(tables_in, 16)
            sp.dma_start(sinT[:, :], a["sinT"]).then_inc(tables_in, 16)
            sp.dma_start(tri[:, :, :].rearrange("p a b -> p (a b)"), a["tri"].partition_broadcast(128)).then_inc(tables_in, 16)
            sp.dma_start(pos[0:NP, :], a["L0_tok_pos_emb"][0, 1:NP + 1, :]).then_inc(tables_in, 16)
            sp.dma_start(pos[NP:NP + 1, :], a["L0_tok_pos_emb"][0, 0:1, :]).then_inc(tables_in, 16)
            sp.dma_start(gateb[:, :], a["L0_ffn_gate_b"].partition_broadcast(128)).then_inc(tables_in, 16)
            for t, name in ((lngT, "L0_attn_ln_gamma"), (lnbT, "L0_attn_ln_beta"), (bs1T, "L0_ffn_bs1"), (bs3T, "L0_ffn_bs3")):
                sp.dma_start(t[:, :], a[name].rearrange("(c k) -> k c", k=128), allow_slow_non_contiguous=True).then_inc(tables_in, 16)
            sp.dma_start(counts[:, :], a["counts"].partition_broadcast(128)).then_inc(tables_in, 16)
            sp.dma_start(next_row[:, :], a["counts"][COUNT_BASE:COUNT_BASE + E].partition_broadcast(128)).then_inc(tables_in, 16)
            sp.dma_start(before[:, :], a["before"]).then_inc(tables_in, 16)
            sp.dma_start(number[:, :], a["number"]).then_inc(tables_in, 16)
            for c in range(KD):
                sp.dma_start(gwT[:, c, :], a["L0_ffn_gate_w"][:, c * 128:(c + 1) * 128].rearrange("e k -> k e"),
                              allow_slow_non_contiguous=True).then_inc(tables_in, 16)
            sp.dma_start(be2s[0:E, :], a["L0_ffn_be2"]).then_inc(tables_in, 16)
            sp.dma_start(be2s[E:E + 1, :], a["L0_ffn_bs2"].unsqueeze(0)).then_inc(tables_in, 16)
            sp.dma_start(wv32, a["L0_attn_w_qkv"][:, 2 * HEADS * DH:].rearrange("(c k) n -> k c n", c=KD)).then_inc(wv_in, 16)
            sp.dma_start(wout32, a["L0_attn_w_out"].rearrange("(c k) n -> k c n", c=OC)).then_inc(wout_in, 16)
            for w, name in ((ws1, "L0_ffn_ws1"), (ws3, "L0_ffn_ws3"), (ws2, "L0_ffn_ws2")):
                sp.dma_start(w[:, :, :], a[name].rearrange("(c k) n -> k c n", k=128)).then_inc(shared_in, 16)
            sp.dma_start(we2[:, :, :], a["L0_ffn_We2"].rearrange("e k n -> k e n")).then_inc(experts_in, 16)

            def store_image_tokens(half):
                sp.dma_start(zscr[half * HB:(half + 1) * HB, :, :].rearrange("b (h w) d -> (b h) w d", w=SIDE), z[half]).then_inc(z_out[half], 16)

            sp.wait_ge(z_done, 1)
            store_image_tokens(0)
            sp.wait_ge(z_out[0], 16)

            def load_tokens(g, src):
                sp.dma_start(h[0:NP, :, :], zscr[src, :, :].rearrange("b n d -> n b d")).then_inc(h_in, 16)
                sp.dma_start(h[NP:NP + 1, :, :], a["L0_tok_cls_token"][0, :, :].unsqueeze(1).to_broadcast([1, GB, D])).then_inc(h_in, 16)
                sp.dma_start(h[NP + 1:N, :, :], a["txt"][src, :, :].rearrange("b n d -> n b d")).then_inc(h_in, 16)

            def restack(g):
                for j in range(QUADS):
                    for half in range(2):
                        sp.wait_ge(rope_sum.sem, rope_sum.at(g, 2 * (2 * j + 1) + half + 1))
                        for r in range(4):
                            to = (r % 2) * DH + half * HALF
                            restacked[j % ROPES].by(sp.dma_start(qkr[to:to + HALF, :, 2 * j + r // 2, :],
                                                                 rotated[HALF * r:HALF * (r + 1), j % ROPES, :, half, :]), 16)

            load_tokens(-1, slice(0, GB))
            restack(-1)
            sp.wait_ge(z_done, 2)
            store_image_tokens(1)
            sp.wait_ge(w_low, W_COLUMNS // CHUNK)
            for half, name in enumerate(("L0_ffn_We1", "L0_ffn_We3")):
                for c in range(KD):
                    sp.dma_start(w13[:, :, c, half * INTER:(half + 1) * INTER],
                                 a[name][:, c * 128:(c + 1) * 128, :].rearrange("e k n -> k e n")).then_inc(experts_in, 16)
            sp.wait_ge(z_out[1], 16)

            def body(g, prepare):
                if prepare:
                    await_taken(sp, g, ("wo", GB - 1))
                    load_tokens(g, bass.ds((g + 1) * GB, GB))
                    restack(g)

            passes(sp, body)
            pad_lists(sp, 0)
            sp.wait_ge(pads_out, 16 * E)
            sp.wait_ge(tables_step, TABLE_STEPS)
            sp.wait_ge(scattered.sem, scattered.at(GROUPS - 1, scattered.per_pass))

            def step(at, turn, k):
                t = at(0)
                if live(t):
                    row = sp.value_load(tile_row[0:1, t:t + 1] if isinstance(t, int) else tile_row[0:1, bass.ds(t, 1)],
                                        min_val=0, max_val=E * CAP - TS)
                    passed(sp, e_turned, at(UNROLL))
                    passed(sp, e_wid_done, at(UNROLL))
                    sp.dma_start(e_rows[:, k, :], xrows[bass.ds(row, TS), :]).then_inc(e_rows_in[k], 16)

            tiles(sp, step, 0)
            def load_results(t):
                sp.dma_start(f_y[t % PLACES][0:N, :, :, :].rearrange("n b c d -> n b (c d)"),
                             yrows[t * TOPK * GT:(t + 1) * TOPK * GT, :].rearrange("(b n c) d -> n b (c d)", b=GB, c=TOPK)).then_inc(f_in[t % PLACES], 16)

            sp.wait_ge(h_stored, 16 + 16 * GROUPS)
            for t in range(GROUPS):
                sp.dma_start(f_h[t][0:N, :, :], hrows[t, :, :, :]).then_inc(f_sums_in, 16)
            for k in range(UNROLL):
                moved_tile(sp, e_stored, k, TILES // UNROLL)
            for t in range(GROUPS):
                if t >= PLACES:
                    sp.wait_ge(f_sum, t - PLACES + 1)
                load_results(t)
            for k in range(PLACES):
                sp.wait_ge(out_stored[k], 48 * GROUPS // PLACES)

        @block.gpsimd
        def _(pool):
            for s in signals:
                if s not in ahead and s.start:
                    pool.sem_inc(s.sem, 1)
            pool.sem_inc(h_stored, 16)
            nc.gpsimd.memset(minus_half[:, :], -0.5).then_inc(consts, 1)
            nc.gpsimd.memset(ones[:, :], 1.0).then_inc(consts, 1)
            pool.wait_ge(consts, 2)
            def tokenizer_power(ve_sem, rstd_sem, half, k):
                pool.wait_ge(ve_sem, half + 1)
                q = 2 * half + k
                nc.gpsimd.tensor_tensor(tok_small[:, q, 1, :], tok_small[:, q, 0, :], minus_half[0:PR, 0:SIDE],
                                        ALU.pow).then_inc(rstd_sem, 1)

            tokenizer_power(p_ve, p_rstd, 0, 0)
            tokenizer_power(p_ve, p_rstd, 1, 0)

            def split_low(i):
                pool.wait_ge(w_high, i + 1)
                cols = slice(i * CHUNK, (i + 1) * CHUNK)
                nc.gpsimd.tensor_tensor(w_parts[:, 1, cols], w13_space[:, cols], w_parts[:, 0, cols], ALU.subtract).then_inc(w_low, 1)

            split_low(0)
            tokenizer_power(z_ve, z_rstd, 0, 1)
            for i in range(1, W_COLUMNS // CHUNK):
                split_low(i)

            def power(g, k, src, dst, wait, done, images=(0, GB), part=0):
                pool.wait_ge(wait.sem, wait.at(g, part + 1))
                lo, hi = images
                done.by(nc.gpsimd.tensor_tensor(ln_small[0:N, k, dst, lo:hi], ln_small[0:N, k, src, lo:hi],
                                                minus_half[0:N, lo:hi], ALU.pow))

            def prepare_next(g):
                power(g, 0, 0, 1, ln["a"]["ve"], ln["a"]["rstd"])
                power(g, 0, 4, 5, a_v3, a_r2)

            def rotate(g, tiles_of_heads):
                for i in tiles_of_heads:
                    j, which = divmod(i, 2)
                    t, other = rotated[:, j % ROPES, which, :, :], product[:, i % 2, :, :]
                    pool.wait_ge(rope_mul.sem, rope_mul.at(g, 2 * i + 2))
                    rope_sum.by(nc.gpsimd.tensor_tensor(t[:, 0, :], t[:, 0, :], other[:, 0, :], ALU.subtract))
                    for half in range(2):
                        await_taken(pool, g, ("qk", i, half))
                    rope_sum.by(nc.gpsimd.tensor_tensor(t[:, 1, :], other[:, 1, :], t[:, 1, :], ALU.add))

            def body(g, prepare):
                for part in range(2):
                    power(g, 1, 0, 1, ln["f"]["ve"], ln["f"]["rstd"], (2 * part, 2 * part + 2), part)
                if prepare:
                    prepare_next(g)
                    rotate(g, range(2 * QUADS))
                pool.wait_ge(gate_step.sem, gate_step.at(g, gate_step.per_pass))
                pool.sem_inc(carrier, 1)
                for c in range(TOPK):
                    for b in range(GB):
                        scattered.by(pool.indirect_dma_start(xrows, bass.IndirectOffsetOnAxis(row_of[0:N, c, b:b + 1], 0),
                                                             rows[0:N, b, :], None), 16)
                pool.wait_ge(scattered.sem, scattered.at(g, scattered.per_pass))
                lists_done.given += 1
                pool.sem_inc(lists_done.sem, 1)

            prepare_next(-1)
            rotate(-1, range(2))
            tokenizer_power(z_ve, z_rstd, 1, 1)
            rotate(-1, range(2, 2 * QUADS))
            passes(pool, body)

            def step(at, turn, k):
                t = at(3)
                if live(t):
                    passed(pool, e_y_done, t)
                    passed(pool, e_id_done, t)
                    pool.sem_inc(carrier, 1)
                    j = (k - 3) % UNROLL
                    pool.indirect_dma_start(yrows, bass.IndirectOffsetOnAxis(e_id[:, j:j + 1], 0), e_y[:, j, :], None).then_inc(e_stored[j], 16)

            tiles(pool, step, 3)

        @block.scalar
        def _(act):
            act.dma_start(ident[:, :], a["ident"]).then_inc(ident_in, 16)
            act.dma_start(wp[:, :, :].rearrange("p (c k) e -> p c k e", c=C)[:, :, 0, :],
                          a["L0_tok_W_proj"].rearrange("(k q c) e -> q k c e", k=2, c=C)[:, 0, :, :]).then_inc(wp_in, 16)
            act.dma_start(wp[:, :, :].rearrange("p (c k) e -> p c k e", c=C)[:, :, 1, :],
                          a["L0_tok_W_proj"].rearrange("(k q c) e -> q k c e", k=2, c=C)[:, 1, :, :]).then_inc(wp_in, 16)
            for t, name in ((g1T, "L0_tok_ln1_g"), (b1T, "L0_tok_ln1_b")):
                for c in range(C):
                    act.dma_start(t[:, 2 * c:2 * c + 2], a[name].rearrange("(k q c) -> q c k", k=2, c=C)[:, c, :],
                                  allow_slow_non_contiguous=True).then_inc(tok_in, 16)
            for t, name in ((bproj, "L0_tok_b_proj"), (g2, "L0_tok_ln2_g"), (b2, "L0_tok_ln2_b")):
                act.dma_start(t, a[name].partition_broadcast(PR)).then_inc(tok_in, 16)
            act.wait_ge(tok_in, 16 * 9)
            for t in range(2 * SIDE):
                act.wait_ge(p_turned, t + 1)
                if t >= 2:
                    act.wait_ge(p_proj, t - 1)
                for m in range(PCH):
                    last = nc.scalar.activation(patchT[:, t % 2, m, :], ps[:, 2 * (t % 2) + m // 3, (m % 3) * PR:(m % 3 + 1) * PR],
                                                ACT.Identity, scale=g1T[:, m:m + 1], bias=b1T[:, m:m + 1])
                    last.then_inc(p_affine, 1)
                i = t - 3
                if 0 <= i < W_COLUMNS // CHUNK:
                    act.wait_ge(*((wqk_in, 16 * 8) if i * CHUNK < KD * 4 * HEADS * HALF else
                                  (wv_in, 16) if i * CHUNK < KD * 4 * HEADS * HALF + KD * HEADS * DH else (wout_in, 16)))
                    cols = slice(i * CHUNK, (i + 1) * CHUNK)
                    nc.scalar.activation(w13_space[:, cols], w13_space[:, cols], ACT.Copy, scale=W_SCALE).then_inc(w_scaled, 1)
                    act.wait_ge(w_scaled, i + 1)
                    nc.scalar.copy(w_parts[:, 0, cols], w13_space[:, cols]).then_inc(w_high, 1)
            act.wait_ge(tables_in, 16 * TABLES)

            def prepare_next(g):
                for kc in range(KD):
                    bank = await_full(act, g, ("xT", kc))
                    taken[bank].by(nc.scalar.activation(xT32[:, kc, :], ps[:, bank, 0:GT], ACT.Identity,
                                                        scale=lngT[:, kc:kc + 1], bias=lnbT[:, kc:kc + 1]))
                for kc in range(KD):
                    await_taken(act, g, ("xT", kc))
                    x_high.by(nc.scalar.copy(xT[:, 0, kc, :], xT32[:, kc, :]))
                take_v(g, (0, 1, 2))

            def take_v(g, images):
                for b in images:
                    for n in range(2):
                        bank = await_full(act, g, ("v", b, n))
                        taken[bank].by(nc.scalar.activation(vv[0:N, b, n * 512:(n + 1) * 512], ps[0:N, bank, :], ACT.Copy,
                                                            scale=V_SCALE / W_SCALE))

            def body(g, prepare):
                take_v(g, (3,))
                def softmax_exp(b):
                    for r in range(4):
                        await_taken(act, g, ("s", b, r))
                        p = prob[0:N, b % 2, r, :, :]
                        s_exp.by(nc.scalar.activation(p, p, ACT.Exp, scale=SCALE))

                def take_oT(b):
                    for c in range(2):
                        bank = await_full(act, g, ("oT", b, c))
                        o_high.by(nc.scalar.copy(oT[:, 0, 4 * c:4 * c + 4, :], ps[:, bank, 0:4 * N].rearrange("p (m t) -> p m t", m=4)))

                softmax_exp(0)
                for b in range(GB):
                    if b:
                        await_full(act, g, ("o", b - 1, 1))
                    for r in range(4):
                        bank = await_full(act, g, ("pT", b, r))
                        taken[bank].by(nc.scalar.copy(probT[0:N, r, :], ps[0:N, bank, 0:4 * N]))
                    if b:
                        take_oT(b - 1)
                    if b + 1 < GB:
                        softmax_exp(b + 1)
                take_oT(GB - 1)
                for kc in range(KD):
                    act.wait_ge(f_turned.sem, f_turned.at(g, kc + 1))
                    f_early.by(nc.scalar.copy(fT[:, kc, 0:GT // 2], ps[:, TURN[("fT", kc)][0], 0:GT // 2]))
                if not prepare:
                    for half, name in enumerate(("L0_ffn_be1", "L0_ffn_be3")):
                        act.dma_start(b13[:, :, half * INTER:(half + 1) * INTER], a[name].partition_broadcast(128)).then_inc(biases_in, 16)

                for kc in range(KD):
                    bank = await_full(act, g, ("fT", kc))
                    taken[bank].by(nc.scalar.copy(fT[:, kc, GT // 2:GT], ps[:, bank, GT // 2:GT]))

                def silu(q):
                    key = f"s{q}"
                    bias = bs1T[:, q:q + 1]
                    bank = await_full(act, g, (key, 1))
                    taken[bank].by(nc.scalar.activation(sil[:, q % 2, :], ps[:, bank, 0:GT], ACT.Silu, bias=bias))

                await_taken(act, g, ("gate",))
                gate_exp.by(nc.scalar.activation(gate[0:N, 1, :, :], gate[0:N, 0, :, :], ACT.Exp))
                for q in range(SHC):
                    silu(q)
                if prepare:
                    prepare_next(g)
                bank = await_full(act, g, ("cT",))
                taken[bank].by(nc.scalar.copy(cT, ps[0:E + 1, bank, 0:GT]))
                act.wait_ge(acc_half.sem, acc_half.at(g, 2 * 2))
                for p in range(2):
                    await_taken(act, g, ("y", "b", p))
                act.dma_start((hrows[bass.ds(g, 1), :, :, :] if prepare else hrows[g:g + 1, :, :, :]).rearrange("o n b d -> n (o b) d"),
                              h2[0:N, :, :]).then_inc(h_stored, 16)

            prepare_next(-1)
            act.wait_ge(z_out[1], 16)
            passes(act, body)

            pad_lists(act, 1)

            def step(at, turn, k):
                t = at(0)
                if live(t):
                    passed(act, e_turned, t)
                    passed(act, e_h_done, at(2))
                    nc.scalar.copy(e_xT[:, k % 2, :, :].rearrange("p c t -> p (c t)"), ps[:, k % 2, 0:KD * TS]).then_inc(e_xT_done, 1)
                t = at(1)
                if live(t):
                    j = (k - 1) % 2
                    passed(act, e_biased, t)
                    x = e_hb[:, j, 0:INTER]
                    nc.scalar.activation(x, x, ACT.Silu).then_inc(e_silu, 1)
                t = at(2)
                if live(t):
                    passed(act, e_hid_turned, t)
                    passed(act, e_y_full, at(4))
                    nc.scalar.copy(e_hidT[:, k % 2, :], ps[:, 4 + k % 2, 0:TS]).then_inc(e_hidT_done, 1)

            tiles(act, step, 2)

            for t in range(GROUPS):
                act.wait_ge(f_sum, t + 1)
                for lo, hi, t0 in ((0, NP, 1), (NP, NP + 1, 0), (NP + 1, N, NP + 1)):
                    act.dma_start(out[images(t), t0:t0 + hi - lo, :].rearrange("b n d -> n b d"),
                                  f_h[t][lo:hi, :, :]).then_inc(out_stored[t % PLACES], 16)

        @block.vector
        def _(dve):
            def patch_stats(half, columns):
                dve.wait_ge(img_in[half], 16 * HB)
                for w in columns:
                    for c in range(C):
                        nc.vector.bn_stats(tok_stats[:, 2 * half, w, 6 * c:6 * c + 6], img[half][:, c, :, w, :]).then_inc(p_stats, 1)

            def patch_variance(half):
                dve.wait_ge(p_stats, C * SIDE * (half + 1))
                for w in range(SIDE):
                    nc.vector.bn_aggr(tok_mv[:, 2 * half, w, :], tok_stats[:, 2 * half, w, :]).then_inc(p_mv, 1)
                dve.wait_ge(p_mv, SIDE * (half + 1))
                nc.vector.tensor_scalar(tok_small[:, 2 * half, 0, :], tok_mv[:, 2 * half, :, 1], EPS, None, ALU.add).then_inc(p_ve, 1)

            def patch_norm(t):
                half, w = divmod(t, SIDE)
                if t >= 2:
                    dve.wait_ge(p_turned, t - 1)
                nc.vector.tensor_scalar(patch[:, t % 2, :].rearrange("p (c a q) -> p c a q", c=C, a=PATCH), img[half][:, :, :, w, :],
                                        tok_mv[:, 2 * half, w, 0:1], tok_small[:, 2 * half, 1, w:w + 1],
                                        ALU.subtract, ALU.mult).then_inc(p_norm, 1)

            def token_stats(t):
                half, w = divmod(t, SIDE)
                dve.wait_ge(p_proj, t + 1)
                nc.vector.tensor_tensor(z[half][:, w, :], ps[0:PR, 4 + t % 2, 0:D], bproj, ALU.add).then_inc(z_bias, 1)
                dve.wait_ge(z_bias, t + 1)
                nc.vector.bn_stats(tok_stats[:, 2 * half + 1, w, 0:6], z[half][:, w, :]).then_inc(z_stats, 1)

            def token_variance(half):
                q = 2 * half + 1
                dve.wait_ge(z_stats, SIDE * (half + 1))
                for w in range(SIDE):
                    nc.vector.bn_aggr(tok_mv[:, q, w, :], tok_stats[:, q, w, 0:6]).then_inc(z_mv, 1)
                dve.wait_ge(z_mv, SIDE * (half + 1))
                nc.vector.tensor_scalar(tok_small[:, q, 0, :], tok_mv[:, q, :, 1], EPS, None, ALU.add).then_inc(z_ve, 1)

            def token_norm(half):
                q = 2 * half + 1
                dve.wait_ge(z_rstd, half + 1)
                for w in range(SIDE):
                    zz = z[half][:, w, :]
                    nc.vector.tensor_scalar(zz, zz, tok_mv[:, q, w, 0:1], tok_small[:, q, 1, w:w + 1], ALU.subtract, ALU.mult).then_inc(z_norm, 1)

            def token_gain(half):
                dve.wait_ge(z_norm, SIDE * (half + 1))
                zz = z[half][:, :, :]
                nc.vector.tensor_tensor(zz, zz, g2.unsqueeze(1).to_broadcast([PR, SIDE, D]), ALU.mult).then_inc(z_scaled, 1)

            def token_bias(half):
                dve.wait_ge(z_scaled, half + 1)
                zz = z[half][:, :, :]
                nc.vector.tensor_tensor(zz, zz, b2.unsqueeze(1).to_broadcast([PR, SIDE, D]), ALU.add).then_inc(z_done, 1)

            dve.wait_ge(tok_in, 16 * 9)
            patch_stats(0, range(SIDE))
            patch_variance(0)
            beside = {1: lambda: patch_stats(1, range(0, 2)), 2: lambda: patch_stats(1, range(2, 4)),
                      3: lambda: patch_stats(1, range(4, 5)), 4: lambda: (patch_stats(1, range(5, 6)), patch_variance(1)),
                      6: lambda: token_variance(0), 7: lambda: token_norm(0), 8: lambda: token_gain(0), 9: lambda: token_bias(0)}
            dve.wait_ge(p_rstd, 1)
            patch_norm(0)
            for t in range(2 * SIDE):
                if t + 1 == SIDE:
                    dve.wait_ge(p_rstd, 2)
                if t + 1 < 2 * SIDE:
                    patch_norm(t + 1)
                if t:
                    token_stats(t - 1)
                if t in beside:
                    beside[t]()
            token_stats(2 * SIDE - 1)

            dve.wait_ge(tables_in, 16 * TABLES)
            dve.wait_ge(consts, 2)

            def prepare_sums(g):
                dve.wait_ge(h_in, g * 48 + 96)
                h_ready.by(nc.vector.tensor_tensor(h[0:NP + 1, :, :], h[0:NP + 1, :, :],
                                                   pos[:, :].unsqueeze(1).to_broadcast([NP + 1, GB, D]), ALU.add))
                dve.wait_ge(h_ready.sem, h_ready.at(g, 1))
                s = ln["a"]
                for b in range(GB):
                    s["stats"].by(nc.vector.bn_stats(ln_stats[0:N, 0, b, :], h[0:N, b, :]))
                dve.wait_ge(s["stats"].sem, s["stats"].at(g, GB))
                nc.vector.memset(wait_carrier[:, :], 0.0)
                for b in range(GB):
                    s["mv"].by(nc.vector.bn_aggr(ln_mv[0:N, 0, b, :], ln_stats[0:N, 0, b, :]))
                dve.wait_ge(s["mv"].sem, s["mv"].at(g, GB))
                s["ve"].by(nc.vector.tensor_scalar(ln_small[0:N, 0, 0, :], ln_mv[0:N, 0, :, 1], EPS, None, ALU.add))

            def prepare_second(g):
                sm = ln_small[0:N, 0, :, :]
                dve.wait_ge(ln["a"]["rstd"].sem, ln["a"]["rstd"].at(g, 1))
                a_v1.by(nc.vector.tensor_tensor(sm[:, 2, :], ln_mv[0:N, 0, :, 1], sm[:, 1, :], ALU.mult))
                dve.wait_ge(a_v1.sem, a_v1.at(g, 1))
                a_v2.by(nc.vector.tensor_tensor(sm[:, 3, :], sm[:, 2, :], sm[:, 1, :], ALU.mult))
                dve.wait_ge(a_v2.sem, a_v2.at(g, 1))
                a_v3.by(nc.vector.tensor_scalar(sm[:, 4, :], sm[:, 3, :], EPS, None, ALU.add))

            def prepare_norm(g):
                sm = ln_small[0:N, 0, :, :]
                dve.wait_ge(a_r2.sem, a_r2.at(g, 1))
                a_r12.by(nc.vector.tensor_tensor(sm[:, 6, :], sm[:, 1, :], sm[:, 5, :], ALU.mult))
                dve.wait_ge(a_r12.sem, a_r12.at(g, 1))
                for b in range(GB):
                    ln["a"]["norm"].by(nc.vector.tensor_scalar(xn[0:N, b, :], h[0:N, b, :], ln_mv[0:N, 0, b, 0:1], sm[:, 6, b:b + 1],
                                                               ALU.subtract, ALU.mult))

            cos = cosT[:, :].unsqueeze(1).to_broadcast([128, GB, N])
            sin = sinT[:, :].unsqueeze(1).to_broadcast([128, GB, N])

            def by_image(ap):
                return ap.rearrange("p (b t) -> p b t", b=GB)

            def split_tokens(g):
                for kc in range(KD):
                    dve.wait_ge(x_high.sem, x_high.at(g, kc + 1))
                    x_low.by(nc.vector.tensor_tensor(xT[:, 1, kc, :], xT32[:, kc, :], xT[:, 0, kc, :], ALU.subtract))

            def rotate(g, tiles_of_heads):
                for i in tiles_of_heads:
                    j, which = divmod(i, 2)
                    moved = restacked[j % ROPES]
                    if not (isinstance(g, int) and j < ROPES):
                        dve.wait_ge(moved.sem, moved.at(g, 8 * 16 * (j // ROPES)))
                    if not (isinstance(g, int) and i < 2):
                        dve.wait_ge(rope_sum.sem, rope_sum.at(g, 2 * (i - 2) + 2))
                    for half, (first, second) in enumerate(((cos, sin), (sin, cos))):
                        bank = await_full(dve, g, ("qk", i, half))
                        x = by_image(ps[:, bank, 0:GT])
                        t = product[:, i % 2, :, :] if half else rotated[:, j % ROPES, which, :, :]
                        rope_mul.by(nc.vector.tensor_tensor(by_image(t[:, 0, :]), x, first, ALU.mult))
                        taken[bank].by(nc.vector.tensor_tensor(by_image(t[:, 1, :]), x, second, ALU.mult))

            def body(g, prepare):
                def own(s, n):
                    dve.wait_ge(s.sem, s.at(g, n))

                def centre(b):
                    for r in range(4):
                        bank = await_full(dve, g, ("s", b, r))
                        s_max.by(nc.vector.tensor_reduce(smax[0:N, b % 2, r, :], ps[0:N, bank, 0:4 * N].rearrange("p (j t) -> p j t", j=4),
                                                         AX.X, ALU.max))
                    for r in range(4):
                        own(s_max, 4 * b + r + 1)
                        bank = TURN[("s", b, r)][0]
                        taken[bank].by(nc.vector.tensor_tensor(
                            prob[0:N, b % 2, r, :, :], ps[0:N, bank, 0:4 * N].rearrange("p (j t) -> p j t", j=4),
                            smax[0:N, b % 2, r, :].unsqueeze(2).to_broadcast([N, 4, N]), ALU.subtract))

                def token_stats(b):
                    await_taken(dve, g, ("wo", b))
                    ln["f"]["stats"].by(nc.vector.bn_stats(ln_stats[0:N, 1, b, :], h2[0:N, b, :]))

                def token_variance(part):
                    own(ln["f"]["stats"], 2 * part + 2)
                    nc.vector.memset(wait_carrier[:, :], 0.0)
                    for b in (2 * part, 2 * part + 1):
                        ln["f"]["mv"].by(nc.vector.bn_aggr(ln_mv[0:N, 1, b, :], ln_stats[0:N, 1, b, :]))
                    own(ln["f"]["mv"], 2 * part + 2)
                    both = slice(2 * part, 2 * part + 2)
                    ln["f"]["ve"].by(nc.vector.tensor_scalar(ln_small[0:N, 1, 0, both], ln_mv[0:N, 1, both, 1], EPS, None, ALU.add))

                def token_norm(part):
                    dve.wait_ge(ln["f"]["rstd"].sem, ln["f"]["rstd"].at(g, part + 1))
                    for b in (2 * part, 2 * part + 1):
                        ln["f"]["norm"].by(nc.vector.tensor_scalar(rows[0:N, b, 0:D], h2[0:N, b, :], ln_mv[0:N, 1, b, 0:1],
                                                                   ln_small[0:N, 1, 1, b:b + 1], ALU.subtract, ALU.mult))

                def split_heads(b):
                    for c in range(2):
                        dve.wait_ge(o_high.sem, o_high.at(g, 2 * b + c + 1))
                        bank = await_full(dve, g, ("oT", b, c))
                        taken[bank].by(nc.vector.tensor_tensor(oT[:, 1, 4 * c:4 * c + 4, :], ps[:, bank, 0:4 * N].rearrange("p (m t) -> p m t", m=4),
                                                               oT[:, 0, 4 * c:4 * c + 4, :], ALU.subtract))

                def add_attention(b):
                    bank = await_full(dve, g, ("wo", b))
                    taken[bank].by(nc.vector.scalar_tensor_tensor(h2[0:N, b, :], ps[0:N, bank, 0:D], 1.0 / (W_SCALE * V_SCALE),
                                                                  h[0:N, b, :], ALU.mult, ALU.add))

                dve.wait_ge(h_stored, g * 16 + 16)
                centre(0)
                for b in range(GB):
                    if b == 0:
                        dve.wait_ge(lists_done.sem, lists_done.at(g, 0))
                    if b + 1 < GB:
                        centre(b + 1)
                    dve.wait_ge(s_exp.sem, s_exp.at(g, 4 * b + 4))
                    s_sum.by(nc.vector.tensor_reduce(ssum[0:N, b % 2, :, :], prob[0:N, b % 2, :, :, :], AX.X, ALU.add))
                    own(s_sum, b + 1)
                    s_rec.by(nc.vector.reciprocal(srec[0:N, b % 2, :, :], ssum[0:N, b % 2, :, :]))
                    own(s_rec, b + 1)
                    if b:
                        split_heads(b - 1)
                    for c in range(2):
                        bank = await_full(dve, g, ("o", b, c))
                        inv = srec[0:N, b % 2, :, 2 * c:2 * c + 2].rearrange("p r j -> p j r").unsqueeze(3).to_broadcast([N, 2, 4, DH])
                        taken[bank].by(nc.vector.tensor_tensor(
                            o[0:N, c * 512:(c + 1) * 512].rearrange("p (j r d) -> p j r d", j=2, r=4),
                            ps[0:N, bank, :].rearrange("p (j r d) -> p j r d", j=2, r=4), inv, ALU.mult))
                    if b:
                        add_attention(b - 1)
                        token_stats(b - 1)
                    if b == 2:
                        token_variance(0)
                nc.vector.memset(rows[:, :, ONE:ONE + 1], 1.0)
                token_norm(0)
                split_heads(GB - 1)
                add_attention(GB - 1)
                token_stats(GB - 1)
                token_variance(1)
                token_norm(1)

                def gated(q):
                    key = f"s{q}"
                    bias, dst = bs3T[:, q:q + 1], shid[:, q, :]
                    await_taken(dve, g, (key, 1))
                    bank = await_full(dve, g, (key, 3))
                    taken[bank].by(nc.vector.scalar_tensor_tensor(dst, ps[:, bank, 0:GT], bias, sil[:, q % 2, :], ALU.add, ALU.mult))

                summed = []

                def add_out(e):
                    for p in range(2):
                        bank = await_full(dve, g, ("y", e, p))
                        for bb in range(2):
                            b = 2 * p + bb
                            if summed:
                                own(acc_half, 2 * (len(summed) - 1) + p + 1) if bb == 0 else await_taken(dve, g, ("y", summed[-1], p))
                            src = ps[0:N, bank, bb * D:(bb + 1) * D]
                            ins = nc.vector.tensor_tensor(h2[0:N, b, :], src, h2[0:N, b, :], ALU.add)
                            (taken[bank] if bb else acc_half).by(ins)
                    summed.append(e)

                steps = [0]

                def step(ins):
                    gate_step.by(ins)
                    steps[0] += 1
                    own(gate_step, steps[0])

                def beats(dst, tmp, x, n):
                    other = x.unsqueeze(2).to_broadcast([N, GB, n, n])
                    own_x = x.unsqueeze(3).to_broadcast([N, GB, n, n])
                    low = tri[0:N, 0:n, 0:n].unsqueeze(1).to_broadcast([N, GB, n, n])
                    step(nc.vector.tensor_tensor(dst, other, own_x, ALU.is_equal))
                    step(nc.vector.tensor_tensor(dst, dst, low, ALU.mult))
                    step(nc.vector.tensor_tensor(tmp, other, own_x, ALU.is_gt))
                    step(nc.vector.tensor_tensor(dst, dst, tmp, ALU.add))

                G = [gate[0:N, i, :, :] for i in range(8)]
                S = [few[0:N, i, :, :] for i in range(8)]
                mx, sm, rs = S[0][:, :, 0], S[0][:, :, 1], S[0][:, :, 2]
                prob_e, biased = G[2], G[3]

                def over(x, n):
                    return x.unsqueeze(2).to_broadcast([N, GB, n])

                def centre_logits():
                    bank = await_full(dve, g, ("gate",))
                    logits = ps[0:N, bank, 0:GB * E].rearrange("p (b e) -> p b e", b=GB)
                    step(nc.vector.tensor_reduce(mx, logits, AX.X, ALU.max))
                    taken[bank].by(nc.vector.tensor_tensor(G[0], logits, over(mx, E), ALU.subtract))

                def choose_groups():
                    dve.wait_ge(gate_exp.sem, gate_exp.at(g, 1))
                    step(nc.vector.tensor_reduce(sm, G[1], AX.X, ALU.add))
                    step(nc.vector.reciprocal(rs, sm))
                    step(nc.vector.tensor_tensor(prob_e, G[1], over(rs, E), ALU.mult))
                    step(nc.vector.tensor_tensor(biased, prob_e, gateb[0:N, :].unsqueeze(1).to_broadcast([N, GB, E]), ALU.add))
                    quad = biased.rearrange("p b (g h i) -> p (b g) h i", g=G4, h=2)
                    hi = G[4].rearrange("p b (x i) -> p (b x) i", i=2)[:, 0:GB * G4, :]
                    lo = G[5].rearrange("p b (x i) -> p (b x) i", i=2)[:, 0:GB * G4, :]
                    first, second = (S[i].rearrange("p b g -> p (b g)") for i in (1, 2))
                    tmp = S[3].rearrange("p b g -> p (b g)")
                    step(nc.vector.tensor_tensor(hi, quad[:, :, 0, :], quad[:, :, 1, :], ALU.max))
                    step(nc.vector.tensor_tensor(lo, quad[:, :, 0, :], quad[:, :, 1, :], ALU.min))
                    step(nc.vector.tensor_tensor(first, hi[:, :, 0], hi[:, :, 1], ALU.max))
                    step(nc.vector.tensor_tensor(second, hi[:, :, 0], hi[:, :, 1], ALU.min))
                    step(nc.vector.tensor_tensor(tmp, lo[:, :, 0], lo[:, :, 1], ALU.max))
                    step(nc.vector.tensor_tensor(second, second, tmp, ALU.max))
                    step(nc.vector.tensor_tensor(S[4], S[1], S[2], ALU.add))
                    small = [pairs[0:N, i, :, :, :] for i in range(2)]
                    beats(small[0], small[1], S[4], G4)
                    step(nc.vector.tensor_reduce(S[5], small[0], AX.X, ALU.add))
                    step(nc.vector.tensor_scalar(S[6], S[5], 2.0, None, ALU.is_lt))
                    step(nc.vector.tensor_scalar(S[7], S[6], 1.0, FAR, ALU.subtract, ALU.mult))
                    def spread(x):
                        return x.unsqueeze(3).to_broadcast([N, GB, G4, EPG])

                    def grouped(x):
                        return x.rearrange("p b (g i) -> p b g i", g=G4)

                    step(nc.vector.tensor_tensor(grouped(G[4]), grouped(biased), spread(S[6]), ALU.mult))
                    step(nc.vector.tensor_tensor(grouped(G[4]), grouped(G[4]), spread(S[7]), ALU.add))

                def choose_experts():
                    first_of = counts[0:N, COUNT_DOWN:COUNT_DOWN + E].unsqueeze(1).to_broadcast([N, GB, E])
                    for n in range(TOPK):
                        step(nc.vector.tensor_reduce(mx, G[4], AX.X, ALU.max))
                        step(nc.vector.tensor_tensor(G[5], G[4], over(mx, E), ALU.is_equal))
                        step(nc.vector.tensor_tensor(G[5], G[5], first_of, ALU.mult))
                        step(nc.vector.tensor_reduce(sm, G[5], AX.X, ALU.max))
                        step(nc.vector.tensor_tensor(G[6 + n], first_of, over(sm, E), ALU.is_equal))
                        if n == 0:
                            step(nc.vector.scalar_tensor_tensor(G[4], G[6], -FAR, G[4], ALU.mult, ALU.add))
                    step(nc.vector.tensor_tensor(chosen[0:N, :, :], G[6], G[7], ALU.add))
                    assert steps[0] == CHOSEN_STEP, steps
                    step(nc.vector.tensor_tensor(cw[0:N, :, 0:E], chosen[0:N, :, :], prob_e, ALU.mult))

                def list_rows():
                    bank = await_full(dve, g, ("rank",))
                    rank = ps[0:N, bank, 0:GB * E].rearrange("p (b e) -> p b e", b=GB)
                    place = G[1]
                    step(nc.vector.tensor_tensor(place, rank, next_row[0:N, :].unsqueeze(1).to_broadcast([N, GB, E]), ALU.add))
                    step(nc.vector.tensor_tensor(gate[0:N, 4:6, :, :], gate[0:N, 6:8, :, :],
                                                 place.unsqueeze(1).to_broadcast([N, TOPK, GB, E]), ALU.mult))
                    step(nc.vector.tensor_reduce(row_f[0:N, :, :], gate[0:N, 4:6, :, :], AX.X, ALU.add))
                    step(nc.vector.tensor_scalar(row_of[0:N, :, :], row_f[0:N, :, :], 1.0, None, ALU.subtract))
                    step(nc.vector.tensor_tensor(rows[0:N, :, IDS:ROW], G[6], over(number[0:N, 0:GB], E), ALU.add))
                    taken[bank].by(nc.vector.tensor_tensor(next_row[:, :], next_row[:, :], ps[:, bank, GB * E:(GB + 1) * E], ALU.add))
                    await_taken(dve, g, ("rank",))
                    step(nc.vector.tensor_scalar(number[0:N, 0:GB], number[0:N, 0:GB], float(TOPK * GT), None, ALU.add))
                    assert steps[0] == gate_step.per_pass, steps

                centre_logits()
                if prepare:
                    prepare_sums(g)
                gated(0)
                if prepare:
                    prepare_second(g)
                gated(1)
                if prepare:
                    prepare_norm(g)
                if prepare:
                    split_tokens(g)
                if prepare:
                    rotate(g, range(1))
                add_out("s")
                if prepare:
                    rotate(g, range(1, QUADS))
                choose_groups()
                if prepare:
                    rotate(g, range(QUADS, 2 * QUADS))
                choose_experts()
                list_rows()
                add_out("b")

            prepare_sums(-1)
            prepare_second(-1)
            prepare_norm(-1)
            split_tokens(-1)
            rotate(-1, range(2))
            token_variance(1)
            token_norm(1)
            token_gain(1)
            token_bias(1)
            dve.wait_ge(z_done, 2)
            rotate(-1, range(2, 2 * QUADS))
            passes(dve, body)

            steps = [0]

            def step(ins):
                ins.then_inc(tables_step, 1)
                steps[0] += 1
                dve.wait_ge(tables_step, steps[0])

            def table(first, n):
                return counts[:, first:first + n]

            length, n_tiles, first_tile = (t_e[:, i, :] for i in range(3))
            expert, row, lists_first, list_length, within = (t_tile[:, i:i + 1] for i in range(5))
            tile_no = number[:, GB + 1:GB + 2]
            FULL = COUNTS - COUNT_FULL
            step(nc.vector.memset(pad_rows[:, 0:IDS], 0.0))
            step(nc.vector.tensor_copy(pad_rows[:, IDS:ROW], number[:, GB:GB + 1].to_broadcast([128, E])))
            step(nc.vector.tensor_scalar(pad_row[:, :], next_row[0:1, :], 1.0, None, ALU.subtract))
            assert steps[0] == PAD_STEPS, steps
            step(nc.vector.tensor_tensor(length, next_row[:, :], table(COUNT_BASE, E), ALU.subtract))
            begun = t_cmp.rearrange("p (e n) -> p e n", e=E)
            step(nc.vector.tensor_tensor(begun, length.unsqueeze(2).to_broadcast([128, E, FULL]),
                                         table(COUNT_FULL, FULL).unsqueeze(1).to_broadcast([128, E, FULL]), ALU.is_gt))
            step(nc.vector.tensor_reduce(n_tiles, begun, AX.X, ALU.add))
            lower = t_cmp[:, 0:E * E].rearrange("p (e n) -> p e n", e=E)
            step(nc.vector.tensor_tensor(lower, n_tiles.unsqueeze(1).to_broadcast([128, E, E]), tri[:, :, :], ALU.mult))
            step(nc.vector.tensor_reduce(first_tile, lower, AX.X, ALU.add))
            begun = t_cmp[:, 0:E - 1]
            step(nc.vector.tensor_scalar(begun, first_tile[:, 1:E], tile_no, None, ALU.is_le))
            step(nc.vector.tensor_reduce(expert, begun, AX.X, ALU.add))
            step(nc.vector.tensor_tensor(begun, begun, first_tile[:, 1:E], ALU.mult))
            step(nc.vector.tensor_reduce(lists_first, begun, AX.X, ALU.max))
            own_list = t_cmp[:, 0:E]
            step(nc.vector.tensor_scalar(own_list, table(COUNT_EXPERT, E), expert, None, ALU.is_equal))
            step(nc.vector.tensor_tensor(own_list, own_list, length, ALU.mult))
            step(nc.vector.tensor_reduce(list_length, own_list, AX.X, ALU.add))
            step(nc.vector.tensor_tensor(within, tile_no, lists_first, ALU.subtract))
            step(nc.vector.scalar_tensor_tensor(within, within, float(TS), list_length, ALU.mult, ALU.min))
            step(nc.vector.scalar_tensor_tensor(row, expert, float(CAP), within, ALU.mult, ALU.add))
            assert steps[0] == TILE_STEPS, steps
            padded = t_small[:, 0, :]
            packed = t_small[:, 1, 0:TILES // UNROLL + 1]
            step(nc.vector.memset(padded, 0.0))
            dve.wait_ge(tables_turned, 1)
            step(nc.vector.tensor_copy(tile_row[:, :], ps[0:1, 0, 128:128 + TILES]))
            step(nc.vector.tensor_copy(padded[:, BEHIND:BEHIND + TILES], ps[0:1, 0, 0:TILES]))
            for j in range(WINDOW):
                part = padded[:, j:j + (TILES // UNROLL) * UNROLL + 1:UNROLL]
                if j == 0:
                    step(nc.vector.tensor_copy(packed, part))
                else:
                    step(nc.vector.scalar_tensor_tensor(packed, part, float(E ** j), packed, ALU.mult, ALU.add))
            step(nc.vector.tensor_copy(windows[:, :], packed))
            assert steps[0] == TABLE_STEPS, steps

            dve.wait_ge(biases_in, 16 * 2)
            window = [None]

            def step(at, turn, k):
                t0, t1, t2, t3 = (at(n) for n in range(4))
                if k == 0:
                    window[0] = experts_around(dve, at)
                if live(t1):
                    e1 = expert_at(dve, window[0], k, 1)
                if live(t2):
                    j = (k - 2) % 2
                    passed(dve, e_silu, t2)
                    passed(dve, e_hid_turned, at(4))
                    nc.vector.tensor_tensor(e_hid[:, j, :], e_hb[:, j, 0:INTER], e_hb[:, j, INTER:2 * INTER], ALU.mult).then_inc(e_hid_done, 1)
                if live(t1):
                    j = (k - 1) % UNROLL
                    moved_tile(dve, e_rows_in, j, turn(1))
                    passed(dve, e_y_done, at(1 + UNROLL))
                    passed(dve, e_id_done, at(1 + UNROLL))
                    nc.vector.tensor_scalar(e_wid[:, j, 0:1], e_rows[:, j, D:D + E][:, bass.ds(e1, 1)], 1.0, None, ALU.mult)
                    nc.vector.tensor_scalar(e_wid[:, j, 1:2], e_rows[:, j, IDS:ROW][:, bass.ds(e1, 1)], 1.0, None, ALU.mult).then_inc(e_wid_done, 1)
                if live(t1):
                    j = (k - 1) % 2
                    passed(dve, e_h_done, t1)
                    passed(dve, e_hid_done, at(3))
                    nc.vector.tensor_tensor(e_hb[:, j, :], ps[:, 2 + j, 0:2 * INTER],
                                            b13[:, bass.ds(e1, 1), :].rearrange("p o n -> p (o n)"), ALU.add).then_inc(e_biased, 1)
                if live(t3):
                    j = (k - 3) % UNROLL
                    moved_tile(dve, e_stored, j, turn(3 + UNROLL))
                    passed(dve, e_wid_done, t3)
                    trash = counts[:, COUNT_TRASH:COUNT_TRASH + TILES][:, t3:t3 + 1] if isinstance(t3, int) else \
                        counts[:, COUNT_TRASH:COUNT_TRASH + TILES][:, bass.ds(t3, 1)]
                    nc.vector.scalar_tensor_tensor(e_trash[:, j:j + 1], e_wid[:, j, 1:2], float(TRASH), trash, ALU.is_ge, ALU.mult).then_inc(e_trash_done, 1)
                    passed(dve, e_trash_done, t3)
                    nc.vector.tensor_tensor(e_id[:, j:j + 1], e_wid[:, j, 1:2], e_trash[:, j:j + 1], ALU.add).then_inc(e_id_done, 1)
                    passed(dve, e_y_full, t3)
                    nc.vector.tensor_scalar(e_y[:, j, :], ps[:, 6 + j % 2, 0:D], e_wid[:, j, 0:1], None, ALU.mult).then_inc(e_y_done, 1)

            tiles(dve, step, 3)

            dve.wait_ge(f_sums_in, 16 * GROUPS)
            for t in range(GROUPS):
                k = t % PLACES
                dve.wait_ge(f_in[k], 16 * (t // PLACES + 1))
                sums = f_h[t][0:N, :, :]
                nc.vector.tensor_tensor(sums, sums, f_y[k][0:N, :, 0, :], ALU.add).then_inc(f_half, 1)
                dve.wait_ge(f_half, t + 1)
                nc.vector.tensor_tensor(sums, sums, f_y[k][0:N, :, 1, :], ALU.add).then_inc(f_sum, 1)

        @block.tensor
        def _(pe):
            pe.wait_ge(ident_in, 16)
            def turn(t):
                pe.wait_ge(p_norm, t + 1)
                if t >= 2:
                    pe.wait_ge(p_affine, PCH * (t - 1))
                for m in range(PCH):
                    last = nc.tensor.transpose(ps[:, 2 * (t % 2) + m // 3, (m % 3) * PR:(m % 3 + 1) * PR],
                                               patch[:, t % 2, m * 128:(m + 1) * 128], ident[0:PR, 0:PR])
                last.then_inc(p_turned, 1)

            def project(t):
                pe.wait_ge(p_affine, PCH * (t + 1))
                if t >= 2:
                    pe.wait_ge(z_bias, t - 1)
                for m in range(PCH):
                    last = nc.tensor.matmul(ps[0:PR, 4 + t % 2, 0:D], patchT[:, t % 2, m, :], wp[:, m, :],
                                            start=(m == 0), stop=(m == PCH - 1))
                last.then_inc(p_proj, 1)

            turn(0)
            pe.wait_ge(wp_in, 16 * 2)
            for t in range(2 * SIDE):
                if t + 1 < 2 * SIDE:
                    turn(t + 1)
                project(t)
            def turn_tokens(g, key, x, s, images=range(GB)):
                pe.wait_ge(s.sem, s.at(g, images[-1] + 1))
                for kc in range(KD):
                    bank = TURN[(key, kc)][0] if images[0] else claim(g, (key, kc))
                    for b in images:
                        last = nc.tensor.transpose(ps[:, bank, b * N:(b + 1) * N], x[0:N, b, kc * 128:(kc + 1) * 128], ident[0:N, 0:N])
                    if images[-1] == GB - 1:
                        full[bank].by(last)
                    else:
                        f_turned.by(last)

            def project_qk(g):
                for kc in range(KD):
                    await_taken(pe, g, ("xT", kc))
                pe.wait_ge(x_low.sem, x_low.at(g, KD))
                for i in range(2 * QUADS):
                    j, which = divmod(i, 2)
                    for half in range(2):
                        bank = claim(g, ("qk", i, half))
                        for kc in range(KD):
                            for wp, xp in SPLIT:
                                last = nc.tensor.matmul(ps[:, bank, 0:GT], wqk[:, wp, kc, which, half, j * 128:(j + 1) * 128], xT[:, xp, kc, :],
                                                        start=(kc == 0 and (wp, xp) == SPLIT[0]), stop=(kc == KD - 1 and (wp, xp) == SPLIT[-1]))
                        full[bank].by(last)

            def project_v(g, images):
                for b in images:
                    for n in range(2):
                        bank = claim(g, ("v", b, n))
                        for kc in range(KD):
                            for wp, xp in SPLIT:
                                last = nc.tensor.matmul(ps[0:N, bank, :], xT[:, xp, kc, b * N:(b + 1) * N], wv[:, wp, kc, n * 512:(n + 1) * 512],
                                                        start=(kc == 0 and (wp, xp) == SPLIT[0]), stop=(kc == KD - 1 and (wp, xp) == SPLIT[-1]))
                        full[bank].by(last)

            turn_tokens(-1, "xT", xn, ln["a"]["norm"])
            pe.wait_ge(w_low, W_COLUMNS // CHUNK)
            project_qk(-1)
            project_v(-1, (0, 1, 2))

            def body(g, prepare):
                def scores(b):
                    cols = slice(b * N, (b + 1) * N)
                    for r in range(4):
                        claim(g, ("s", b, r))
                    for j in range(QUADS):
                        for r in range(4):
                            rows = slice(DH * (r % 2), DH * (r % 2 + 1))
                            last = nc.tensor.matmul(ps[0:N, r, j * N:(j + 1) * N], qkr[rows, 0, 2 * j + r // 2, cols],
                                                    qkr[rows, 1, 2 * j + r // 2, cols], start=True, stop=True)
                            if j == QUADS - 1:
                                full[r].by(last)

                def turn_probs(b):
                    for r in range(4):
                        pe.wait_ge(s_exp.sem, s_exp.at(g, 4 * b + r + 1))
                        bank = claim(g, ("pT", b, r))
                        for j in range(QUADS):
                            last = nc.tensor.transpose(ps[0:N, bank, j * N:(j + 1) * N], prob[0:N, b % 2, r, j, :], ident[0:N, 0:N])
                        full[bank].by(last)

                def attend(b):
                    for r in range(4):
                        await_taken(pe, g, ("pT", b, r))
                    for c in range(2):
                        bank = claim(g, ("o", b, c))
                        for i in range(8):
                            head = 8 * c + i
                            j, r = divmod(head, 4)
                            last = nc.tensor.matmul(ps[0:N, bank, i * DH:(i + 1) * DH], probT[0:N, r, j * N:(j + 1) * N],
                                                    vv[0:N, b, head * DH:(head + 1) * DH], start=True, stop=True)
                        full[bank].by(last)

                def turn_heads(b):
                    for c in range(2):
                        await_taken(pe, g, ("o", b, c))
                    for c in range(2):
                        bank = claim(g, ("oT", b, c))
                        for m in range(4):
                            chunk = 4 * c + m
                            last = nc.tensor.transpose(ps[:, bank, m * N:(m + 1) * N], o[0:N, chunk * 128:(chunk + 1) * 128], ident[0:N, 0:N])
                        full[bank].by(last)

                def project_heads(b):
                    for c in range(2):
                        await_taken(pe, g, ("oT", b, c))
                    bank = claim(g, ("wo", b))
                    for c in range(OC):
                        for wp, xp in SPLIT:
                            last = nc.tensor.matmul(ps[0:N, bank, 0:D], oT[:, xp, c, :], wout[:, wp, c, :],
                                                    start=(c == 0 and (wp, xp) == SPLIT[0]), stop=(c == OC - 1 and (wp, xp) == SPLIT[-1]))
                    full[bank].by(last)

                for moved in restacked:
                    pe.wait_ge(moved.sem, moved.at(g, 0))
                scores(0)
                project_v(g, (3,))
                for b in range(GB):
                    if b == 0:
                        for bb in range(GB):
                            for n in range(2):
                                await_taken(pe, g if bb == 3 else g - 1, ("v", bb, n))
                    if b + 1 < GB:
                        scores(b + 1)
                    turn_probs(b)
                    if b:
                        turn_heads(b - 1)
                    attend(b)
                    if b:
                        project_heads(b - 1)
                def hidden(q, part):
                    cols = slice(part * GT // 2, (part + 1) * GT // 2)
                    for n, ws in ((1, ws1), (3, ws3)):
                        key = (f"s{q}", n)
                        bank = TURN[key][0] if part else claim(g, key)
                        for kc in range(KD):
                            last = nc.tensor.matmul(ps[:, bank, cols], ws[:, kc, q * 128:(q + 1) * 128], fT[:, kc, cols],
                                                    start=(kc == 0), stop=(kc == KD - 1))
                        if part:
                            full[bank].by(last)

                turn_heads(GB - 1)
                turn_tokens(g, "fT", rows, ln["f"]["norm"], (0, 1))
                project_heads(GB - 1)
                pe.wait_ge(shared_in, 16 * 3)
                pe.wait_ge(f_early.sem, f_early.at(g, KD))
                for q in range(SHC):
                    hidden(q, 0)
                turn_tokens(g, "fT", rows, ln["f"]["norm"], (2, 3))
                for kc in range(KD):
                    await_taken(pe, g, ("fT", kc))
                bank = claim(g, ("gate",))
                for b in range(GB):
                    for kc in range(KD):
                        last = nc.tensor.matmul(ps[0:N, bank, b * E:(b + 1) * E], fT[:, kc, b * N:(b + 1) * N], gwT[:, kc, :],
                                                start=(kc == 0), stop=(kc == KD - 1))
                full[bank].by(last)

                def out_rows(key, lhs, rhs):
                    for p in range(2):
                        bank = claim(g, ("y", key, p))
                        for bb in range(2):
                            b = 2 * p + bb
                            for c in range(len(lhs)):
                                last = nc.tensor.matmul(ps[0:N, bank, bb * D:(bb + 1) * D], lhs[c][:, b * N:(b + 1) * N], rhs[c],
                                                        start=(c == 0), stop=(c == len(lhs) - 1))
                        full[bank].by(last)

                for q in range(SHC):
                    hidden(q, 1)
                for q in range(SHC):
                    await_taken(pe, g, (f"s{q}", 3))
                if prepare:
                    turn_tokens(g, "xT", xn, ln["a"]["norm"])
                out_rows("s", [shid[:, c, :] for c in range(SHC)], [ws2[:, c, :] for c in range(SHC)])
                if prepare:
                    project_qk(g)
                    project_v(g, (0, 1, 2))
                pe.wait_ge(gate_step.sem, gate_step.at(g, CHOSEN_STEP + 1))
                bank = claim(g, ("cT",))
                for b in range(GB):
                    last = nc.tensor.transpose(ps[0:E + 1, bank, b * N:(b + 1) * N], cw[0:N, b, :], ident[0:N, 0:N])
                full[bank].by(last)
                bank = claim(g, ("rank",))
                for b in range(GB):
                    for bb in range(b + 1):
                        nc.tensor.matmul(ps[0:N, bank, b * E:(b + 1) * E], before[:, :] if bb == b else ones[0:N, 0:N],
                                         chosen[0:N, bb, :], start=(bb == 0), stop=(bb == b))
                for b in range(GB):
                    last = nc.tensor.matmul(ps[:, bank, GB * E:(GB + 1) * E], ones[0:N, :], chosen[0:N, b, :],
                                            start=(b == 0), stop=(b == GB - 1))
                full[bank].by(last)
                await_taken(pe, g, ("cT",))
                out_rows("b", [cT], [be2s[:, :]])

            passes(pe, body)

            for key in [("rank",), ("cT",), ("y", "b", 0), ("y", "b", 1), ("s0", 1), ("s0", 3), ("s1", 1), ("s1", 3)]:
                await_taken(pe, GROUPS - 1, key)
            pe.wait_ge(tables_step, TILE_STEPS)
            for i in range(2):
                last = nc.tensor.transpose(ps[0:1, 0, i * 128:(i + 1) * 128], t_tile[:, i:i + 1], ident[:, :])
            last.then_inc(tables_turned, 1)
            pe.wait_ge(experts_in, 16 * 5)
            pe.wait_ge(tables_step, TABLE_STEPS)
            window = [None]

            def step(at, turn, k):
                t0, t1, t2, t3 = (at(n) for n in range(4))
                if k == 0:
                    window[0] = experts_around(pe, at)
                if live(t1):
                    e1 = expert_at(pe, window[0], k, 1)
                if live(t3):
                    e3 = expert_at(pe, window[0], k, 3)
                if live(t0):
                    moved_tile(pe, e_rows_in, k, turn(0))
                    passed(pe, e_xT_done, at(2))
                    for kc in range(KD):
                        last = nc.tensor.transpose(ps[:, k % 2, kc * TS:(kc + 1) * TS], e_rows[:, k, kc * 128:(kc + 1) * 128], ident[:, :])
                    last.then_inc(e_turned, 1)
                if live(t1):
                    j = (k - 1) % 2
                    passed(pe, e_xT_done, t1)
                    passed(pe, e_biased, at(3))
                    for kc in range(KD):
                        last = nc.tensor.matmul(ps[:, 2 + j, 0:2 * INTER], e_xT[:, j, kc, :],
                                                w13[:, bass.ds(e1, 1), kc, :].rearrange("p o n -> p (o n)"),
                                                start=(kc == 0), stop=(kc == KD - 1))
                    last.then_inc(e_h_done, 1)
                if live(t2):
                    j = (k - 2) % 2
                    passed(pe, e_hid_done, t2)
                    passed(pe, e_hidT_done, at(4))
                    nc.tensor.transpose(ps[:, 4 + j, 0:TS], e_hid[:, j, :], ident[:, :]).then_inc(e_hid_turned, 1)
                if live(t3):
                    j = (k - 3) % 2
                    passed(pe, e_hidT_done, t3)
                    passed(pe, e_y_done, at(5))
                    nc.tensor.matmul(ps[:, 6 + j, 0:D], e_hidT[:, j, :], we2[:, bass.ds(e3, 1), :].rearrange("p o n -> p (o n)"),
                                     start=True, stop=True).then_inc(e_y_full, 1)

            tiles(pe, step, 3)

        for s in signals:
            assert s.given == 2 * s.per_pass, (s.name, s.given, s.per_pass)


INPUTS = ["x", "txt", "L0_tok_ln1_g", "L0_tok_ln1_b", "L0_tok_W_proj", "L0_tok_b_proj", "L0_tok_ln2_g", "L0_tok_ln2_b",
          "L0_tok_cls_token", "L0_tok_pos_emb", "L0_attn_ln_gamma", "L0_attn_ln_beta", "L0_attn_w_qkv", "L0_attn_w_out",
          "L0_ffn_gate_w", "L0_ffn_gate_b", "L0_ffn_We1", "L0_ffn_be1", "L0_ffn_We2", "L0_ffn_be2", "L0_ffn_We3",
          "L0_ffn_be3", "L0_ffn_ws1", "L0_ffn_bs1", "L0_ffn_ws2", "L0_ffn_bs2", "L0_ffn_ws3", "L0_ffn_bs3"]


def shape_constants():
    import numpy as np
    inv = (1.0 / 10000.0 ** (np.arange(0, DH, 2, dtype=np.float32) / np.float32(DH))).astype(np.float32)
    rows = np.arange(N)
    step = np.where(rows < NP, rows, np.where(rows == NP, 0, rows - 1)).astype(np.float32)
    angle = (inv[:, None] * step[None, :]).astype(np.float32)
    return {"cosT": np.tile(np.cos(angle), (4, 1)).astype(np.float32) / np.float32(W_SCALE),
            "sinT": np.tile(np.sin(angle), (4, 1)).astype(np.float32) / np.float32(W_SCALE),
            "ident": np.eye(128, dtype=np.float32),
            "counts": np.concatenate([np.arange(E), np.arange(E) * CAP + 1, np.arange(TILES), np.arange(TILES) * TS,
                                      E - np.arange(E),
                                      np.arange(COUNTS - COUNT_FULL) * TS]).astype(np.float32),
            "before": np.triu(np.ones((N, N), np.float32), 1),
            "number": np.concatenate([(TOPK * (np.arange(GB)[None, :] * N + np.arange(128)[:, None])),
                                      TRASH + np.arange(128)[:, None], np.arange(128)[:, None]], axis=1).astype(np.float32),
            "tri": (np.arange(E)[None, :] < np.arange(E)[:, None]).astype(np.float32).reshape(-1)}


def kernel(**inputs):
    import numpy as np
    import concourse.bacc as bacc
    from concourse.bass_utils import run_bass_kernel_spmd

    nc = bacc.Bacc("TRN2", target_bir_lowering=False, num_devices=1)
    arrays, aps = {}, {}
    for name, array in [(n, inputs[n]) for n in INPUTS] + list(shape_constants().items()):
        array = np.ascontiguousarray(array)
        arrays[f"in_{name}"] = array
        aps[name] = nc.dram_tensor(f"in_{name}", array.shape, F32, kind="ExternalInput").ap()
    zscr = nc.dram_tensor("image_tokens", (B, NP, D), F32, kind="Internal").ap()
    out = nc.dram_tensor("out_0", (B, N, D), F32, kind="ExternalOutput").ap()
    hrows = nc.dram_tensor("sums_without_experts", (GROUPS, N, GB, D), F32, kind="Internal").ap()
    xrows = nc.dram_tensor("expert_lists", (E * CAP, ROW), F32, kind="Internal").ap()
    yrows = nc.dram_tensor("expert_results", (TRASH + TILES * TS, D), F32, kind="Internal").ap()
    early_fusion_program(nc, aps, out, zscr, hrows, xrows, yrows)
    result = run_bass_kernel_spmd(nc, [arrays], core_ids=[0])
    return result.results[0]["out_0"]
```
